# Optimizing a Trainium2 kernel written in Bass

```python
import numpy as np
import jax
import jax.numpy as jnp

def _softmax(x, axis=-1):
    return jax.nn.softmax(x, axis=axis)

def _gelu(x):
    return jax.nn.gelu(x, approximate=True)

def _silu(x):
    return jax.nn.silu(x)

def _sigmoid(x):
    return jax.nn.sigmoid(x)

def _layernorm(x, axis=-1, eps=1e-05):
    m = jnp.mean(x, axis=axis, keepdims=True)
    v = jnp.var(x, axis=axis, keepdims=True)
    return (x - m) / jnp.sqrt(v + eps)

def _scatter_add(tgt, idx, src, axis=0):
    return tgt.at[idx].add(src)

def _segment_sum(src, seg, n):
    return jax.ops.segment_sum(src, seg, n)
kernel_name = 'mk_xattn_seq_d4_seqx_r8_bd4a74'

def setup_inputs(seed: int=0):
    np.random.seed(seed)
    _w = jnp.asarray

    def _rec_inputs():
        import jax
        import jax.numpy as jnp
        _rk = jax.random.key(seed)
        x = -0.0002928 + 1 * jax.random.normal(jax.random.fold_in(_rk, 1), (4, 256, 128), jnp.float32)
        _lenS = 256 - jax.random.randint(jax.random.fold_in(_rk, 7), (4,), 0, max(1, 256 // 4) + 1, jnp.int32)
        _lenS2 = 256 - jax.random.randint(jax.random.fold_in(_rk, 8), (4,), 0, max(1, 256 // 4) + 1, jnp.int32)
        _ctx_1024P = jax.random.normal(jax.random.fold_in(_rk, 11), (4, 16, 128), jnp.float32)
        _ctx_1024c = jax.random.dirichlet(jax.random.fold_in(_rk, 511), 0.3 * jnp.ones((16,), jnp.float32), (4, 256))
        _ctx_1024t = jnp.einsum('bsk,bkd->bsd', _ctx_1024c, _ctx_1024P)
        _ctx_1024t = _ctx_1024t * jax.lax.rsqrt(jnp.mean(jnp.square(_ctx_1024t)) + 1e-12) * 0.953939
        ctx_1024 = -1.39393e-06 + 0.999914 * (_ctx_1024t + 0.3 * jax.random.normal(jax.random.fold_in(_rk, 611), (4, 256, 128), jnp.float32))
        _validS = jnp.arange(256)[None, :] < _lenS[:, None]
        _validS2 = jnp.arange(256)[None, :] < _lenS2[:, None]
        _causal = jnp.tril(jnp.ones((256, 256), dtype=bool))
        mask_Bx1x1xS2_if1 = jnp.where(jnp.ones((4, 1, 1, 256), dtype=bool), 1, 0).astype(jnp.int32)
        mask_1x1xSxS2_ik0 = jnp.where(jnp.broadcast_to(_validS2[0:1, None, None, :], (1, 1, 256, 256)), 0, 1).astype(jnp.int32)
        mask_BxS2_ik0 = jnp.where(jnp.broadcast_to(_validS2[:, :], (4, 256)), 0, 1).astype(jnp.int32)
        return (x, ctx_1024, mask_Bx1x1xS2_if1, mask_1x1xSxS2_ik0, mask_BxS2_ik0)
    x, ctx_1024, mask_Bx1x1xS2_if1, mask_1x1xSxS2_ik0, mask_BxS2_ik0 = _rec_inputs()

    def _L0_xattn_setup():
        import jax, jax.numpy as jnp
        import numpy as np
        EPS = 1e-05

        def _layernorm(x, g, b):
            m = jnp.mean(x, axis=-1, keepdims=True)
            v = jnp.mean((x - m) ** 2, axis=-1, keepdims=True)
            return (x - m) / jnp.sqrt(v + EPS) * g + b

        def _mha(x, kv, Wq, Wk, Wv, mask, causal):
            m = mask[:, None]
            Q = jnp.einsum('bsd,hdk->bhsk', x, Wq) * m
            K = jnp.einsum('bsd,hdk->bhsk', kv, Wk) * m
            V = jnp.einsum('bsd,hdk->bhsk', kv, Wv) * m
            energy = jnp.einsum('bhsk,bhtk->bhst', Q, K)
            S = energy.shape[-1]
            lengths = jnp.sum(energy[:, :, 0, :] != 0, axis=-1)
            cols = jnp.arange(S)
            energy = jnp.where(cols[None, None, None, :] >= lengths[:, :, None, None], -jnp.inf, energy)
            if causal:
                energy = jnp.where(cols[None, :] > cols[:, None], -jnp.inf, energy)
            dk = Wq.shape[-1]
            score = jax.nn.softmax(energy / jnp.sqrt(jnp.asarray(dk, energy.dtype)), axis=-1)
            out = jnp.einsum('bhst,bhtk->bhsk', score, V) * m
            B, H, Sx, dkk = out.shape
            return out.transpose(0, 2, 1, 3).reshape(B, Sx, H * dkk)
        key = jax.random.key(seed)
        ks = jax.random.split(key, 20)
        B, S, D, H = (2, 256, 128, 16)
        dk = D // H
        sd = 0.02
        inp = {'x': jax.random.normal(ks[0], (B, S, D), jnp.float32), 'context': jax.random.normal(ks[1], (B, S, D), jnp.float32), 'Wq1': jax.random.normal(ks[2], (H, D, dk), jnp.float32) * sd, 'Wk1': jax.random.normal(ks[3], (H, D, dk), jnp.float32) * sd, 'Wv1': jax.random.normal(ks[4], (H, D, dk), jnp.float32) * sd, 'Wq2': jax.random.normal(ks[5], (H, D, dk), jnp.float32) * sd, 'Wk2': jax.random.normal(ks[6], (H, D, dk), jnp.float32) * sd, 'Wv2': jax.random.normal(ks[7], (H, D, dk), jnp.float32) * sd, 'ln1_g': jnp.ones((D,), jnp.float32), 'ln1_b': jnp.zeros((D,), jnp.float32), 'ln2_g': jnp.ones((D,), jnp.float32), 'ln2_b': jnp.zeros((D,), jnp.float32), 'ln3_g': jnp.ones((D,), jnp.float32), 'ln3_b': jnp.zeros((D,), jnp.float32), 'fc1_w': jax.random.normal(ks[8], (D, D), jnp.float32) * sd, 'fc1_b': jnp.zeros((D,), jnp.float32), 'fc2_w': jax.random.normal(ks[9], (D, D), jnp.float32) * sd, 'fc2_b': jnp.zeros((D,), jnp.float32)}
        return inp
    _L0_xattn_all = _L0_xattn_setup()
    _L0_xattn_in = {k: v for k, v in _L0_xattn_all.items() if k in ('Wq1', 'Wk1', 'Wv1', 'Wq2', 'Wk2', 'Wv2', 'ln1_g', 'ln1_b', 'ln2_g', 'ln2_b', 'ln3_g', 'ln3_b', 'fc1_w', 'fc1_b', 'fc2_w', 'fc2_b')}
    del _L0_xattn_all

    def _L1_xattn_setup():
        import jax, jax.numpy as jnp
        import numpy as np
        B, T, E = (4, 256, 128)
        H, HS = (16, 64)
        EPS = 1e-05

        def _layernorm(x, g, b):
            mu = jnp.mean(x, axis=-1, keepdims=True)
            var = jnp.mean(jnp.square(x - mu), axis=-1, keepdims=True)
            return (x - mu) * jax.lax.rsqrt(var + EPS) * g + b
        key = jax.random.key(seed)
        ks = jax.random.split(key, 8)
        q = jax.random.normal(ks[0], (B, T, E), dtype=jnp.float32)
        s_in = 1.0 / np.sqrt(E)
        s_o = 1.0 / np.sqrt(H * HS)
        return {'q': q, 'kv': q, 'ln_g': jnp.ones((E,), jnp.float32), 'ln_b': jnp.zeros((E,), jnp.float32), 'wq': jax.random.uniform(ks[1], (E, H * HS), jnp.float32, -s_in, s_in), 'bq': jax.random.uniform(ks[2], (H * HS,), jnp.float32, -s_in, s_in), 'wkv': jax.random.uniform(ks[3], (E, 2 * H * HS), jnp.float32, -s_in, s_in), 'bkv': jax.random.uniform(ks[4], (2 * H * HS,), jnp.float32, -s_in, s_in), 'wo': jax.random.uniform(ks[5], (H * HS, E), jnp.float32, -s_o, s_o), 'bo': jax.random.uniform(ks[6], (E,), jnp.float32, -s_o, s_o)}
    _L1_xattn_all = _L1_xattn_setup()
    _L1_xattn_in = {k: v for k, v in _L1_xattn_all.items() if k in ('ln_g', 'ln_b', 'wq', 'bq', 'wkv', 'bkv', 'wo', 'bo')}
    del _L1_xattn_all

    def _L2_xattn_setup():
        import jax, jax.numpy as jnp
        import numpy as np
        B, S, T, D, H, DF = (2, 256, 256, 128, 16, 512)
        DK = D // H
        EPS = 1e-05

        def _linear_params(key, d_in, d_out):
            kw, kb = jax.random.split(key)
            s = 1.0 / np.sqrt(d_in)
            W = jax.random.uniform(kw, (d_out, d_in), jnp.float32, -s, s)
            b = jax.random.uniform(kb, (d_out,), jnp.float32, -s, s)
            return (W, b)

        def _lin(x, W, b):
            return x @ W.T + b

        def _ln(x, g, b):
            mu = jnp.mean(x, -1, keepdims=True)
            var = jnp.mean(jnp.square(x - mu), -1, keepdims=True)
            return (x - mu) * jax.lax.rsqrt(var + EPS) * g + b

        def _mha(q_in, k_in, v_in, Wq, bq, Wk, bk, Wv, bv, Wo, bo, mask):
            Bq = q_in.shape[0]
            q = _lin(q_in, Wq, bq).reshape(Bq, -1, H, DK).transpose(0, 2, 1, 3)
            k = _lin(k_in, Wk, bk).reshape(Bq, -1, H, DK).transpose(0, 2, 1, 3)
            v = _lin(v_in, Wv, bv).reshape(Bq, -1, H, DK).transpose(0, 2, 1, 3)
            scores = jnp.einsum('bhqd,bhkd->bhqk', q, k) / np.sqrt(DK)
            scores = jnp.where(mask == 0, -jnp.inf, scores)
            attn = jax.nn.softmax(scores, axis=-1)
            out = jnp.einsum('bhqk,bhkd->bhqd', attn, v)
            out = out.transpose(0, 2, 1, 3).reshape(Bq, -1, H * DK)
            return _lin(out, Wo, bo)
        key = jax.random.key(seed)
        ks = jax.random.split(key, 16)
        inp = {}
        inp['x'] = jax.random.normal(ks[0], (B, S, D), jnp.float32)
        inp['enc_out'] = jax.random.normal(ks[1], (B, T, D), jnp.float32)
        inp['src_mask'] = jnp.ones((B, 1, 1, T), jnp.int32)
        inp['tgt_mask'] = jnp.tril(jnp.ones((S, S), jnp.int32))[None, None, :, :]
        for i, nm in enumerate(['q1', 'k1', 'v1', 'o1']):
            W, b = _linear_params(ks[2 + i], D, D)
            inp['W' + nm], inp['b' + nm] = (W, b)
        for i, nm in enumerate(['q2', 'k2', 'v2', 'o2']):
            W, b = _linear_params(ks[6 + i], D, D)
            inp['W' + nm], inp['b' + nm] = (W, b)
        inp['Wf1'], inp['bf1'] = _linear_params(ks[10], D, DF)
        inp['Wf2'], inp['bf2'] = _linear_params(ks[11], DF, D)
        for i in (1, 2, 3):
            inp[f'g{i}'] = jnp.ones((D,), jnp.float32)
            inp[f'be{i}'] = jnp.zeros((D,), jnp.float32)
        return inp
    _L2_xattn_all = _L2_xattn_setup()
    _L2_xattn_in = {k: v for k, v in _L2_xattn_all.items() if k in ('Wq1', 'bq1', 'Wk1', 'bk1', 'Wv1', 'bv1', 'Wo1', 'bo1', 'Wq2', 'bq2', 'Wk2', 'bk2', 'Wv2', 'bv2', 'Wo2', 'bo2', 'Wf1', 'bf1', 'Wf2', 'bf2', 'g1', 'be1', 'g2', 'be2', 'g3', 'be3')}
    del _L2_xattn_all

    def _L3_xattn_setup():
        import jax, jax.numpy as jnp
        import numpy as np
        PAD = float(-2 ** 32 + 1)
        NUM_HEADS = 16
        LN_EPS = 1e-05

        def _split_heads(x, h):
            B, T, D = x.shape
            d = D // h
            return x.reshape(B, T, h, d).transpose(2, 0, 1, 3).reshape(h * B, T, d)

        def _merge_heads(x, h):
            hB, T, d = x.shape
            B = hB // h
            return x.reshape(h, B, T, d).transpose(1, 2, 0, 3).reshape(B, T, h * d)
        key = jax.random.key(seed)
        ks = jax.random.split(key, 12)
        B, T, D = (2, 256, 128)
        s = 1.0 / np.sqrt(D)
        return {'q': jax.random.normal(ks[0], (B, T, D), jnp.float32), 'k': jax.random.normal(ks[1], (B, T, D), jnp.float32), 'v': jax.random.normal(ks[2], (B, T, D), jnp.float32), 'mask': jax.random.randint(ks[3], (B, T), 0, 2, jnp.int32), 'causality': 0, 'edge_fea': jnp.zeros((1,), jnp.float32), 'wq': jax.random.normal(ks[4], (D, D), jnp.float32) * s, 'bq': jax.random.normal(ks[5], (D,), jnp.float32) * 0.01, 'wk': jax.random.normal(ks[6], (D, D), jnp.float32) * s, 'bk': jax.random.normal(ks[7], (D,), jnp.float32) * 0.01, 'wv': jax.random.normal(ks[8], (D, D), jnp.float32) * s, 'bv': jax.random.normal(ks[9], (D,), jnp.float32) * 0.01, 'gamma': jnp.ones((D,), jnp.float32), 'beta': jnp.zeros((D,), jnp.float32)}
    _L3_xattn_all = _L3_xattn_setup()
    _L3_xattn_in = {k: v for k, v in _L3_xattn_all.items() if k in ('edge_fea', 'wq', 'bq', 'wk', 'bk', 'wv', 'bv', 'gamma', 'beta')}
    del _L3_xattn_all
    return {'x': x, 'ctx_1024': ctx_1024, 'mask_Bx1x1xS2_if1': mask_Bx1x1xS2_if1, 'mask_1x1xSxS2_ik0': mask_1x1xSxS2_ik0, 'mask_BxS2_ik0': mask_BxS2_ik0, 'L0_xattn_Wq1': _L0_xattn_in['Wq1'], 'L0_xattn_Wk1': _L0_xattn_in['Wk1'], 'L0_xattn_Wv1': _L0_xattn_in['Wv1'], 'L0_xattn_Wq2': _L0_xattn_in['Wq2'], 'L0_xattn_Wk2': _L0_xattn_in['Wk2'], 'L0_xattn_Wv2': _L0_xattn_in['Wv2'], 'L0_xattn_ln1_g': _L0_xattn_in['ln1_g'], 'L0_xattn_ln1_b': _L0_xattn_in['ln1_b'], 'L0_xattn_ln2_g': _L0_xattn_in['ln2_g'], 'L0_xattn_ln2_b': _L0_xattn_in['ln2_b'], 'L0_xattn_ln3_g': _L0_xattn_in['ln3_g'], 'L0_xattn_ln3_b': _L0_xattn_in['ln3_b'], 'L0_xattn_fc1_w': _L0_xattn_in['fc1_w'], 'L0_xattn_fc1_b': _L0_xattn_in['fc1_b'], 'L0_xattn_fc2_w': _L0_xattn_in['fc2_w'], 'L0_xattn_fc2_b': _L0_xattn_in['fc2_b'], 'L1_xattn_ln_g': _L1_xattn_in['ln_g'], 'L1_xattn_ln_b': _L1_xattn_in['ln_b'], 'L1_xattn_wq': _L1_xattn_in['wq'], 'L1_xattn_bq': _L1_xattn_in['bq'], 'L1_xattn_wkv': _L1_xattn_in['wkv'], 'L1_xattn_bkv': _L1_xattn_in['bkv'], 'L1_xattn_wo': _L1_xattn_in['wo'], 'L1_xattn_bo': _L1_xattn_in['bo'], 'L2_xattn_Wq1': _L2_xattn_in['Wq1'], 'L2_xattn_bq1': _L2_xattn_in['bq1'], 'L2_xattn_Wk1': _L2_xattn_in['Wk1'], 'L2_xattn_bk1': _L2_xattn_in['bk1'], 'L2_xattn_Wv1': _L2_xattn_in['Wv1'], 'L2_xattn_bv1': _L2_xattn_in['bv1'], 'L2_xattn_Wo1': _L2_xattn_in['Wo1'], 'L2_xattn_bo1': _L2_xattn_in['bo1'], 'L2_xattn_Wq2': _L2_xattn_in['Wq2'], 'L2_xattn_bq2': _L2_xattn_in['bq2'], 'L2_xattn_Wk2': _L2_xattn_in['Wk2'], 'L2_xattn_bk2': _L2_xattn_in['bk2'], 'L2_xattn_Wv2': _L2_xattn_in['Wv2'], 'L2_xattn_bv2': _L2_xattn_in['bv2'], 'L2_xattn_Wo2': _L2_xattn_in['Wo2'], 'L2_xattn_bo2': _L2_xattn_in['bo2'], 'L2_xattn_Wf1': _L2_xattn_in['Wf1'], 'L2_xattn_bf1': _L2_xattn_in['bf1'], 'L2_xattn_Wf2': _L2_xattn_in['Wf2'], 'L2_xattn_bf2': _L2_xattn_in['bf2'], 'L2_xattn_g1': _L2_xattn_in['g1'], 'L2_xattn_be1': _L2_xattn_in['be1'], 'L2_xattn_g2': _L2_xattn_in['g2'], 'L2_xattn_be2': _L2_xattn_in['be2'], 'L2_xattn_g3': _L2_xattn_in['g3'], 'L2_xattn_be3': _L2_xattn_in['be3'], 'L3_xattn_edge_fea': _L3_xattn_in['edge_fea'], 'L3_xattn_wq': _L3_xattn_in['wq'], 'L3_xattn_bq': _L3_xattn_in['bq'], 'L3_xattn_wk': _L3_xattn_in['wk'], 'L3_xattn_bk': _L3_xattn_in['bk'], 'L3_xattn_wv': _L3_xattn_in['wv'], 'L3_xattn_bv': _L3_xattn_in['bv'], 'L3_xattn_gamma': _L3_xattn_in['gamma'], 'L3_xattn_beta': _L3_xattn_in['beta']}

def reference(x, ctx_1024, mask_Bx1x1xS2_if1, mask_1x1xSxS2_ik0, mask_BxS2_ik0, L0_xattn_Wq1, L0_xattn_Wk1, L0_xattn_Wv1, L0_xattn_Wq2, L0_xattn_Wk2, L0_xattn_Wv2, L0_xattn_ln1_g, L0_xattn_ln1_b, L0_xattn_ln2_g, L0_xattn_ln2_b, L0_xattn_ln3_g, L0_xattn_ln3_b, L0_xattn_fc1_w, L0_xattn_fc1_b, L0_xattn_fc2_w, L0_xattn_fc2_b, L1_xattn_ln_g, L1_xattn_ln_b, L1_xattn_wq, L1_xattn_bq, L1_xattn_wkv, L1_xattn_bkv, L1_xattn_wo, L1_xattn_bo, L2_xattn_Wq1, L2_xattn_bq1, L2_xattn_Wk1, L2_xattn_bk1, L2_xattn_Wv1, L2_xattn_bv1, L2_xattn_Wo1, L2_xattn_bo1, L2_xattn_Wq2, L2_xattn_bq2, L2_xattn_Wk2, L2_xattn_bk2, L2_xattn_Wv2, L2_xattn_bv2, L2_xattn_Wo2, L2_xattn_bo2, L2_xattn_Wf1, L2_xattn_bf1, L2_xattn_Wf2, L2_xattn_bf2, L2_xattn_g1, L2_xattn_be1, L2_xattn_g2, L2_xattn_be2, L2_xattn_g3, L2_xattn_be3, L3_xattn_edge_fea, L3_xattn_wq, L3_xattn_bq, L3_xattn_wk, L3_xattn_bk, L3_xattn_wv, L3_xattn_bv, L3_xattn_gamma, L3_xattn_beta):
    import jax
    import jax.numpy as jnp

    def _L0_xattn_ref(x, context, Wq1, Wk1, Wv1, Wq2, Wk2, Wv2, ln1_g, ln1_b, ln2_g, ln2_b, ln3_g, ln3_b, fc1_w, fc1_b, fc2_w, fc2_b):
        import jax, jax.numpy as jnp
        import numpy as np
        EPS = 1e-05

        def _layernorm(x, g, b):
            m = jnp.mean(x, axis=-1, keepdims=True)
            v = jnp.mean((x - m) ** 2, axis=-1, keepdims=True)
            return (x - m) / jnp.sqrt(v + EPS) * g + b

        def _mha(x, kv, Wq, Wk, Wv, mask, causal):
            m = mask[:, None]
            Q = jnp.einsum('bsd,hdk->bhsk', x, Wq) * m
            K = jnp.einsum('bsd,hdk->bhsk', kv, Wk) * m
            V = jnp.einsum('bsd,hdk->bhsk', kv, Wv) * m
            energy = jnp.einsum('bhsk,bhtk->bhst', Q, K)
            S = energy.shape[-1]
            lengths = jnp.sum(energy[:, :, 0, :] != 0, axis=-1)
            cols = jnp.arange(S)
            energy = jnp.where(cols[None, None, None, :] >= lengths[:, :, None, None], -jnp.inf, energy)
            if causal:
                energy = jnp.where(cols[None, :] > cols[:, None], -jnp.inf, energy)
            dk = Wq.shape[-1]
            score = jax.nn.softmax(energy / jnp.sqrt(jnp.asarray(dk, energy.dtype)), axis=-1)
            out = jnp.einsum('bhst,bhtk->bhsk', score, V) * m
            B, H, Sx, dkk = out.shape
            return out.transpose(0, 2, 1, 3).reshape(B, Sx, H * dkk)
        mask0 = 1.0 - jnp.all(x == 0, axis=2, keepdims=True).astype(x.dtype)
        z = _mha(x, x, Wq1, Wk1, Wv1, mask0, causal=True)
        x1 = _layernorm(x + z, ln1_g, ln1_b)
        mask1 = 1.0 - jnp.all(x1 == 0, axis=2, keepdims=True).astype(x1.dtype)
        z = _mha(x1, context, Wq2, Wk2, Wv2, mask1, causal=False)
        x2 = _layernorm(x1 + z, ln2_g, ln2_b)
        z = jnp.maximum(x2 @ fc1_w.T + fc1_b, 0.0) * mask0
        z = (z @ fc2_w.T + fc2_b) * mask0
        return _layernorm(x2 + z, ln3_g, ln3_b)

    def _L1_xattn_ref(q, kv, ln_g, ln_b, wq, bq, wkv, bkv, wo, bo):
        import jax, jax.numpy as jnp
        import numpy as np
        B, T, E = (4, 256, 128)
        H, HS = (16, 64)
        EPS = 1e-05

        def _layernorm(x, g, b):
            mu = jnp.mean(x, axis=-1, keepdims=True)
            var = jnp.mean(jnp.square(x - mu), axis=-1, keepdims=True)
            return (x - mu) * jax.lax.rsqrt(var + EPS) * g + b
        oq = q
        qn = _layernorm(q, ln_g, ln_b)
        kvn = _layernorm(kv, ln_g, ln_b)
        b, qT, _ = q.shape
        kvT = kv.shape[1]
        qp = (qn @ wq + bq).reshape(b, qT, H, HS).transpose(0, 2, 1, 3)
        kvp = kvn @ wkv + bkv
        kp, vp = jnp.split(kvp, 2, axis=-1)
        kp = kp.reshape(b, kvT, H, HS).transpose(0, 2, 1, 3)
        vp = vp.reshape(b, kvT, H, HS).transpose(0, 2, 1, 3)
        attn = jnp.einsum('bhqd,bhkd->bhqk', qp, kp) / jnp.sqrt(jnp.float32(HS))
        causal = jnp.tril(jnp.ones((qT, kvT), dtype=bool))
        attn = jnp.where(causal, attn, -jnp.inf)
        attn = jax.nn.softmax(attn, axis=-1)
        ctx = jnp.einsum('bhqk,bhkd->bhqd', attn, vp)
        ctx = ctx.transpose(0, 2, 1, 3).reshape(b, qT, H * HS)
        out = ctx @ wo + bo + oq
        return out

    def _L2_xattn_ref(x, enc_out, src_mask, tgt_mask, Wq1, bq1, Wk1, bk1, Wv1, bv1, Wo1, bo1, Wq2, bq2, Wk2, bk2, Wv2, bv2, Wo2, bo2, Wf1, bf1, Wf2, bf2, g1, be1, g2, be2, g3, be3):
        import jax, jax.numpy as jnp
        import numpy as np
        B, S, T, D, H, DF = (2, 256, 256, 128, 16, 512)
        DK = D // H
        EPS = 1e-05

        def _linear_params(key, d_in, d_out):
            kw, kb = jax.random.split(key)
            s = 1.0 / np.sqrt(d_in)
            W = jax.random.uniform(kw, (d_out, d_in), jnp.float32, -s, s)
            b = jax.random.uniform(kb, (d_out,), jnp.float32, -s, s)
            return (W, b)

        def _lin(x, W, b):
            return x @ W.T + b

        def _ln(x, g, b):
            mu = jnp.mean(x, -1, keepdims=True)
            var = jnp.mean(jnp.square(x - mu), -1, keepdims=True)
            return (x - mu) * jax.lax.rsqrt(var + EPS) * g + b

        def _mha(q_in, k_in, v_in, Wq, bq, Wk, bk, Wv, bv, Wo, bo, mask):
            Bq = q_in.shape[0]
            q = _lin(q_in, Wq, bq).reshape(Bq, -1, H, DK).transpose(0, 2, 1, 3)
            k = _lin(k_in, Wk, bk).reshape(Bq, -1, H, DK).transpose(0, 2, 1, 3)
            v = _lin(v_in, Wv, bv).reshape(Bq, -1, H, DK).transpose(0, 2, 1, 3)
            scores = jnp.einsum('bhqd,bhkd->bhqk', q, k) / np.sqrt(DK)
            scores = jnp.where(mask == 0, -jnp.inf, scores)
            attn = jax.nn.softmax(scores, axis=-1)
            out = jnp.einsum('bhqk,bhkd->bhqd', attn, v)
            out = out.transpose(0, 2, 1, 3).reshape(Bq, -1, H * DK)
            return _lin(out, Wo, bo)
        out = _mha(x, x, x, Wq1, bq1, Wk1, bk1, Wv1, bv1, Wo1, bo1, tgt_mask)
        x = _ln(x + out, g1, be1)
        out = _mha(x, enc_out, enc_out, Wq2, bq2, Wk2, bk2, Wv2, bv2, Wo2, bo2, src_mask)
        x = _ln(x + out, g2, be2)
        ff = _lin(jax.nn.relu(_lin(x, Wf1, bf1)), Wf2, bf2)
        return _ln(x + ff, g3, be3)

    def _L3_xattn_ref(q, k, v, mask, causality, edge_fea, wq, bq, wk, bk, wv, bv, gamma, beta):
        import jax, jax.numpy as jnp
        import numpy as np
        PAD = float(-2 ** 32 + 1)
        NUM_HEADS = 16
        LN_EPS = 1e-05

        def _split_heads(x, h):
            B, T, D = x.shape
            d = D // h
            return x.reshape(B, T, h, d).transpose(2, 0, 1, 3).reshape(h * B, T, d)

        def _merge_heads(x, h):
            hB, T, d = x.shape
            B = hB // h
            return x.reshape(h, B, T, d).transpose(1, 2, 0, 3).reshape(B, T, h * d)
        h = NUM_HEADS
        B, T, D = q.shape
        depth = D // h
        qh = _split_heads(q @ wq.T + bq, h)
        kh = _split_heads(k @ wk.T + bk, h)
        vh = _split_heads(v @ wv.T + bv, h)
        scores = jnp.einsum('ntd,nsd->nts', qh, kh) / jnp.sqrt(jnp.asarray(depth, qh.dtype))
        km = jnp.repeat(mask.astype(scores.dtype), h, axis=0)[:, None, :]
        scores = scores + km * PAD
        if causality:
            tril = jnp.tril(jnp.ones((T, T), scores.dtype))
            scores = jnp.where(tril[None] == 0, jnp.full_like(scores, PAD), scores)
        attn = jax.nn.softmax(scores, axis=-1)
        ctx = jnp.einsum('nts,nsd->ntd', attn, vh)
        out = _merge_heads(ctx, h) + q
        mu = jnp.mean(out, axis=-1, keepdims=True)
        var = jnp.var(out, axis=-1, keepdims=True)
        out = (out - mu) / jnp.sqrt(var + LN_EPS) * gamma + beta
        return out
    x = _L0_xattn_ref(x, ctx_1024, L0_xattn_Wq1, L0_xattn_Wk1, L0_xattn_Wv1, L0_xattn_Wq2, L0_xattn_Wk2, L0_xattn_Wv2, L0_xattn_ln1_g, L0_xattn_ln1_b, L0_xattn_ln2_g, L0_xattn_ln2_b, L0_xattn_ln3_g, L0_xattn_ln3_b, L0_xattn_fc1_w, L0_xattn_fc1_b, L0_xattn_fc2_w, L0_xattn_fc2_b)
    x = _L1_xattn_ref(x, ctx_1024, L1_xattn_ln_g, L1_xattn_ln_b, L1_xattn_wq, L1_xattn_bq, L1_xattn_wkv, L1_xattn_bkv, L1_xattn_wo, L1_xattn_bo)
    x = _L2_xattn_ref(x, ctx_1024, mask_Bx1x1xS2_if1, mask_1x1xSxS2_ik0, L2_xattn_Wq1, L2_xattn_bq1, L2_xattn_Wk1, L2_xattn_bk1, L2_xattn_Wv1, L2_xattn_bv1, L2_xattn_Wo1, L2_xattn_bo1, L2_xattn_Wq2, L2_xattn_bq2, L2_xattn_Wk2, L2_xattn_bk2, L2_xattn_Wv2, L2_xattn_bv2, L2_xattn_Wo2, L2_xattn_bo2, L2_xattn_Wf1, L2_xattn_bf1, L2_xattn_Wf2, L2_xattn_bf2, L2_xattn_g1, L2_xattn_be1, L2_xattn_g2, L2_xattn_be2, L2_xattn_g3, L2_xattn_be3)
    x = _L3_xattn_ref(x, ctx_1024, ctx_1024, mask_BxS2_ik0, 0, L3_xattn_edge_fea, L3_xattn_wq, L3_xattn_bq, L3_xattn_wk, L3_xattn_bk, L3_xattn_wv, L3_xattn_bv, L3_xattn_gamma, L3_xattn_beta)
    return x

_drawn_inputs = setup_inputs


def setup_inputs(seed=0):
    import zlib

    import numpy as np

    out = dict(_drawn_inputs(seed))
    spreads = {'L0_xattn_ln1_g': (1.0, 0.2),
     'L0_xattn_ln1_b': (0.0, 0.1),
     'L0_xattn_ln2_g': (1.0, 0.2),
     'L0_xattn_ln2_b': (0.0, 0.1),
     'L0_xattn_ln3_g': (1.0, 0.2),
     'L0_xattn_ln3_b': (0.0, 0.1),
     'L0_xattn_fc1_b': (0.0, 0.768),
     'L0_xattn_fc2_b': (0.0, 0.1),
     'L1_xattn_ln_g': (1.0, 0.2),
     'L1_xattn_ln_b': (0.0, 0.305),
     'L2_xattn_g1': (1.0, 0.2),
     'L2_xattn_be1': (0.0, 0.1),
     'L2_xattn_g2': (1.0, 0.2),
     'L2_xattn_be2': (0.0, 0.1),
     'L2_xattn_g3': (1.0, 0.2),
     'L2_xattn_be3': (0.0, 0.1),
     'L3_xattn_gamma': (1.0, 0.2),
     'L3_xattn_beta': (0.0, 0.1)}
    factors = {'L0_xattn_Wq1': 8.0,
     'L0_xattn_Wk1': 8.0,
     'L0_xattn_Wq2': 8.0,
     'L0_xattn_Wk2': 8.0,
     'L1_xattn_wq': 3.087,
     'L1_xattn_bq': 31.997,
     'L1_xattn_bkv': 2.743,
     'L1_xattn_bo': 4.054,
     'L2_xattn_bq1': 28.121,
     'L2_xattn_bk1': 64.0,
     'L2_xattn_Wq2': 3.099,
     'L2_xattn_bq2': 8.0,
     'L2_xattn_Wk2': 3.145,
     'L2_xattn_bk2': 64.0,
     'L2_xattn_bf1': 3.532,
     'L3_xattn_bq': 24.632,
     'L3_xattn_bk': 64.0,
     'L3_xattn_bv': 6.015}
    for name, (base, spread) in spreads.items():
        noise = np.random.default_rng([zlib.crc32(name.encode()), seed]).standard_normal(out[name].shape)
        drawn = base * np.exp(spread * noise) if base else spread * noise
        out[name] = jnp.asarray(drawn.astype(out[name].dtype))
    for name, factor in factors.items():
        out[name] = (out[name] * factor).astype(out[name].dtype)
    return out
```

```python
from contextlib import ExitStack

import numpy as np

import concourse.bass as bass
from concourse import mybir

F32 = mybir.dt.float32
BF16 = mybir.dt.bfloat16
I32 = mybir.dt.int32
ALU = mybir.AluOpType
ACT = mybir.ActivationFunctionType
AX = mybir.AxisListType

P = 128
B, S, D, H = 4, 256, 128, 16
DK = D // H
HS = 64
T = S // P
EPS = 1e-5
NEG = -(2.0 ** 126)
CAP = 2.0 ** 125
PAD = float(-2 ** 32 + 1)
PARTS = 3
MASK_ROW = 96
NEGMAX_ROW = 97
SCORE_ROWS = MASK_ROW + 1
ALL_ROWS = NEGMAX_ROW + PARTS
RING = 3

L0S, L0C, L1, L2S, L2C, L3 = range(6)
LAYERS = [L0S, L0C, L1, L2S, L2C, L3]
STEPS = [(layer, b) for layer in LAYERS for b in range(B)]
N = len(STEPS)
CAUSAL = (L0S, L1)
UNITS = 8

WEIGHTS = [("L0.q1", 128), ("L0.k1", 128), ("L0.v1", 128), ("L0.q2", 128), ("L0.k2", 128), ("L0.v2", 128),
           ("L0.fc1", 128), ("L0.fc2", 128), ("L1.q", 1024), ("L1.k", 1024), ("L1.v", 1024), ("L1.o", 1024),
           ("L2.q1", 128), ("L2.k1", 128), ("L2.v1", 128), ("L2.o1", 128),
           ("L2.q2", 128), ("L2.k2", 128), ("L2.v2", 128), ("L2.o2", 128), ("L2.f1", 512), ("L2.f2", 512),
           ("L3.q", 128), ("L3.k", 128), ("L3.v", 128)]
ROWS = [("L0.g1", 128), ("L0.b1", 128), ("L0.g2", 128), ("L0.b2", 128), ("L0.g3", 128), ("L0.b3", 128),
        ("L0.fc2b", 128), ("L1.g", 128), ("L1.b", 128), ("L1.bv", 1024), ("L1.bo", 128),
        ("L2.bv1", 128), ("L2.bo1", 128), ("L2.g1", 128), ("L2.be1", 128),
        ("L2.bv2", 128), ("L2.bo2", 128), ("L2.g2", 128), ("L2.be2", 128),
        ("L2.bf2", 128), ("L2.g3", 128), ("L2.be3", 128), ("L3.bv", 128), ("L3.g", 128), ("L3.b", 128)]
COLS = [("L0.fc1b", 1), ("L1.bq", 8), ("L1.bk", 8), ("L2.bq1", 1), ("L2.bk1", 1), ("L2.bq2", 1), ("L2.bk2", 1),
        ("L2.bf1", 4), ("L3.bq", 1), ("L3.bk", 1)]
CONSTS = [("own_head", 16), ("key", 256), ("ident", 128), ("causal", 128), ("causalT", 128), ("pick", 256)]


def offsets(table):
    at, found = 0, {}
    for name, n in table:
        found[name] = (at, at + n)
        at += n
    return found, at


W_AT, W_N = offsets(WEIGHTS)
W_HOME = dict(W_AT)
W_HOME.update({f"L2.{x}1": W_AT[f"L0.{x}1"] for x in "qkv"} | {f"L2.{x}2": W_AT[f"L0.{x}2"] for x in "qkv"})
RESIDENT = W_AT["L2.q1"][0]
W_HOME["L2.o1"] = (RESIDENT, RESIDENT + P)
W_HOME["L2.f1"] = (W_AT["L1.q"][0], W_AT["L1.q"][0] + 512)
W_HOME["L2.f2"] = (W_AT["L1.q"][0] + 512, W_AT["L1.q"][1])
for i, name in enumerate(("L2.o2", "L3.q", "L3.k", "L3.v")):
    W_HOME[name] = (W_AT["L1.k"][0] + i * P, W_AT["L1.k"][0] + (i + 1) * P)
LATE = {"first": ["L2.q1", "L2.k1", "L2.v1", "L2.o1"], "second": ["L2.q2", "L2.k2", "L2.v2"],
        "third": ["L2.o2", "L2.f1", "L2.f2", "L3.q", "L3.k", "L3.v"]}
R_AT, R_N = offsets(ROWS)
C_AT, C_N = offsets(COLS)
K_AT, K_N = offsets(CONSTS)
K_BF = K_AT["ident"][0]
K_F32 = K_AT["causal"][0]
W_CUTS = [0, W_AT["L0.fc1"][0], W_AT["L1.k"][0], W_AT["L1.o"][0], RESIDENT]


def narrow(n):
    return 0 <= n < N and STEPS[n][0] != L1


def wide(n):
    return 0 <= n < N and STEPS[n][0] == L1


NARROW = [n for n in range(N) if narrow(n)]
ORD = {n: j for j, n in enumerate(NARROW)}


def tail_pieces(n):
    layer = STEPS[n][0]
    return [(x, n) for x in {
        L0S: ["turn0", "turn1", "x_turn", "kv_turn"],
        L0C: ["turn0", "turn1", "x_turn", "ff1", "ff2", "y_turn"],
        L1: ["out", "x_turn"],
        L2S: ["turn0", "turn1", "z_turn", "out", "x_turn"],
        L2C: ["turn0", "turn1", "z_turn", "out", "x_turn", "ff1a", "ff1b", "ff2", "y_turn"],
        L3: ["turn0", "turn1"],
    }[layer]]


def slot_pieces(k):
    got = tail_pieces(k - 1) if k >= 1 else []
    if narrow(k + 3):
        got += [("qk", k + 3)] + ([("count", k + 3)] if STEPS[k + 3][0] in (L0S, L0C) else []) + [("v", k + 3)]
    if wide(k + 1):
        got += [(f"v1_{i}", k + 1) for i in range(4)]
    return got


def make_plan():
    plan = []
    for k in range(-3, N + 1):
        pieces = slot_pieces(k)
        for u in range(UNITS):
            i = UNITS * k + u
            live = 0 <= k < N
            for n, p in [divmod(i + 3, UNITS)] if i >= 0 else []:
                if wide(n):
                    plan.append(("qk1", n, p))
            for n, p in [divmod(i + 2, UNITS)] if i >= 0 else []:
                if wide(n):
                    plan.append(("s1", n, p))
            if i + 1 >= 0 and i + 1 < UNITS * N:
                plan.append(("st", *divmod(i + 1, UNITS)))
            n, v = (k + 1, 4 + u) if u < 4 else (k + 2, u - 4)
            if narrow(n):
                plan.append(("s", n, v))
            if u == 5 and narrow(k + 1):
                plan.append(("nm", k + 1, 0))
            for j, (name, n) in enumerate(pieces):
                if j * UNITS // len(pieces) == u:
                    plan.append((name, n, 0))
            if live:
                plan.append(("pv", k, u))
            for n, p in [divmod(i + 2, UNITS)] if i >= 0 else []:
                if wide(n):
                    plan.append(("nm1", n, p))
    return plan


PLAN = make_plan()


def score_banks(n, v):
    g, t = divmod(v, T)
    if STEPS[n][0] in CAUSAL and t == 0:
        return [(t, 4 * g, 4, P)]
    return [(t, 4 * g + 2 * x, 2, S) for x in range(2)]


def number(events):
    return {e: i for i, e in enumerate(events)}


WORK = number([e for e in PLAN if e[0] not in ("st", "pv", "s", "s1")])
SBANK = number([(kind, n, v, x) for kind, n, v in PLAN if kind in ("s", "s1")
                for x in range(len(score_banks(n, v)) if kind == "s" else 2)])
OUSE = number([(n, h) for n in range(N) for h in range(UNITS if wide(n) else 2)])


def attention_stack_program(nc, x, x_t, ctx, ctx_t, weights, rows, cols, consts, src_mask, tgt_mask, tgt_mask_t,
                            key_mask, out):
    with ExitStack() as stack:
        def sb(name, shape, dt=F32):
            return stack.enter_context(nc.sbuf_tensor(name, shape, dt))

        def psum(name, shape):
            return stack.enter_context(nc.psum_tensor(name, shape, F32))

        def sem(name):
            return stack.enter_context(nc.semaphore(name))

        w_sb = sb("w_sb", [P, RESIDENT + P])
        row_sb = sb("row_sb", [P, R_N])
        col_sb = sb("col_sb", [P, C_N])
        const_sb = sb("const_sb", [P, K_F32])
        const_bf = sb("const_bf", [P, K_N - K_BF], BF16)
        q_stack = [sb(f"q_stack{i}", [P, H, S], BF16) for i in range(RING)]
        k_stack = [sb(f"k_stack{i}", [P, H, S], BF16) for i in range(RING)]
        qk_sb = [sb(f"qk_sb{i}", [P, 2, S]) for i in range(2)]
        parts = [sb(f"parts{i}", [P, 2, PARTS, S], BF16) for i in range(2)]
        rest = sb("rest", [P, 2, S])
        v_sb = [sb(f"v_sb{b}", [P, T, H, 32]) for b in range(B)]
        v1_sb = [sb(f"v1_sb{i}", [P, T, H * HS]) for i in range(2)]
        q1_sb = [sb(f"q1_sb{i}", [P, 2, S]) for i in range(3)]
        k1_sb = [sb(f"k1_sb{i}", [P, S]) for i in range(3)]
        ctx1_t = sb("ctx1_t", [P, UNITS, S])
        rec1 = sb("rec1", [P, S])
        ones = sb("ones", [P, HS])
        probs = [sb(f"probs{i}", [P, 4 * S]) for i in range(2)]
        negmax = [sb(f"negmax{i}", [P, T, H]) for i in range(2)]
        nm_rest = sb("nm_rest", [P, T, H])
        nm_parts = [sb(f"nm_parts{i}", [P, T, PARTS, H], BF16) for i in range(2)]
        nm_rows = [sb(f"nm_rows{i}", [PARTS * H, S], BF16) for i in range(2)]
        nm1 = sb("nm1", [P, T, 2])
        nm1_rest = sb("nm1_rest", [P, T, 2])
        nm1_parts = sb("nm1_parts", [P, T, P], BF16)
        nm1_rows = [sb(f"nm1_rows{i}", [P, S], BF16) for i in range(2)]
        q0_own = sb("q0_own", [P, H])
        nonzero = sb("nonzero", [H, S])
        length = sb("length", [H, 1])
        key_row = [sb(f"key_row{b}", [H, S], BF16) for b in range(B)]
        src_rows = sb("src_rows", [H, B, S], BF16)
        zero_row = sb("zero_row", [H, S], BF16)
        pad_row = sb("pad_row", [H, S], BF16)
        tgt_bias = sb("tgt_bias", [P, T, S], BF16)
        tgt_bias_t = sb("tgt_bias_t", [P, T, S], BF16)
        raw = [t[:, :, :].rearrange("p t n -> p (t n)") for t in v1_sb]
        int_tgt = raw[0][:, 0:4 * S].bitcast(I32).rearrange("p (w t k) -> p w t k", w=2, t=T)
        int_src = raw[0][0:H, 4 * S:8 * S].bitcast(I32).rearrange("p (b k) -> p b k", b=B)
        int_key = raw[1][:, 0:S].bitcast(I32)
        key_f = raw[1][:, S:2 * S]
        const_f = raw[1][:, 2 * S:2 * S + K_N - K_F32]
        key_min = sb("key_min", [P, 1])
        q_gate = sb("q_gate", [P, 1])
        q_gate_bias = sb("q_gate_bias", [P, 1])
        o_sb = sb("o_sb", [P, 4, S])
        res = [[sb(f"res{b}_{i}", [P, T, D]) for i in range(2)] for b in range(B)]
        ctx_sb = [sb(f"ctx_sb{b}", [P, T, D]) for b in range(B)]
        x_turned = [sb(f"x_turned{b}", [P, S]) for b in range(B)]
        ctx_turned = [sb(f"ctx_turned{b}", [P, S]) for b in range(B)]
        ctxm_turned = [sb(f"ctxm_turned{b}", [P, S]) for b in range(B)]
        kvn_turned = [sb(f"kvn_turned{b}", [P, S]) for b in range(B)]
        z_sb = sb("z_sb", [P, T, D])
        z_turned = sb("z_turned", [P, S])
        y_sb = sb("y_sb", [P, T, D])
        xh_sb = sb("xh_sb", [P, T, D])
        kvn_sb = sb("kvn_sb", [P, T, D])
        ctxm_sb = sb("ctxm_sb", [P, T, D])
        hidden = ctx1_t[:, 4:8, :]
        rec = sb("rec", [P, H])
        stats = sb("stats", [P, T, 6])
        mean_var = sb("mean_var", [P, T, 2])
        var_eps = sb("var_eps", [P, T])
        rstd = sb("rstd", [P, T])
        minus_half = sb("minus_half", [P, T])
        absmax = sb("absmax", [P, T])
        live0 = [sb(f"live0_{b}", [P, T]) for b in range(B)]
        live1 = [sb(f"live1_{b}", [P, T]) for b in range(B)]

        st_ps = [psum(f"st_ps{i}", [P, 1024]) for i in range(2)]
        s_ps = [psum(f"s_ps{i}", [P, 512]) for i in range(2)]
        o_ps = psum("o_ps", [P, 512])
        m_ps = psum("m_ps", [P, 512])
        m_bf = m_ps[:, :].bitcast(BF16)

        small_loaded = sem("small_loaded")
        rows_loaded = sem("rows_loaded")
        ctx_t_loaded = sem("ctx_t_loaded")
        x0_loaded = sem("x0_loaded")
        x_loaded = sem("x_loaded")
        tok_loaded = sem("tok_loaded")
        w_loaded = [sem(f"w_loaded{i}") for i in range(len(W_CUTS) - 1)]
        late_loaded = {x: sem(f"late_loaded_{x}") for x in LATE}
        masks_loaded = sem("masks_loaded")
        dve_step = sem("dve_step")
        pool_step = sem("pool_step")
        stacks_blank = sem("stacks_blank")
        consts_ready = sem("consts_ready")
        masks_ready = sem("masks_ready")
        work_full = sem("work_full")
        work_free = sem("work_free")
        s_full = sem("s_full")
        s_free = sem("s_free")
        st_full = sem("st_full")
        exp_done = sem("exp_done")
        pv_done = sem("pv_done")
        o_free = sem("o_free")
        o_ready = sem("o_ready")
        qk_ready = sem("qk_ready")
        q0_ready = sem("q0_ready")
        parts_ready = sem("parts_ready")
        bounced = [sem(f"bounced{i}") for i in range(2)]
        stacked = [sem(f"stacked{i}") for i in range(RING)]
        key_row_ready = sem("key_row_ready")
        v_ready = sem("v_ready")
        nm_parts_ready = sem("nm_parts_ready")
        nm_rows_ready = sem("nm_rows_ready")
        nm_stacked = [sem(f"nm_stacked{i}") for i in range(RING)]
        qk1_ready = sem("qk1_ready")
        nm1_parts_ready = sem("nm1_parts_ready")
        nm1_rows_ready = sem("nm1_rows_ready")
        v1_ready = sem("v1_ready")
        ctx1_ready = sem("ctx1_ready")
        z_ready = sem("z_ready")
        z_turned_ready = sem("z_turned_ready")
        x_ready = sem("x_ready")
        x_turned_ready = sem("x_turned_ready")
        kv_ready = sem("kv_ready")
        kv_turned_ready = sem("kv_turned_ready")
        y_ready = sem("y_ready")
        y_turned_ready = sem("y_turned_ready")
        hidden_ready = sem("hidden_ready")
        var_ready = sem("var_ready")
        rstd_ready = sem("rstd_ready")
        result_ready = sem("result_ready")
        stored = sem("stored")

        bounce = [nc.dram_tensor(f"bounce{i}", [2, PARTS, P, S], BF16, kind="Internal").ap() for i in range(2)]

        def W(name, a=0, n=None):
            lo, hi = W_HOME[name]
            return w_sb[:, lo + a:(hi if n is None else lo + a + n)]

        def R(name, a=0, n=None):
            lo, hi = R_AT[name]
            return row_sb[:, lo + a:(hi if n is None else lo + a + n)]

        def R2(name):
            return R(name).unsqueeze(1).to_broadcast([P, T, D])

        def C(name, i=0):
            lo = C_AT[name][0] + i
            return col_sb[:, lo:lo + 1]

        def K(name):
            return const_sb[:, K_AT[name][0]:K_AT[name][1]]

        def KB(name):
            return const_bf[:, K_AT[name][0] - K_BF:K_AT[name][1] - K_BF]

        def by_head(ap, heads):
            return ap.unsqueeze(1).to_broadcast([ap.shape[0], heads, ap.shape[1]])

        def has(name):
            return {n: i + 1 for i, n in enumerate(n for n in range(N) if (name, n, 0) in WORK)}

        X_TURNS, Y_TURNS, Z_TURNS = has("x_turn"), has("y_turn"), has("z_turn")
        KV_TURNS, COUNTS = has("kv_turn"), has("count")
        HIDDEN, at = {}, 0
        for n in range(N):
            if STEPS[n][0] in (L0C, L2C):
                at += 1 if STEPS[n][0] == L0C else 2
                HIDDEN[n] = at

        def step_of(layer, b):
            return STEPS.index((layer, b))

        STARTS_IN = {L0S: 0, L0C: 1, L1: 1, L2S: 0, L2C: 1, L3: 1}

        block = stack.enter_context(nc.Block())

        @block.sync
        def _(sp):
            sp.dma_start(x_turned[0][:, :], x_t[:, 0:S]).then_inc(x0_loaded, 16)
            sp.dma_start(w_sb[:, W_CUTS[0]:W_CUTS[1]], weights[:, W_CUTS[0]:W_CUTS[1]]).then_inc(w_loaded[0], 16)
            sp.dma_start(const_sb[:, :], consts[:, 0:K_F32]).then_inc(small_loaded, 16)
            sp.dma_start(const_f, consts[:, K_F32:K_N]).then_inc(small_loaded, 16)
            sp.dma_start(col_sb[:, :], cols).then_inc(small_loaded, 16)
            for b in range(1, B):
                sp.dma_start(x_turned[b][:, :], x_t[:, b * S:(b + 1) * S]).then_inc(x_loaded, 16)
            for b in range(B):
                sp.dma_start(res[b][0][:, :, :], x[b].rearrange("(t p) d -> p t d", p=P)).then_inc(tok_loaded, 16)
                sp.dma_start(ctx_sb[b][:, :, :], ctx[b].rearrange("(t p) d -> p t d", p=P)).then_inc(tok_loaded, 16)

            def stack_step(n):
                j, layer, b = ORD[n], *STEPS[n]
                slot = j % RING
                sp.wait_ge(parts_ready, j + 1)
                if j >= 2:
                    sp.wait_ge(stacked[(j - 2) % RING], 16 * 5 * ((j - 2) // RING + 1))
                sp.dma_start(bounce[j % 2].rearrange("w a p q -> p (w a) q"),
                             parts[j % 2][:, :, :, :].rearrange("p w a q -> p (w a) q")).then_inc(bounced[j % 2], 16)
                if layer in (L0S, L0C):
                    sp.wait_ge(key_row_ready, COUNTS[n])
                    row = key_row[b][:, :]
                else:
                    if j == ORD[step_of(L2S, 0)]:
                        sp.wait_ge(masks_ready, 1)
                    row = {L2S: zero_row[:, :], L2C: src_rows[:, b, :], L3: pad_row[:, :]}[layer]
                if j >= RING:
                    sp.wait_ge(pv_done, UNITS * NARROW[j - RING] + UNITS)
                sp.wait_ge(bounced[j % 2], 16 * (j // 2 + 1))
                src = bounce[j % 2]
                for a in range(PARTS):
                    part = src[0, a].rearrange("(d h) q -> d (h q)", h=H)
                    sp.dma_start(q_stack[slot][24 * a:24 * a + 24, :, :].rearrange("p h q -> p (h q)"),
                                 part.unsqueeze(0).to_broadcast([PARTS, DK, H * S])).then_inc(stacked[slot], 16)
                every = src[1].rearrange("a (d h) q -> (a d) (h q)", h=H)
                sp.dma_start(k_stack[slot][0:72, :, :].rearrange("p h q -> p (h q)"),
                             every.unsqueeze(0).to_broadcast([PARTS, PARTS * DK, H * S])).then_inc(stacked[slot], 16)
                sp.dma_start(k_stack[slot][MASK_ROW:MASK_ROW + 1, :, :], row).then_inc(stacked[slot], 16)

            sp.wait_ge(stacks_blank, 1)
            def late_weights(x):
                for name in LATE[x]:
                    lo, hi = W_AT[name]
                    sp.dma_start(W(name), weights[:, lo:hi]).then_inc(late_loaded[x], 16)

            for kind, n, _ in PLAN:
                if kind == "v" and narrow(n):
                    stack_step(n)
                    if n == B:
                        sp.wait_ge(work_full, WORK[("v", B - 1, 0)] + 1)
                        late_weights("first")
                    elif n == step_of(L2S, 0):
                        sp.wait_ge(work_full, WORK[("v", 2 * B - 1, 0)] + 1)
                        late_weights("second")
                    elif n == step_of(L2C, 0):
                        sp.wait_ge(work_full, WORK[("qk1", step_of(L1, B - 1), UNITS - 1)] + 1)
                        late_weights("third")
                elif kind == "nm":
                    j = ORD[n]
                    sp.wait_ge(nm_rows_ready, j + 1)
                    sp.dma_start(q_stack[j % RING][NEGMAX_ROW:NEGMAX_ROW + PARTS, :, :],
                                 nm_rows[j % 2][:, :]).then_inc(nm_stacked[j % RING], 16)
            for b in range(B):
                sp.wait_ge(result_ready, b + 1)
                sp.dma_start(out[b].rearrange("(t p) d -> p t d", p=P), res[b][0][:, :, :]).then_inc(stored, 16)
            sp.wait_ge(stored, 16 * B)

        @block.gpsimd
        def _(pool):
            steps = [0]

            def then(ins):
                steps[0] += 1
                ins.then_inc(pool_step, 1)
                pool.wait_ge(pool_step, steps[0])

            pool.dma_start(row_sb[:, :], rows.to_broadcast([P, R_N])).then_inc(rows_loaded, 16)
            for i in range(1, len(W_CUTS) - 1):
                a, z = W_CUTS[i], W_CUTS[i + 1]
                pool.dma_start(w_sb[:, a:z], weights[:, a:z]).then_inc(w_loaded[i], 16)
            for b in range(B):
                pool.dma_start(ctx_turned[b][:, :], ctx_t[:, b * S:(b + 1) * S]).then_inc(ctx_t_loaded, 16)
            pool.dma_start(int_src[:, :, :], src_mask.to_broadcast([H, B * S])).then_inc(masks_loaded, 16)
            pool.dma_start(int_tgt[:, 0, :, :], tgt_mask.rearrange("(t p) k -> p t k", p=P)).then_inc(masks_loaded, 16)
            pool.dma_start(int_tgt[:, 1, :, :], tgt_mask_t.rearrange("(t p) k -> p t k", p=P)).then_inc(masks_loaded, 16)
            for d in range(DK):
                pool.dma_start(int_key[H * d:H * d + H, :],
                               key_mask.unsqueeze(1).to_broadcast([B, H // B, S])).then_inc(masks_loaded, 16)
            for i in range(RING):
                for t in (q_stack[i], k_stack[i]):
                    then(nc.gpsimd.memset(t[:, :, :].rearrange("p h q -> p (h q)").bitcast(F32), 0.0))
                    then(nc.gpsimd.memset(t[MASK_ROW:ALL_ROWS, :, :], 1.0))
            for t in v_sb:
                then(nc.gpsimd.memset(t[:, :, :, :], 0.0))
                then(nc.gpsimd.memset(t[:, :, :, DK:DK + 1], 1.0))
            for t in q1_sb:
                then(nc.gpsimd.memset(t[:, :, :], 0.0))
            then(nc.gpsimd.memset(ones[:, :], 1.0))
            then(nc.gpsimd.memset(nm1_parts[:, :, :], 0.0))
            then(nc.gpsimd.memset(zero_row[:, :], 0.0))
            nc.gpsimd.memset(minus_half[:, :], -0.5).then_inc(stacks_blank, 1)
            pool.wait_ge(stacks_blank, 1)

            norms = [0]

            def inverse_root():
                norms[0] += 1
                pool.wait_ge(var_ready, norms[0])
                then(nc.gpsimd.tensor_scalar(var_eps[:, :], mean_var[:, :, 1], EPS, None, ALU.add))
                nc.gpsimd.tensor_tensor(rstd[:, :], var_eps[:, :], minus_half[:, :], ALU.pow).then_inc(rstd_ready, 1)

            for kind, n, _ in PLAN:
                for _ in range(norms_after(kind, n)):
                    inverse_root()
                if kind == "qk":
                    j = ORD[n]
                    q = qk_sb[j % 2]
                    p = parts[j % 2]
                    pool.wait_ge(qk_ready, j + 1)
                    if j >= 2:
                        pool.wait_ge(bounced[j % 2], 16 * (j // 2))
                    then(nc.gpsimd.tensor_copy(p[:, :, 0, :], q[:, :, :]))
                    then(nc.gpsimd.tensor_tensor(rest[:, :, :], q[:, :, :], p[:, :, 0, :], ALU.subtract))
                    then(nc.gpsimd.tensor_copy(p[:, :, 1, :], rest[:, :, :]))
                    nc.gpsimd.tensor_tensor(p[:, :, 2, :], rest[:, :, :], p[:, :, 1, :],
                                            ALU.subtract).then_inc(parts_ready, 1)
                    pool.wait_ge(parts_ready, j + 1)

        @block.tensor
        def _(pe):
            def mm(o, lhs, rhs, start):
                return nc.tensor.matmul(o, lhs, rhs, start=start, stop=True, skip_group_check=True)

            def turn(o, i, bf=False):
                ident = KB("ident") if bf else K("ident")
                return nc.tensor.transpose(o, i, ident)

            def bias(o, rhs):
                return mm(o, KB("ident"), rhs, False)

            def bank_heads(ps, heads, width, lo, hi):
                return ps[:, 0:heads * width].rearrange("p (h q) -> p h q", h=heads)[:, :, lo:hi]

            def scores(n, v):
                layer, b = STEPS[n]
                j = ORD[n]
                q, k = q_stack[j % RING], k_stack[j % RING]
                if v == 0:
                    pe.wait_ge(stacked[j % RING], 16 * 5 * (j // RING + 1))
                    if n == step_of(L2S, 0):
                        pe.wait_ge(masks_ready, 1)
                for x, (t, h0, heads, keys) in enumerate(score_banks(n, v)):
                    i = SBANK[("s", n, v, x)]
                    ps = s_ps[i % 2]
                    if i >= 2:
                        pe.wait_ge(s_free, i - 1)
                    for e in range(heads):
                        last = mm(ps[:, e * keys:(e + 1) * keys], q[0:SCORE_ROWS, h0 + e, t * P:(t + 1) * P],
                                  k[0:SCORE_ROWS, h0 + e, 0:keys], e == 0)
                    if layer == L0S:
                        last = bias(bank_heads(ps, heads, keys, t * P, (t + 1) * P), by_head(KB("causal"), heads))
                    elif layer == L2S:
                        last = bias(bank_heads(ps, heads, keys, 0, keys), by_head(tgt_bias[:, t, :], heads))
                    last.then_inc(s_full, 1)

            def scores_t(n, u):
                layer, b = STEPS[n]
                i = UNITS * n + u
                if i >= 2:
                    pe.wait_ge(exp_done, i - 1)
                ps = st_ps[i % 2]
                if wide(n):
                    pair = UNITS * b + u
                    pe.wait_ge(nm1_rows_ready, pair + 1)
                    q, k, nm = q1_sb[pair % 3], k1_sb[pair % 3], nm1_rows[pair % 2]
                    pick = KB("pick").rearrange("p (e k) -> p e k", e=2)
                    for t in range(T):
                        wq = S - t * P
                        for e in range(2):
                            o = ps[:, 512 * t + e * wq:512 * t + (e + 1) * wq]
                            mm(o, k[:, t * P:(t + 1) * P], q[:, e, t * P:S], e == 0)
                        for e in range(2):
                            o = ps[:, 512 * t + e * wq:512 * t + (e + 1) * wq]
                            mm(o, pick[:, e, :], nm[:, t * P:S], False)
                        last = bias(bank_heads(ps[:, 512 * t:512 * t + 512], 2, wq, 0, P), by_head(KB("causalT"), 2))
                    last.then_inc(st_full, 1)
                    return
                g, t = divmod(u, T)
                j = ORD[n]
                q, k = q_stack[j % RING], k_stack[j % RING]
                if u == 0:
                    pe.wait_ge(nm_stacked[j % RING], 16 * (j // RING + 1))
                lo = t * P if layer in CAUSAL else 0
                wq = S - lo
                for e in range(4):
                    last = mm(ps[:, e * wq:(e + 1) * wq], k[0:ALL_ROWS, 4 * g + e, t * P:(t + 1) * P],
                              q[0:ALL_ROWS, 4 * g + e, lo:S], (e * wq) % 512 == 0)
                if layer == L0S and t == 0:
                    for x in range(2):
                        last = bias(bank_heads(ps[:, 512 * x:512 * x + 512], 2, S, 0, P), by_head(KB("causalT"), 2))
                elif layer == L0S:
                    last = bias(bank_heads(ps, 4, P, 0, P), by_head(KB("causalT"), 4))
                elif layer == L2S:
                    for x in range(2):
                        last = bias(bank_heads(ps[:, 512 * x:512 * x + 512], 2, S, 0, S),
                                    by_head(tgt_bias_t[:, t, :], 2))
                last.then_inc(st_full, 1)

            def times_v(n, u):
                layer, b = STEPS[n]
                i = UNITS * n + u
                p = probs[i % 2]
                pe.wait_ge(exp_done, i + 1)
                if wide(n):
                    use = OUSE[(n, u)]
                    if u == 0:
                        pe.wait_ge(v1_ready, 4 * (b + 1))
                    pe.wait_ge(o_free, use)
                    for t in range(T):
                        wq = S - t * P
                        for e in range(2):
                            h = 2 * u + e
                            mm(o_ps[HS * e:HS * e + HS, t * P:S], v1_sb[b % 2][:, t, h * HS:(h + 1) * HS],
                               p[:, 512 * t + e * wq:512 * t + (e + 1) * wq], t == 0)
                    for t in range(T):
                        wq = S - t * P
                        for e in range(2):
                            last = mm(o_ps[HS * e:HS * e + HS, S + t * P:2 * S], ones[:, :],
                                      p[:, 512 * t + e * wq:512 * t + (e + 1) * wq], False)
                    last.then_inc(pv_done, 1)
                    return
                g, t = divmod(u, T)
                if u == 0:
                    pe.wait_ge(v_ready, ORD[n] + 1)
                if u % 4 == 0 and OUSE[(n, u // 4)]:
                    pe.wait_ge(o_free, OUSE[(n, u // 4)])
                lo = t * P if layer in CAUSAL else 0
                wq = S - lo
                for e in range(4):
                    last = mm(o_ps[32 * e:32 * e + 32, (g % 2) * S + lo:(g % 2) * S + S],
                              v_sb[b][:, t, 4 * g + e, :], p[:, e * wq:(e + 1) * wq], t == 0)
                last.then_inc(pv_done, 1)

            def qk_wide(n, u):
                b = STEPS[n][1]
                pair = UNITS * b + u
                if u == 0:
                    pe.wait_ge(y_turned_ready, Y_TURNS[step_of(L0C, b)])
                    pe.wait_ge(w_loaded[1], 16)
                    pe.wait_ge(w_loaded[2], 16)
                mm(m_ps[:, 0:S], W("L1.q", u * P, P), x_turned[b][:, :], True)
                return mm(m_ps[:, S:2 * S], W("L1.k", u * P, P), kvn_turned[b][:, :], False)

            def scores_wide(n, u):
                b = STEPS[n][1]
                pair = UNITS * b + u
                q, k = q1_sb[pair % 3], k1_sb[pair % 3]
                pe.wait_ge(qk1_ready, pair + 1)
                for x, t in enumerate((1, 0)):
                    i = SBANK[("s1", n, u, x)]
                    ps = s_ps[i % 2]
                    pe.wait_ge(s_free, i - 1)
                    keys = (t + 1) * P
                    for e in range(2):
                        mm(ps[:, e * keys:(e + 1) * keys], q[:, e, t * P:(t + 1) * P], k[:, 0:keys], e == 0)
                    bias(bank_heads(ps, 2, keys, t * P, (t + 1) * P), by_head(KB("causal"), 2)).then_inc(s_full, 1)

            def piece(kind, n, u):
                layer, b = STEPS[n]
                if kind == "qk":
                    if layer == L0S:
                        pe.wait_ge(*((x0_loaded, 16) if b == 0 else (x_loaded, 16 * (B - 1))))
                        pe.wait_ge(w_loaded[0], 16)
                        mm(m_ps[:, 0:S], W("L0.q1"), x_turned[b][:, :], True)
                        return mm(m_ps[:, S:], W("L0.k1"), x_turned[b][:, :], False)
                    if layer == L0C:
                        pe.wait_ge(x_turned_ready, X_TURNS[step_of(L0S, b)])
                        mm(m_ps[:, 0:S], W("L0.q2"), x_turned[b][:, :], True)
                        return mm(m_ps[:, S:], W("L0.k2"), ctxm_turned[b][:, :], False)
                    if layer == L2S:
                        pe.wait_ge(x_turned_ready, X_TURNS[step_of(L1, b)])
                        pe.wait_ge(late_loaded["first"], 16 * len(LATE["first"]))
                        mm(m_ps[:, 0:S], W("L2.q1"), x_turned[b][:, :], True)
                        return mm(m_ps[:, S:], W("L2.k1"), x_turned[b][:, :], False)
                    if layer == L2C:
                        pe.wait_ge(x_turned_ready, X_TURNS[step_of(L2S, b)])
                        pe.wait_ge(late_loaded["second"], 16 * len(LATE["second"]))
                        pe.wait_ge(ctx_t_loaded, 16 * B)
                        mm(m_ps[:, 0:S], W("L2.q2"), x_turned[b][:, :], True)
                        return mm(m_ps[:, S:], W("L2.k2"), ctx_turned[b][:, :], False)
                    pe.wait_ge(y_turned_ready, Y_TURNS[step_of(L2C, b)])
                    mm(m_ps[:, 0:S], W("L3.q"), x_turned[b][:, :], True)
                    return mm(m_ps[:, S:], W("L3.k"), ctx_turned[b][:, :], False)
                if kind == "v":
                    src = {L0S: x_turned, L0C: ctxm_turned, L2S: x_turned, L2C: ctx_turned, L3: ctx_turned}[layer][b]
                    w = {L0S: "L0.v1", L0C: "L0.v2", L2S: "L2.v1", L2C: "L2.v2", L3: "L3.v"}[layer]
                    for t in range(T):
                        last = mm(m_ps[:, t * P:(t + 1) * P], src[:, t * P:(t + 1) * P], W(w), t == 0)
                    return last
                if kind == "count":
                    pe.wait_ge(q0_ready, COUNTS[n])
                    return mm(m_ps[0:H, 0:S], q0_own[:, :], qk_sb[ORD[n] % 2][:, 1, :], True)
                if kind == "nm":
                    j = ORD[n]
                    pe.wait_ge(nm_parts_ready, j + 1)
                    for t in range(T):
                        last = turn(m_bf[0:PARTS * H, t * P:(t + 1) * P],
                                    nm_parts[j % 2][:, t, :, :].rearrange("p a h -> p (a h)"), bf=True)
                    return last
                if kind == "nm1":
                    pe.wait_ge(nm1_parts_ready, UNITS * b + u + 1)
                    for t in range(T):
                        last = turn(m_bf[:, t * P:(t + 1) * P], nm1_parts[:, t, :], bf=True)
                    return last
                if kind in ("turn0", "turn1"):
                    t = int(kind[-1])
                    if t == 0:
                        pe.wait_ge(o_ready, 2 * ORD[n] + 2)
                    for g in range(4):
                        last = turn(m_ps[:, g * P:(g + 1) * P], o_sb[:, g, t * P:(t + 1) * P])
                    return last
                if kind == "z_turn":
                    pe.wait_ge(z_ready, Z_TURNS[n])
                    for t in range(T):
                        last = turn(m_ps[:, t * P:(t + 1) * P], z_sb[:, t, :])
                    return last
                if kind == "out":
                    if layer == L1:
                        pe.wait_ge(w_loaded[3], 16)
                        pe.wait_ge(ctx1_ready, UNITS * (b + 1))
                        for t in range(T):
                            for p in range(UNITS):
                                last = mm(m_ps[:, t * P:(t + 1) * P], ctx1_t[:, p, t * P:(t + 1) * P],
                                          W("L1.o", p * P, P), t == 0 and p == 0)
                        return last
                    pe.wait_ge(z_turned_ready, Z_TURNS[n])
                    if layer == L2C:
                        pe.wait_ge(late_loaded["third"], 16 * len(LATE["third"]))
                    for t in range(T):
                        last = mm(m_ps[:, t * P:(t + 1) * P], z_turned[:, t * P:(t + 1) * P],
                                  W("L2.o1" if layer == L2S else "L2.o2"), t == 0)
                    return last
                if kind == "x_turn":
                    pe.wait_ge(x_ready, X_TURNS[n])
                    r = res[b][x_buffer(layer)]
                    for t in range(T):
                        last = turn(m_ps[:, t * P:(t + 1) * P], r[:, t, :])
                    if layer == L0S:
                        for t in range(T):
                            last = turn(m_ps[:, S + t * P:S + (t + 1) * P], ctxm_sb[:, t, :])
                    return last
                if kind == "kv_turn":
                    pe.wait_ge(kv_ready, KV_TURNS[n])
                    for t in range(T):
                        last = turn(m_ps[:, t * P:(t + 1) * P], kvn_sb[:, t, :])
                    return last
                if kind == "ff1":
                    pe.wait_ge(x_turned_ready, X_TURNS[n])
                    pe.wait_ge(w_loaded[1], 16)
                    return mm(m_ps[:, 0:S], W("L0.fc1"), x_turned[b][:, :], True)
                if kind in ("ff1a", "ff1b"):
                    pe.wait_ge(x_turned_ready, X_TURNS[n])
                    for x in range(2):
                        c = (2 if kind == "ff1b" else 0) + x
                        last = mm(m_ps[:, x * S:(x + 1) * S], W("L2.f1", c * P, P), x_turned[b][:, :], x == 0)
                    return last
                if kind == "ff2":
                    pe.wait_ge(hidden_ready, HIDDEN[n])
                    name, cs = ("L0.fc2", 1) if layer == L0C else ("L2.f2", 4)
                    for t in range(T):
                        for c in range(cs):
                            last = mm(m_ps[:, t * P:(t + 1) * P], hidden[:, c, t * P:(t + 1) * P],
                                      W(name, c * P, P), t == 0 and c == 0)
                    return last
                if kind == "y_turn":
                    pe.wait_ge(y_ready, Y_TURNS[n])
                    r = y_sb if layer == L0C else res[b][1]
                    for t in range(T):
                        last = turn(m_ps[:, t * P:(t + 1) * P], r[:, t, :])
                    return last
                if kind.startswith("v1_"):
                    t, half = divmod(int(kind[-1]), 2)
                    if kind == "v1_0":
                        pe.wait_ge(kv_turned_ready, KV_TURNS[step_of(L0S, b)])
                        pe.wait_ge(w_loaded[2], 16)
                    return mm(m_ps[:, :], kvn_turned[b][:, t * P:(t + 1) * P], W("L1.v", half * 512, 512), True)
                raise ValueError(kind)

            pe.wait_ge(small_loaded, 48)
            pe.wait_ge(consts_ready, 2)
            pe.wait_ge(stacks_blank, 1)
            for kind, n, u in PLAN:
                if kind == "st":
                    scores_t(n, u)
                elif kind == "pv":
                    times_v(n, u)
                elif kind == "s":
                    scores(n, u)
                elif kind == "s1":
                    scores_wide(n, u)
                else:
                    use = WORK[(kind, n, u)]
                    if use:
                        pe.wait_ge(work_free, use)
                    made = qk_wide(n, u) if kind == "qk1" else piece(kind, n, u)
                    made.then_inc(work_full, 1)

        @block.scalar
        def _(act):
            def full(kind, n, u=0):
                act.wait_ge(work_full, WORK[(kind, n, u)] + 1)

            def biased(o, i, c):
                return nc.scalar.activation(o, i, ACT.Identity, bias=c, scale=1.0)

            act.wait_ge(small_loaded, 48)
            act.wait_ge(stacks_blank, 1)
            for kind, n, u in PLAN:
                layer, b = STEPS[n]
                if kind == "st":
                    i = UNITS * n + u
                    if i >= 2:
                        act.wait_ge(pv_done, i - 1)
                    act.wait_ge(st_full, i + 1)
                    if wide(n):
                        size, scale = 3 * S, HS ** -0.5
                    else:
                        size, scale = (512 if layer in CAUSAL and u % T else 1024), DK ** -0.5
                    nc.scalar.activation(probs[i % 2][:, 0:size], st_ps[i % 2][:, 0:size], ACT.Exp,
                                         scale=scale).then_inc(exp_done, 1)
                elif kind == "pv" and narrow(n) and u % 4 == 3:
                    half = u // 4
                    act.wait_ge(pv_done, UNITS * n + u + 1)
                    j = ORD[n]
                    if j and half == 0:
                        act.wait_ge(work_full, WORK[("turn1", NARROW[j - 1], 0)] + 1)
                    nc.scalar.activation(o_sb[:, 2 * half:2 * half + 2, :],
                                         o_ps[:, :].rearrange("p (g q) -> p g q", g=2), ACT.Copy).then_inc(o_free, 1)
                    act.wait_ge(o_free, OUSE[(n, half)] + 1)
                    act.sem_inc(o_ready, 1)
                elif kind == "qk":
                    full(kind, n)
                    j = ORD[n]
                    q = qk_sb[j % 2]
                    if j >= 2:
                        act.wait_ge(parts_ready, j - 1)
                        if ("count", NARROW[j - 2], 0) in WORK:
                            act.wait_ge(work_full, WORK[("count", NARROW[j - 2], 0)] + 1)
                    if layer in (L0S, L0C):
                        nc.scalar.activation(q[:, :, :], m_ps[:, :].rearrange("p (w q) -> p w q", w=2),
                                             ACT.Copy).then_inc(work_free, 1)
                    else:
                        bq, bk = {L2S: ("L2.bq1", "L2.bk1"), L2C: ("L2.bq2", "L2.bk2"), L3: ("L3.bq", "L3.bk")}[layer]
                        if layer == L3:
                            if b == 0:
                                act.wait_ge(masks_ready, 1)
                            nc.scalar.activation(q[:, 0, :], m_ps[:, 0:S], ACT.Identity, bias=q_gate_bias[:, :],
                                                 scale=q_gate[:, :])
                        else:
                            biased(q[:, 0, :], m_ps[:, 0:S], C(bq))
                        biased(q[:, 1, :], m_ps[:, S:2 * S], C(bk)).then_inc(work_free, 1)
                    act.wait_ge(work_free, WORK[(kind, n, 0)] + 1)
                    act.sem_inc(qk_ready, 1)
                elif kind == "nm":
                    full(kind, n)
                    j = ORD[n]
                    if j >= 2:
                        act.wait_ge(nm_stacked[(j - 2) % RING], 16 * ((j - 2) // RING + 1))
                    nc.scalar.activation(nm_rows[j % 2][:, :], m_bf[0:PARTS * H, 0:S], ACT.Copy).then_inc(work_free, 1)
                    act.wait_ge(work_free, WORK[(kind, n, 0)] + 1)
                    act.sem_inc(nm_rows_ready, 1)
                elif kind == "nm1":
                    pair = UNITS * b + u
                    full(kind, n, u)
                    if pair >= 2:
                        act.wait_ge(st_full, UNITS * step_of(L1, 0) + pair - 1)
                    nc.scalar.activation(nm1_rows[pair % 2][:, :], m_bf[:, 0:S], ACT.Copy).then_inc(work_free, 1)
                    act.wait_ge(work_free, WORK[(kind, n, u)] + 1)
                    act.sem_inc(nm1_rows_ready, 1)
                elif kind == "qk1":
                    pair = UNITS * b + u
                    full(kind, n, u)
                    if pair >= 3:
                        act.wait_ge(st_full, UNITS * step_of(L1, 0) + pair - 2)
                    for e in range(2):
                        half = slice(HS * e, HS * e + HS)
                        lo = C_AT["L1.bq"][0] + u
                        nc.scalar.activation(q1_sb[pair % 3][half, e, :], m_ps[half, 0:S], ACT.Identity,
                                             bias=col_sb[half, lo:lo + 1], scale=1.0)
                    biased(k1_sb[pair % 3][:, :], m_ps[:, S:2 * S], C("L1.bk", u)).then_inc(work_free, 1)
                    act.wait_ge(work_free, WORK[(kind, n, u)] + 1)
                    act.sem_inc(qk1_ready, 1)
                elif kind == "z_turn":
                    full(kind, n)
                    nc.scalar.activation(z_turned[:, :], m_ps[:, 0:S], ACT.Copy).then_inc(work_free, 1)
                    act.wait_ge(work_free, WORK[(kind, n, 0)] + 1)
                    act.sem_inc(z_turned_ready, 1)
                elif kind == "x_turn":
                    full(kind, n)
                    if layer == L0S:
                        nc.scalar.activation(ctxm_turned[b][:, :], m_ps[:, S:2 * S], ACT.Copy)
                    nc.scalar.activation(x_turned[b][:, :], m_ps[:, 0:S], ACT.Copy).then_inc(work_free, 1)
                    act.wait_ge(work_free, WORK[(kind, n, 0)] + 1)
                    act.sem_inc(x_turned_ready, 1)
                elif kind == "kv_turn":
                    full(kind, n)
                    nc.scalar.activation(kvn_turned[b][:, :], m_ps[:, 0:S], ACT.Copy).then_inc(work_free, 1)
                    act.wait_ge(work_free, WORK[(kind, n, 0)] + 1)
                    act.sem_inc(kv_turned_ready, 1)
                elif kind == "y_turn":
                    full(kind, n)
                    nc.scalar.activation(x_turned[b][:, :], m_ps[:, 0:S], ACT.Copy).then_inc(work_free, 1)
                    act.wait_ge(work_free, WORK[(kind, n, 0)] + 1)
                    act.sem_inc(y_turned_ready, 1)
                elif kind in ("ff1", "ff1a", "ff1b"):
                    full(kind, n)
                    cs = {"ff1": [0], "ff1a": [0, 1], "ff1b": [2, 3]}[kind]
                    for x, c in enumerate(cs):
                        ins = nc.scalar.activation(hidden[:, c, :], m_ps[:, x * S:(x + 1) * S], ACT.Relu,
                                                   bias=C("L0.fc1b") if layer == L0C else C("L2.bf1", c), scale=1.0)
                    ins.then_inc(work_free, 1)
                    act.wait_ge(work_free, WORK[(kind, n, 0)] + 1)
                    act.sem_inc(hidden_ready, 1)

        @block.vector
        def _(dve):
            steps = [0]

            def then(ins):
                steps[0] += 1
                ins.then_inc(dve_step, 1)
                dve.wait_ge(dve_step, steps[0])

            def full(kind, n, u=0):
                dve.wait_ge(work_full, WORK[(kind, n, u)] + 1)

            v = nc.vector
            dve.wait_ge(small_loaded, 48)
            v.tensor_copy(const_bf[:, 0:P], K("ident")).then_inc(consts_ready, 1)
            v.tensor_copy(const_bf[:, P:K_N - K_BF], const_f).then_inc(consts_ready, 1)
            dve.wait_ge(tok_loaded, 16 * 2 * B)
            dve.wait_ge(rows_loaded, 16)
            for b in range(B):
                then(v.tensor_reduce(absmax[:, :], res[b][0][:, :, :], AX.X, ALU.max, apply_absolute_value=True))
                then(v.tensor_scalar(live0[b][:, :], absmax[:, :], 0.0, None, ALU.not_equal))
            dve.wait_ge(stacks_blank, 1)

            def masks():
                dve.wait_ge(masks_loaded, 16 * (3 + DK))
                then(v.tensor_scalar(src_rows[:, :, :], int_src[:, :, :], 0.0, NEG, ALU.is_equal, ALU.mult))
                then(v.tensor_scalar(tgt_bias[:, :, :], int_tgt[:, 0, :, :], 0.0, NEG, ALU.is_equal, ALU.mult))
                then(v.tensor_scalar(tgt_bias_t[:, :, :], int_tgt[:, 1, :, :], 0.0, NEG, ALU.is_equal, ALU.mult))
                then(v.tensor_copy(key_f[:, :], int_key[:, :]))
                then(v.tensor_reduce(key_min[:, :], key_f[:, :], AX.X, ALU.min))
                then(v.tensor_scalar(q_gate[:, :], key_min[:, :], 0.0, None, ALU.is_equal))
                then(v.tensor_tensor(q_gate_bias[:, :], q_gate[:, :], C("L3.bq"), ALU.mult))
                v.tensor_scalar(pad_row[:, :], key_f[0:H, :], key_min[0:H, :], PAD * DK ** 0.5, ALU.subtract,
                                ALU.mult).then_inc(masks_ready, 1)

            norms = [0]

            def layer_norm(o, y, g, beta, sem_of=None):
                for t in range(T):
                    ins = v.bn_stats(stats[:, t, :], y[:, t, :])
                then(ins)
                for t in range(T):
                    ins = v.bn_aggr(mean_var[:, t, :], stats[:, t, :])
                ins.then_inc(var_ready, 1)
                norms[0] += 1
                dve.wait_ge(rstd_ready, norms[0])
                for t in range(T):
                    ins = v.tensor_scalar(xh_sb[:, t, :], y[:, t, :], mean_var[:, t, 0:1], rstd[:, t:t + 1],
                                          ALU.subtract, ALU.mult)
                then(ins)
                then(v.tensor_tensor(xh_sb[:, :, :], xh_sb[:, :, :], R2(g), ALU.mult))
                ins = v.tensor_tensor(o, xh_sb[:, :, :], R2(beta), ALU.add)
                if sem_of is None:
                    then(ins)
                else:
                    ins.then_inc(sem_of, 1)

            def row_mask(live, r):
                then(v.tensor_reduce(absmax[:, :], r[:, :, :], AX.X, ALU.max, apply_absolute_value=True))
                then(v.tensor_scalar(live[:, :], absmax[:, :], 0.0, None, ALU.not_equal))

            def split(src, rest_, p):
                then(v.tensor_scalar(src, src, CAP, None, ALU.min))
                then(v.tensor_copy(p(0), src))
                then(v.tensor_tensor(rest_, src, p(0), ALU.subtract))
                then(v.tensor_copy(p(1), rest_))
                return v.tensor_tensor(p(2), rest_, p(1), ALU.subtract)

            for kind, n, u in PLAN:
                layer, b = STEPS[n]
                old = res[b][STARTS_IN[layer]]
                if kind == "s":
                    j = ORD[n]
                    for x, (t, h0, heads, keys) in enumerate(score_banks(n, u)):
                        i = SBANK[("s", n, u, x)]
                        dve.wait_ge(s_full, i + 1)
                        v.tensor_reduce(negmax[j % 2][:, t, h0:h0 + heads],
                                        s_ps[i % 2][:, 0:heads * keys].rearrange("p (h k) -> p h k", h=heads),
                                        AX.X, ALU.max, negate=True).then_inc(s_free, 1)
                        last_bank = i + 1
                    if u == UNITS - 1:
                        dve.wait_ge(s_free, last_bank)
                        if j >= 2:
                            dve.wait_ge(work_full, WORK[("nm", NARROW[j - 2], 0)] + 1)
                        p = nm_parts[j % 2]
                        split(negmax[j % 2][:, :, :], nm_rest[:, :, :],
                              lambda a: p[:, :, a, :]).then_inc(nm_parts_ready, 1)
                elif kind == "s1":
                    pair = UNITS * b + u
                    for x, t in enumerate((1, 0)):
                        i = SBANK[("s1", n, u, x)]
                        keys = (t + 1) * P
                        dve.wait_ge(s_full, i + 1)
                        v.tensor_reduce(nm1[:, t, :],
                                        s_ps[i % 2][:, 0:2 * keys].rearrange("p (h k) -> p h k", h=2),
                                        AX.X, ALU.max, negate=True).then_inc(s_free, 1)
                    dve.wait_ge(s_free, i + 1)
                    if pair:
                        pn, pu = divmod(UNITS * n + u - 1, UNITS)
                        dve.wait_ge(work_full, WORK[("nm1", pn, pu)] + 1)
                    split(nm1[:, :, :], nm1_rest[:, :, :],
                          lambda a: nm1_parts[:, :, 2 * a:2 * a + 2]).then_inc(nm1_parts_ready, 1)
                elif kind == "pv" and wide(n):
                    dve.wait_ge(pv_done, UNITS * n + u + 1)
                    then(v.reciprocal(rec1[:, :], o_ps[:, S:2 * S]))
                    if u == 0 and b:
                        dve.wait_ge(work_full, WORK[("out", n - 1, 0)] + 1)
                    v.tensor_tensor(ctx1_t[:, u, :], o_ps[:, 0:S], rec1[:, :], ALU.mult).then_inc(o_free, 1)
                    dve.wait_ge(o_free, OUSE[(n, u)] + 1)
                    dve.sem_inc(ctx1_ready, 1)
                elif kind == "qk" and layer in (L0S, L0C):
                    dve.wait_ge(qk_ready, ORD[n] + 1)
                    if COUNTS[n] > 1:
                        dve.wait_ge(work_full, WORK[("count", n - 1, 0)] + 1)
                    v.tensor_scalar(q0_own[:, :], K("own_head"), qk_sb[ORD[n] % 2][:, 0, 0:1], None,
                                    ALU.mult).then_inc(q0_ready, 1)
                elif kind == "count":
                    full(kind, n)
                    if layer == L0C:
                        j = ORD[step_of(L0S, b)]
                        dve.wait_ge(stacked[j % RING], 16 * 5 * (j // RING + 1))
                    v.tensor_scalar(nonzero[:, :], m_ps[0:H, 0:S], 0.0, None, ALU.not_equal).then_inc(work_free, 1)
                    dve.wait_ge(work_free, WORK[(kind, n, 0)] + 1)
                    then(v.tensor_reduce(length[:, :], nonzero[:, :], AX.X, ALU.add))
                    lo, hi = K_AT["key"]
                    v.tensor_scalar(key_row[b][:, :], const_sb[0:H, lo:hi], length[:, :], NEG, ALU.is_ge,
                                    ALU.mult).then_inc(key_row_ready, 1)
                elif kind == "v":
                    full(kind, n)
                    if n >= B:
                        dve.wait_ge(pv_done, UNITS * (n - B) + UNITS)
                    o = v_sb[b][:, :, :, 0:DK]
                    i = m_ps[:, 0:S].rearrange("p (t h d) -> p t h d", t=T, d=DK)
                    bv = {L2S: "L2.bv1", L2C: "L2.bv2", L3: "L3.bv"}.get(layer)
                    for t in range(T):
                        if bv is None:
                            ins = v.tensor_copy(o[:, t], i[:, t])
                        else:
                            ins = v.tensor_tensor(o[:, t], i[:, t], R(bv).rearrange("p (h d) -> p h d", d=DK), ALU.add)
                    ins.then_inc(work_free, 1)
                    dve.wait_ge(work_free, WORK[(kind, n, 0)] + 1)
                    dve.sem_inc(v_ready, 1)
                elif kind.startswith("v1_"):
                    t, half = divmod(int(kind[-1]), 2)
                    full(kind, n)
                    if kind == "v1_0" and b >= 2:
                        dve.wait_ge(pv_done, UNITS * (n - 2) + UNITS)
                    v.tensor_tensor(v1_sb[b % 2][:, t, half * 512:half * 512 + 512], m_ps[:, :],
                                    R("L1.bv", half * 512, 512), ALU.add).then_inc(work_free, 1)
                    dve.wait_ge(work_free, WORK[(kind, n, 0)] + 1)
                    dve.sem_inc(v1_ready, 1)
                elif kind in ("turn0", "turn1"):
                    t = int(kind[-1])
                    full(kind, n)
                    heads = m_ps[:, :].rearrange("p (h w) -> p h w", w=32)
                    then(v.reciprocal(rec[:, :], heads[:, :, DK]))
                    if t == 0 and layer in (L2S, L2C) and Z_TURNS[n] > 1:
                        last = [m for m in Z_TURNS if m < n][-1]
                        dve.wait_ge(work_full, WORK[("z_turn", last, 0)] + 1)
                    v.tensor_tensor(z_sb[:, t, :].rearrange("p (h d) -> p h d", d=DK), heads[:, :, 0:DK],
                                    rec[:, :].unsqueeze(2).to_broadcast([P, H, DK]), ALU.mult).then_inc(work_free, 1)
                    if t == 0:
                        continue
                    dve.wait_ge(work_free, WORK[(kind, n, 0)] + 1)
                    if layer in (L2S, L2C):
                        dve.sem_inc(z_ready, 1)
                        continue
                    if layer == L3:
                        then(v.tensor_tensor(y_sb[:, :, :], z_sb[:, :, :], old[:, :, :], ALU.add))
                        layer_norm(res[b][0][:, :, :], y_sb, "L3.g", "L3.b", result_ready)
                        continue
                    live = live0[b] if layer == L0S else live1[b]
                    for t in range(T):
                        ins = v.scalar_tensor_tensor(out=y_sb[:, t, :], in0=z_sb[:, t, :], scalar=live[:, t:t + 1],
                                                     in1=old[:, t, :], op0=ALU.mult, op1=ALU.add)
                    then(ins)
                    if layer == L0C:
                        layer_norm(res[b][0][:, :, :], y_sb, "L0.g2", "L0.b2", x_ready)
                        continue
                    layer_norm(res[b][1][:, :, :], y_sb, "L0.g1", "L0.b1")
                    row_mask(live1[b], res[b][1])
                    if b:
                        dve.wait_ge(work_full, WORK[("x_turn", n - 1, 0)] + 1)
                    for t in range(T):
                        ins = v.tensor_scalar(ctxm_sb[:, t, :], ctx_sb[b][:, t, :], live1[b][:, t:t + 1], None, ALU.mult)
                    ins.then_inc(x_ready, 1)
                    if b:
                        dve.wait_ge(work_full, WORK[("kv_turn", n - 1, 0)] + 1)
                    layer_norm(kvn_sb[:, :, :], ctx_sb[b], "L1.g", "L1.b", kv_ready)
                elif kind == "out":
                    full(kind, n)
                    bo = {L1: "L1.bo", L2S: "L2.bo1", L2C: "L2.bo2"}[layer]
                    v.tensor_tensor(y_sb[:, :, :], m_ps[:, 0:S].rearrange("p (t d) -> p t d", t=T), old[:, :, :],
                                    ALU.add).then_inc(work_free, 1)
                    dve.wait_ge(work_free, WORK[(kind, n, 0)] + 1)
                    if layer == L1:
                        v.tensor_tensor(res[b][0][:, :, :], y_sb[:, :, :], R2(bo), ALU.add).then_inc(x_ready, 1)
                    else:
                        then(v.tensor_tensor(y_sb[:, :, :], y_sb[:, :, :], R2(bo), ALU.add))
                        g, be = ("L2.g1", "L2.be1") if layer == L2S else ("L2.g2", "L2.be2")
                        layer_norm(res[b][x_buffer(layer)][:, :, :], y_sb, g, be, x_ready)
                elif kind == "ff2":
                    full(kind, n)
                    bf, g, be = ("L0.fc2b", "L0.g3", "L0.b3") if layer == L0C else ("L2.bf2", "L2.g3", "L2.be3")
                    x2 = res[b][0]
                    v.tensor_tensor(z_sb[:, :, :], m_ps[:, 0:S].rearrange("p (t d) -> p t d", t=T), R2(bf),
                                    ALU.add).then_inc(work_free, 1)
                    dve.wait_ge(work_free, WORK[(kind, n, 0)] + 1)
                    if layer == L0C:
                        for t in range(T):
                            ins = v.scalar_tensor_tensor(out=y_sb[:, t, :], in0=z_sb[:, t, :],
                                                         scalar=live0[b][:, t:t + 1], in1=x2[:, t, :],
                                                         op0=ALU.mult, op1=ALU.add)
                        then(ins)
                        layer_norm(res[b][1][:, :, :], y_sb, g, be)
                        layer_norm(y_sb[:, :, :], res[b][1], "L1.g", "L1.b", y_ready)
                    else:
                        then(v.tensor_tensor(y_sb[:, :, :], z_sb[:, :, :], x2[:, :, :], ALU.add))
                        layer_norm(res[b][1][:, :, :], y_sb, g, be, y_ready)
                elif kind == "y_turn" and layer == L0C:
                    full(kind, n)
                    if n == step_of(L0C, 0):
                        masks()


def x_buffer(layer):
    return {L0S: 1, L0C: 0, L1: 0, L2S: 1, L2C: 0}[layer]


def norms_after(kind, n):
    layer = STEPS[n][0]
    if kind == "turn1":
        return {L0S: 2, L0C: 1, L2S: 0, L2C: 0, L3: 1}[layer]
    if kind == "out":
        return {L1: 0, L2S: 1, L2C: 1}[layer]
    if kind == "ff2":
        return {L0C: 2, L2C: 1}[layer]
    return 0


def shape_constants():
    c = np.zeros((P, K_N), np.float32)
    i = np.arange(P)
    c[:, slice(*K_AT["ident"])] = np.eye(P)
    c[:, slice(*K_AT["causal"])] = np.where(i[None, :] > i[:, None], NEG, 0)
    c[:, slice(*K_AT["causalT"])] = np.where(i[:, None] > i[None, :], NEG, 0)
    c[:, slice(*K_AT["own_head"])] = i[:, None] % H == np.arange(H)[None, :]
    c[:, slice(*K_AT["key"])] = np.arange(S)[None, :]
    pick = np.zeros((P, 2, P), np.float32)
    for a in range(PARTS):
        for e in range(2):
            pick[2 * a + e, e, :] = 1
    c[:, slice(*K_AT["pick"])] = pick.reshape(P, 2 * P)
    return c


def kernel(**inputs):
    import concourse.bacc as bacc
    from concourse.bass_utils import run_bass_kernel_spmd

    a = {k: np.asarray(v) for k, v in inputs.items()}

    def l0(name):
        return a[f"L0_xattn_{name}"]

    def by_depth(w):
        return w.reshape(D, H, DK).transpose(0, 2, 1).reshape(D, D)

    def tiles(w):
        return w.reshape(-1, P, w.shape[1]).transpose(1, 0, 2).reshape(P, -1)

    def l2(name):
        return a[f"L2_xattn_{name}"]

    def l3(name):
        return a[f"L3_xattn_{name}"]

    wkv = a["L1_xattn_wkv"]
    w = {"L0.fc1": l0("fc1_w").T, "L0.fc2": l0("fc2_w").T, "L1.q": a["L1_xattn_wq"], "L1.k": wkv[:, :H * HS],
         "L1.v": wkv[:, H * HS:], "L1.o": tiles(a["L1_xattn_wo"]), "L2.f1": l2("Wf1").T, "L2.f2": tiles(l2("Wf2").T),
         "L3.q": by_depth(l3("wq").T), "L3.k": by_depth(l3("wk").T), "L3.v": l3("wv").T}
    for i in "12":
        w[f"L0.q{i}"] = l0(f"Wq{i}").transpose(1, 2, 0).reshape(D, D)
        w[f"L0.k{i}"] = l0(f"Wk{i}").transpose(1, 2, 0).reshape(D, D)
        w[f"L0.v{i}"] = l0(f"Wv{i}").transpose(1, 0, 2).reshape(D, D)
        w[f"L2.q{i}"] = by_depth(l2(f"Wq{i}").T)
        w[f"L2.k{i}"] = by_depth(l2(f"Wk{i}").T)
        w[f"L2.v{i}"] = l2(f"Wv{i}").T
        w[f"L2.o{i}"] = l2(f"Wo{i}").T
    r = {"L0.fc2b": l0("fc2_b"), "L1.g": a["L1_xattn_ln_g"], "L1.b": a["L1_xattn_ln_b"],
         "L1.bv": a["L1_xattn_bkv"][H * HS:], "L1.bo": a["L1_xattn_bo"], "L2.bv1": l2("bv1"), "L2.bo1": l2("bo1"),
         "L2.bv2": l2("bv2"), "L2.bo2": l2("bo2"), "L2.bf2": l2("bf2"), "L3.bv": l3("bv"), "L3.g": l3("gamma"),
         "L3.b": l3("beta")}
    for i in "123":
        r[f"L0.g{i}"], r[f"L0.b{i}"] = l0(f"ln{i}_g"), l0(f"ln{i}_b")
        r[f"L2.g{i}"], r[f"L2.be{i}"] = l2(f"g{i}"), l2(f"be{i}")

    def depth_col(v):
        return v.reshape(H, DK).T.reshape(P, 1)

    c = {"L0.fc1b": l0("fc1_b").reshape(P, 1), "L1.bq": a["L1_xattn_bq"].reshape(UNITS, P).T,
         "L1.bk": a["L1_xattn_bkv"][:H * HS].reshape(UNITS, P).T, "L2.bq1": depth_col(l2("bq1")),
         "L2.bk1": depth_col(l2("bk1")), "L2.bq2": depth_col(l2("bq2")), "L2.bk2": depth_col(l2("bk2")),
         "L2.bf1": l2("bf1").reshape(4, P).T, "L3.bq": depth_col(l3("bq")), "L3.bk": depth_col(l3("bk"))}
    tgt = a["mask_1x1xSxS2_ik0"].reshape(S, S)
    arrays = {
        "x": a["x"], "x_t": a["x"].reshape(B * S, D).T, "ctx": a["ctx_1024"], "ctx_t": a["ctx_1024"].reshape(B * S, D).T,
        "weights": np.concatenate([w[name] for name, _ in WEIGHTS], axis=1),
        "rows": np.concatenate([r[name] for name, _ in ROWS]).reshape(1, R_N),
        "cols": np.concatenate([c[name] for name, _ in COLS], axis=1),
        "consts": shape_constants(),
        "src_mask": a["mask_Bx1x1xS2_if1"].reshape(1, B * S), "tgt_mask": tgt, "tgt_mask_t": tgt.T,
        "key_mask": a["mask_BxS2_ik0"],
    }
    arrays = {k: np.ascontiguousarray(v) for k, v in arrays.items()}
    nc = bacc.Bacc("TRN2", target_bir_lowering=False, num_devices=1)
    aps = {k: nc.dram_tensor(f"{k}_dram", v.shape, mybir.dt.from_np(v.dtype), kind="ExternalInput").ap()
           for k, v in arrays.items()}
    out = nc.dram_tensor("out_dram", (B, S, D), F32, kind="ExternalOutput").ap()
    attention_stack_program(nc, out=out, **aps)
    ran = run_bass_kernel_spmd(nc, [{f"{k}_dram": v for k, v in arrays.items()}], core_ids=[0])
    return ran.results[0]["out_dram"]
```

```python
from contextlib import ExitStack

import numpy as np

import concourse.bass as bass
from concourse import mybir

F32 = mybir.dt.float32
BF16 = mybir.dt.bfloat16
I32 = mybir.dt.int32
ALU = mybir.AluOpType
ACT = mybir.ActivationFunctionType
AX = mybir.AxisListType

P = 128
B, S, D, H = 4, 256, 128, 16
DK = D // H
HS = 64
T = S // P
EPS = 1e-5
NEG = -(2.0 ** 126)
CAP = 2.0 ** 125
PAD = float(-2 ** 32 + 1)
PARTS = 3
MASK_ROW = 96
NEGMAX_ROW = 97
SCORE_ROWS = MASK_ROW + 1
ALL_ROWS = NEGMAX_ROW + PARTS
RING = 3

L0S, L0C, L1, L2S, L2C, L3 = range(6)
LAYERS = [L0S, L0C, L1, L2S, L2C, L3]
STEPS = [(layer, b) for layer in LAYERS for b in range(B)]
N = len(STEPS)
CAUSAL = (L0S, L1)
UNITS = 8

WEIGHTS = [("L0.q1", 128), ("L0.k1", 128), ("L0.v1", 128), ("L0.q2", 128), ("L0.k2", 128), ("L0.v2", 128),
           ("L0.fc1", 128), ("L0.fc2", 128), ("L1.q", 1024), ("L1.k", 1024), ("L1.v", 1024), ("L1.o", 1024),
           ("L2.q1", 128), ("L2.k1", 128), ("L2.v1", 128), ("L2.o1", 128),
           ("L2.q2", 128), ("L2.k2", 128), ("L2.v2", 128), ("L2.o2", 128), ("L2.f1", 512), ("L2.f2", 512),
           ("L3.q", 128), ("L3.k", 128), ("L3.v", 128)]
ROWS = [("L0.g1", 128), ("L0.b1", 128), ("L0.g2", 128), ("L0.b2", 128), ("L0.g3", 128), ("L0.b3", 128),
        ("L0.fc2b", 128), ("L1.g", 128), ("L1.b", 128), ("L1.bv", 1024), ("L1.bo", 128),
        ("L2.bo1", 128), ("L2.g1", 128), ("L2.be1", 128), ("L2.bo2", 128), ("L2.g2", 128), ("L2.be2", 128),
        ("L2.bf2", 128), ("L2.g3", 128), ("L2.be3", 128), ("L3.bv", 128), ("L3.g", 128), ("L3.b", 128)]
COLS = [("L0.fc1b", 1), ("L1.bq", 8), ("L1.bk", 8), ("L2.bq1", 1), ("L2.bk1", 1), ("L2.bq2", 1), ("L2.bk2", 1),
        ("L2.bf1", 4), ("L2.bv1", 1), ("L2.bv2", 1), ("L3.bq", 1), ("L3.bk", 1)]
CONSTS = [("own_head", 16), ("key", 256), ("ident", 128), ("causal", 128), ("causalT", 128)]


def offsets(table):
    at, found = 0, {}
    for name, n in table:
        found[name] = (at, at + n)
        at += n
    return found, at


W_AT, W_N = offsets(WEIGHTS)
W_HOME = dict(W_AT)
W_HOME.update({f"L2.{x}1": W_AT[f"L0.{x}1"] for x in "qkv"} | {f"L2.{x}2": W_AT[f"L0.{x}2"] for x in "qkv"})
RESIDENT = W_AT["L2.q1"][0]
W_HOME["L2.o1"] = (RESIDENT, RESIDENT + P)
W_HOME["L2.f1"] = (W_AT["L1.q"][0], W_AT["L1.q"][0] + 512)
W_HOME["L2.f2"] = (W_AT["L1.q"][0] + 512, W_AT["L1.q"][1])
for i, name in enumerate(("L2.o2", "L3.q", "L3.k", "L3.v")):
    W_HOME[name] = (W_AT["L1.k"][0] + i * P, W_AT["L1.k"][0] + (i + 1) * P)
LATE = {"first": ["L2.q1", "L2.k1", "L2.v1", "L2.o1"], "second": ["L2.q2", "L2.k2", "L2.v2"],
        "third": ["L2.o2", "L2.f1", "L2.f2", "L3.q", "L3.k", "L3.v"]}
R_AT, R_N = offsets(ROWS)
C_AT, C_N = offsets(COLS)
K_AT, K_N = offsets(CONSTS)
K_BF = K_AT["ident"][0]
K_F32 = K_AT["causal"][0]
W_CUTS = [0, W_AT["L0.fc1"][0], W_AT["L1.k"][0], W_AT["L1.o"][0], RESIDENT]


def narrow(n):
    return 0 <= n < N and STEPS[n][0] != L1


def wide(n):
    return 0 <= n < N and STEPS[n][0] == L1


NARROW = [n for n in range(N) if narrow(n)]
ORD = {n: j for j, n in enumerate(NARROW)}


TAILS = {
    L0S: [("turn0", 0), ("turn1", 1.5), ("sum", 2), ("norm", 3), ("live", 4.5), ("x_turn", 6)],
    L0C: [("turn0", 0), ("turn1", 1.5), ("sum", 2), ("norm", 3), ("x_turn", 4), ("ff1", 5.5), ("ff2", 6.5),
          ("norm2", 7.5), ("again", 8.5), ("norm3", 9.5), ("y_turn", 10)],
    L1: [("out", 0), ("x_turn", 2)],
    L2S: [("turn0", 0), ("turn1", 1.5), ("z_turn", 2), ("out", 3), ("norm", 4), ("x_turn", 5.5)],
    L2C: [("turn0", 0), ("turn1", 1.5), ("z_turn", 2), ("out", 3), ("norm", 4), ("x_turn", 5.5),
          ("ff1a", 6), ("ff1b", 6.5), ("ff2", 7.5), ("norm2", 8.5), ("y_turn", 9.5)],
    L3: [("turn0", 0), ("turn1", 1.5), ("sum", 2), ("norm", 3)],
}
BEFORE_WIDE = [("turn0", 0), ("turn1", 1), ("sum", 2), ("norm", 2.5), ("x_turn", 3), ("ff1", 3.5), ("ff2", 4),
               ("norm2", 4.5), ("again", 5), ("norm3", 5.5), ("y_turn", 6)]
NO_BANK = ("st", "pv", "s", "scale", "exp", "pt", "sum", "norm", "live", "norm2", "again", "norm3", "split", "kv_sum", "kv_norm",
           "masks")


def pieces_at(k, at):
    got = []
    for n, half, p in ((k, 1, 1), (k + 1, 0, 5)):
        if narrow(n) and p == at:
            got.append(("nm", n, half))
    for n, place in ((k - 2, at + UNITS), (k - 1, at)):
        if 0 <= n < N:
            tail = BEFORE_WIDE if STEPS[n] == (L0C, B - 1) else TAILS[STEPS[n][0]]
            got += [(name, n, 0) for name, p in tail if p == place]
    if narrow(k + 2):
        counted = STEPS[k + 2][0] in (L0S, L0C)
        places = (2, 3, 4, 4) if wide(k) else (2.5, 3.5, 4.5, 5.5)
        got += [(name, k + 2, 0) for name, p in zip(("qk", "split", "count", "v"), places)
                if p == at and (name != "count" or counted)]
    if wide(k + 2):
        places = (3.5, 4.5, 5.5) if narrow(k) else (6, 6.5, 7)
        got += [(name, k + 2, 0) for name, p in zip(("kv_sum", "kv_norm", "kv_turn"), places) if p == at]
    if wide(k + 1):
        got += [(f"v1_{i}", k + 1, 0) for i, p in enumerate((1, 3, 5, 7)) if p == at]
    if k == B - 1 and at in MASKS_AT:
        got.append(("masks", k, MASKS_AT.index(at)))
    return got


WIDE_AT = (512, 0)
MASKS_AT = (0.5, 5.5, 6.5, 7.5)


def make_plan():
    plan = []
    for k in range(-2, N + 2):
        for u in range(UNITS):
            i = UNITS * k + u
            one, two, three = (divmod(i + ahead, UNITS) for ahead in (1, 2, 3))
            if narrow(one[0]) and i + 1 >= 0:
                plan.append(("st", *one))
            if wide(k):
                plan += pieces_at(k, u)
            if wide(one[0]):
                plan.append(("scale", *one))
            if wide(two[0]):
                plan.append(("st", *two))
            if wide(three[0]):
                plan.append(("qk1", *three))
            if wide(two[0]):
                plan.append(("exp", *two))
            if narrow(k + 1):
                plan.append(("s", k + 1, u))
            if not wide(k):
                plan += pieces_at(k, u)
            if 0 <= k < N:
                plan.append(("pv", k, u))
            plan += pieces_at(k, u + 0.5)
            if wide(one[0]):
                plan.append(("pt", *one))
    return plan


PLAN = make_plan()


def score_banks(n, v):
    g, t = divmod(v, T)
    if STEPS[n][0] in CAUSAL and t == 0:
        return [(t, 4 * g, 4, P)]
    return [(t, 4 * g + 2 * x, 2, S) for x in range(2)]


def number(events):
    return {e: i for i, e in enumerate(events)}


WORK = number([e for e in PLAN if e[0] not in NO_BANK])
SBANK = number([(kind, n, v, x) for kind, n, v in PLAN if kind in ("s", "pt")
                for x in range(len(score_banks(n, v)) if kind == "s" else 2)])
SBANK_OF_WIDE = {i: e[0] == "pt" for e, i in SBANK.items()}


def after_sbank(i):
    return i if i and SBANK_OF_WIDE[i] != SBANK_OF_WIDE[i - 1] else i - 1


def after_use(kind, n, u=0):
    return WORK[(kind, n, u)] + 1


NORMS = number([e for e in PLAN if e[0] in ("sum", "again", "kv_sum", "ff2") or e[0] == "out" and narrow(e[1])])
ADDED = {("y_turn", L0C): (1, "L1.bo"), ("x_turn", L1): (0, "L2.bo1"), ("x_turn", L2S): (1, "L2.bo2"),
         ("x_turn", L2C): (0, "L2.bf2"), ("y_turn", L2C): (1, "L3.bv")}
ADDS = number([(kind, STEPS[n]) for kind, n, _ in PLAN if 0 <= n < N and (kind, STEPS[n][0]) in ADDED])
OUSE = number([(n, h) for n in range(N) for h in range(UNITS if wide(n) else 2)])


def attention_stack_program(nc, x, x_t, ctx, ctx_t, weights, rows, cols, consts, fixed_rows, src_mask, tgt_mask, tgt_mask_t,
                            key_mask, out):
    with ExitStack() as stack:
        def sb(name, shape, dt=F32):
            return stack.enter_context(nc.sbuf_tensor(name, shape, dt))

        def psum(name, shape):
            return stack.enter_context(nc.psum_tensor(name, shape, F32))

        def sem(name):
            return stack.enter_context(nc.semaphore(name))

        w_sb = sb("w_sb", [P, RESIDENT + P])
        row_sb = sb("row_sb", [P, R_N])
        col_sb = sb("col_sb", [P, C_N])
        const_sb = sb("const_sb", [P, K_F32])
        const_bf = sb("const_bf", [P, K_N - K_BF], BF16)
        q_stack = [sb(f"q_stack{i}", [P, H, S], BF16) for i in range(RING)]
        k_stack = [sb(f"k_stack{i}", [P, H, S], BF16) for i in range(RING)]
        qk_sb = [sb(f"qk_sb{i}", [P, 2, S]) for i in range(2)]
        parts = [sb(f"parts{i}", [P, 2, PARTS, S], BF16) for i in range(2)]
        rest = sb("rest", [P, 2, S])
        v_sb = [sb(f"v_sb{b}", [P, T, H, 32]) for b in range(B)]
        v1_sb = [sb(f"v1_sb{i}", [P, T, H * HS]) for i in range(2)]
        q1_sb = [sb(f"q1_sb{i}", [P, 2, S]) for i in range(2)]
        k1_sb = [sb(f"k1_sb{i}", [P, S]) for i in range(2)]
        ctx1_t = sb("ctx1_t", [P, UNITS, S])
        probs1_t = sb("probs1_t", [P, 3 * S])
        negmax1 = [sb(f"negmax1_{i}", [P, T, 2]) for i in range(2)]
        sums1 = [sb(f"sums1_{i}", [P, T, 2]) for i in range(2)]
        rec1 = sb("rec1", [P, T, 2])
        probs = [sb(f"probs{i}", [P, 4 * S]) for i in range(2)]
        negmax = [sb(f"negmax{i}", [P, T, H]) for i in range(2)]
        nm_rest = sb("nm_rest", [P, T, 8])
        nm_parts = [sb(f"nm_parts{i}", [P, T, PARTS, 8], BF16) for i in range(2)]
        nm_rows = [sb(f"nm_rows{i}", [PARTS * 8, S], BF16) for i in range(2)]
        q0_own = sb("q0_own", [P, H])
        nonzero = sb("nonzero", [H, S])
        length = sb("length", [H, 1])
        key_row = [sb(f"key_row{b}", [H, S], BF16) for b in range(B)]
        src_rows = sb("src_rows", [H, B, S], BF16)
        zero_row = sb("zero_row", [H, S], BF16)
        pad_row = sb("pad_row", [H, S], BF16)
        tgt_bias = sb("tgt_bias", [P, T, S], BF16)
        tgt_bias_t = sb("tgt_bias_t", [P, T, S], BF16)
        raw = [t[:, :, :].rearrange("p t n -> p (t n)") for t in v1_sb]
        int_tgt = raw[0][:, 0:4 * S].bitcast(I32).rearrange("p (w t k) -> p w t k", w=2, t=T)
        int_src = raw[0][0:H, 4 * S:8 * S].bitcast(I32).rearrange("p (b k) -> p b k", b=B)
        int_key = raw[1][:, 0:S].bitcast(I32)
        key_f = raw[1][:, S:2 * S]
        const_f = raw[1][:, 2 * S:2 * S + K_N - K_F32]
        key_min = sb("key_min", [P, 1])
        q_gate = sb("q_gate", [P, 1])
        q_gate_bias = sb("q_gate_bias", [P, 1])
        o_sb = sb("o_sb", [P, 4, S])
        res = [[sb(f"res{b}_{i}", [P, T, D]) for i in range(2)] for b in range(B)]
        ctx_sb = [sb(f"ctx_sb{b}", [P, T, D]) for b in range(B)]
        x_turned = [sb(f"x_turned{b}", [P, S]) for b in range(B)]
        ctx_turned = [sb(f"ctx_turned{b}", [P, S]) for b in range(B)]
        ctxm_turned = [sb(f"ctxm_turned{b}", [P, S]) for b in range(B)]
        kvn_turned = [sb(f"kvn_turned{b}", [P, S]) for b in range(B)]
        z_sb = sb("z_sb", [P, T, D])
        z_turned = sb("z_turned", [P, S])
        y_sb = sb("y_sb", [P, T, D])
        xh_sb = sb("xh_sb", [P, T, D])
        kvn_sb = sb("kvn_sb", [P, T, D])
        ctxm_sb = sb("ctxm_sb", [P, T, D])
        hidden = ctx1_t[:, 4:8, :]
        rec = sb("rec", [P, H])
        stats = sb("stats", [P, T, 6])
        mean_var = sb("mean_var", [P, T, 2])
        var_eps = sb("var_eps", [P, T])
        rstd = sb("rstd", [P, T])
        minus_half = sb("minus_half", [P, T])
        absmax = sb("absmax", [P, T])
        live0 = [sb(f"live0_{b}", [P, T]) for b in range(B)]
        live1 = [sb(f"live1_{b}", [P, T]) for b in range(B)]

        st_ps = [psum(f"st_ps{i}", [P, 1024]) for i in range(2)]
        s_ps = [psum(f"s_ps{i}", [P, 512]) for i in range(2)]
        o_ps = psum("o_ps", [P, 512])
        m_ps = psum("m_ps", [P, 512])
        m_bf = m_ps[:, :].bitcast(BF16)

        small_loaded = sem("small_loaded")
        rows_loaded = sem("rows_loaded")
        ctx_t_loaded = sem("ctx_t_loaded")
        x0_loaded = sem("x0_loaded")
        x_loaded = sem("x_loaded")
        tok_loaded = sem("tok_loaded")
        ctx_loaded = sem("ctx_loaded")
        bias_added = sem("bias_added")
        w_loaded = [sem(f"w_loaded{i}") for i in range(len(W_CUTS) - 1)]
        late_loaded = {x: sem(f"late_loaded_{x}") for x in LATE}
        masks_loaded = sem("masks_loaded")
        dve_step = sem("dve_step")
        pool_step = sem("pool_step")
        stack_blank = [sem(f"stack_blank{i}") for i in range(RING)]
        v_blank = sem("v_blank")
        blank = sem("blank")
        consts_ready = sem("consts_ready")
        masks_ready = sem("masks_ready")
        work_full = sem("work_full")
        work_free = sem("work_free")
        s_full = sem("s_full")
        s_free = sem("s_free")
        st_full = sem("st_full")
        exp_done = sem("exp_done")
        pv_done = sem("pv_done")
        o_free = sem("o_free")
        q0_ready = sem("q0_ready")
        parts_ready = sem("parts_ready")
        bounced = [sem(f"bounced{i}") for i in range(2)]
        stacked = [sem(f"stacked{i}") for i in range(RING)]
        key_row_ready = sem("key_row_ready")
        nm_parts_ready = sem("nm_parts_ready")
        nm_stacked = [sem(f"nm_stacked{i}") for i in range(2)]
        max1_ready = sem("max1_ready")
        scaled = sem("scaled")
        x_ready = sem("x_ready")
        kv_ready = sem("kv_ready")
        y_ready = sem("y_ready")
        var_ready = sem("var_ready")
        rstd_ready = sem("rstd_ready")
        result_ready = sem("result_ready")
        stored = sem("stored")

        bounce = [nc.dram_tensor(f"bounce{i}", [2, PARTS, P, S], BF16, kind="Internal").ap() for i in range(2)]

        def W(name, a=0, n=None):
            lo, hi = W_HOME[name]
            return w_sb[:, lo + a:(hi if n is None else lo + a + n)]

        def R(name, a=0, n=None):
            lo, hi = R_AT[name]
            return row_sb[:, lo + a:(hi if n is None else lo + a + n)]

        def R2(name):
            return R(name).unsqueeze(1).to_broadcast([P, T, D])

        def C(name, i=0):
            lo = C_AT[name][0] + i
            return col_sb[:, lo:lo + 1]

        def K(name):
            return const_sb[:, K_AT[name][0]:K_AT[name][1]]

        def KB(name):
            return const_bf[:, K_AT[name][0] - K_BF:K_AT[name][1] - K_BF]

        def by_head(ap, heads):
            return ap.unsqueeze(1).to_broadcast([ap.shape[0], heads, ap.shape[1]])

        def has(name):
            return {n: i + 1 for i, n in enumerate(n for n in NARROW if (name, n, 0) in WORK)}

        X_TURNS, Y_TURNS, Z_TURNS, COUNTS = has("x_turn"), has("y_turn"), has("z_turn"), has("count")

        def step_of(layer, b):
            return STEPS.index((layer, b))

        STARTS_IN = {L0S: 0, L0C: 1, L1: 1, L2S: 0, L2C: 1, L3: 1}

        def split(engine, then_, src, rest_, p):
            then_(engine.tensor_scalar(src, src, CAP, None, ALU.min))
            then_(engine.tensor_copy(p(0), src))
            then_(engine.tensor_tensor(rest_, src, p(0), ALU.subtract))
            then_(engine.tensor_copy(p(1), rest_))
            return engine.tensor_tensor(p(2), rest_, p(1), ALU.subtract)

        block = stack.enter_context(nc.Block())

        @block.sync
        def _(sp):
            sp.dma_start(x_turned[0][:, :], x_t[:, 0:S]).then_inc(x0_loaded, 16)
            sp.dma_start(w_sb[:, W_CUTS[0]:W_CUTS[1]], weights[:, W_CUTS[0]:W_CUTS[1]]).then_inc(w_loaded[0], 16)
            sp.dma_start(const_sb[:, :], consts[:, 0:K_F32]).then_inc(small_loaded, 16)
            sp.dma_start(const_f, consts[:, K_F32:K_N]).then_inc(small_loaded, 16)
            sp.dma_start(col_sb[:, :], cols).then_inc(small_loaded, 16)

            def blank_stack(i):
                for t in (q_stack[i], k_stack[i]):
                    rows_ = t[PARTS * PARTS * DK:ALL_ROWS, :, :].rearrange("p h q -> p (h q)").bitcast(F32)
                    sp.dma_start(rows_, fixed_rows).then_inc(stack_blank[i], 16)

            blank_stack(0)
            for b in range(1, B):
                sp.dma_start(x_turned[b][:, :], x_t[:, b * S:(b + 1) * S]).then_inc(x_loaded, 16)
            for b in range(B):
                sp.dma_start(res[b][0][:, :, :], x[b].rearrange("(t p) d -> p t d", p=P)).then_inc(tok_loaded, 16)

            def store_parts(n):
                j = ORD[n]
                sp.wait_ge(parts_ready, j + 1)
                if j >= 2:
                    sp.wait_ge(stacked[(j - 2) % RING], 16 * 5 * ((j - 2) // RING + 1))
                sp.dma_start(bounce[j % 2].rearrange("w a p q -> p (w a) q"),
                             parts[j % 2][:, :, :, :].rearrange("p w a q -> p (w a) q")).then_inc(bounced[j % 2], 16)

            def stack_step(n):
                j, layer, b = ORD[n], *STEPS[n]
                slot = j % RING
                if layer in (L0S, L0C):
                    sp.wait_ge(key_row_ready, COUNTS[n])
                    row = key_row[b][:, :]
                else:
                    if j == ORD[step_of(L2S, 0)]:
                        sp.wait_ge(masks_ready, len(MASKS_AT))
                    row = {L2S: zero_row[:, :], L2C: src_rows[:, b, :], L3: pad_row[:, :]}[layer]
                sp.wait_ge(stack_blank[slot], 32)
                if j >= RING:
                    sp.wait_ge(pv_done, UNITS * NARROW[j - RING] + UNITS)
                sp.wait_ge(bounced[j % 2], 16 * (j // 2 + 1))
                src = bounce[j % 2]
                for a in range(PARTS):
                    part = src[0, a].rearrange("(d h) q -> d (h q)", h=H)
                    sp.dma_start(q_stack[slot][24 * a:24 * a + 24, :, :].rearrange("p h q -> p (h q)"),
                                 part.unsqueeze(0).to_broadcast([PARTS, DK, H * S])).then_inc(stacked[slot], 16)
                every = src[1].rearrange("a (d h) q -> (a d) (h q)", h=H)
                sp.dma_start(k_stack[slot][0:72, :, :].rearrange("p h q -> p (h q)"),
                             every.unsqueeze(0).to_broadcast([PARTS, PARTS * DK, H * S])).then_inc(stacked[slot], 16)
                sp.dma_start(k_stack[slot][MASK_ROW:MASK_ROW + 1, :, :], row).then_inc(stacked[slot], 16)

            blank_stack(1)
            blank_stack(2)
            def late_weights(x):
                for name in LATE[x]:
                    lo, hi = W_AT[name]
                    sp.dma_start(W(name), weights[:, lo:hi]).then_inc(late_loaded[x], 16)

            for kind, n, half in PLAN:
                if kind == "split":
                    store_parts(n)
                elif kind == "v":
                    stack_step(n)
                    if n == B:
                        sp.wait_ge(work_full, WORK[("v", B - 1, 0)] + 1)
                        late_weights("first")
                    elif n == step_of(L2S, 0):
                        sp.wait_ge(work_full, WORK[("v", 2 * B - 1, 0)] + 1)
                        late_weights("second")
                    elif n == step_of(L2C, 0):
                        sp.wait_ge(work_full, WORK[("qk1", step_of(L1, B - 1), UNITS - 1)] + 1)
                        late_weights("third")
                elif kind == "nm":
                    j = ORD[n]
                    sp.wait_ge(work_free, after_use(kind, n, half))
                    sp.dma_start(q_stack[j % RING][NEGMAX_ROW:NEGMAX_ROW + PARTS, 8 * half:8 * half + 8, :],
                                 nm_rows[half][:, :]).then_inc(nm_stacked[half], 16)
            for b in range(B):
                sp.wait_ge(result_ready, b + 1)
                sp.dma_start(out[b].rearrange("(t p) d -> p t d", p=P), res[b][0][:, :, :]).then_inc(stored, 16)
            sp.wait_ge(stored, 16 * B)

        @block.gpsimd
        def _(pool):
            steps = [0]

            def then(ins):
                steps[0] += 1
                ins.then_inc(pool_step, 1)
                pool.wait_ge(pool_step, steps[0])

            for b, t in enumerate(v_sb):
                then(nc.gpsimd.memset(t[:, :, :, :], 0.0))
                nc.gpsimd.memset(t[:, :, :, DK:DK + 1], 1.0).then_inc(v_blank, 1)
            then(nc.gpsimd.memset(zero_row[:, :], 0.0))
            for t in q1_sb:
                then(nc.gpsimd.memset(t[:, :, :], 0.0))
            nc.gpsimd.memset(minus_half[:, :], -0.5).then_inc(blank, 1)
            pool.wait_ge(blank, 1)
            for b in range(B):
                pool.dma_start(ctx_sb[b][:, :, :], ctx[b].rearrange("(t p) d -> p t d", p=P)).then_inc(ctx_loaded, 16)
            pool.wait_ge(stacked[0], 16 * 5)
            pool.dma_start(row_sb[:, :], rows.to_broadcast([P, R_N])).then_inc(rows_loaded, 16)
            for i in range(1, len(W_CUTS) - 1):
                a, z = W_CUTS[i], W_CUTS[i + 1]
                pool.dma_start(w_sb[:, a:z], weights[:, a:z]).then_inc(w_loaded[i], 16)

            def other_loads():
                pool.dma_start(int_src[:, :, :], src_mask.to_broadcast([H, B * S])).then_inc(masks_loaded, 16)
                for i, m in enumerate((tgt_mask, tgt_mask_t)):
                    pool.dma_start(int_tgt[:, i, :, :], m.rearrange("(t p) k -> p t k", p=P)).then_inc(masks_loaded, 16)
                for d in range(DK):
                    pool.dma_start(int_key[H * d:H * d + H, :],
                                   key_mask.unsqueeze(1).to_broadcast([B, H // B, S])).then_inc(masks_loaded, 16)
                for b in range(B):
                    pool.dma_start(ctx_turned[b][:, :], ctx_t[:, b * S:(b + 1) * S]).then_inc(ctx_t_loaded, 16)

            for kind, n, u in PLAN:
                layer, b = STEPS[n] if 0 <= n < N else (None, None)
                if kind == "s" and u % 4 == 3:
                    j, half = ORD[n], u // 4
                    pool.wait_ge(s_free, SBANK[("s", n, u, len(score_banks(n, u)) - 1)] + 1)
                    if j:
                        pool.wait_ge(work_full, after_use("nm", NARROW[j - 1], half))
                    p = nm_parts[half]
                    split(nc.gpsimd, then, negmax[j % 2][:, :, 8 * half:8 * half + 8], nm_rest[:, :, :],
                          lambda a: p[:, :, a, :]).then_inc(nm_parts_ready, 1)
                if (kind, n, u) in NORMS:
                    pool.wait_ge(var_ready, NORMS[(kind, n, u)] + 1)
                    then(nc.gpsimd.tensor_scalar(var_eps[:, :], mean_var[:, :, 1], EPS, None, ALU.add))
                    nc.gpsimd.tensor_tensor(rstd[:, :], var_eps[:, :], minus_half[:, :], ALU.pow).then_inc(rstd_ready, 1)
                if (kind, layer) in ADDED:
                    buffer, bias = ADDED[(kind, layer)]
                    pool.wait_ge(work_full, after_use(kind, n))
                    nc.gpsimd.tensor_tensor(res[b][buffer][:, :, :], res[b][buffer][:, :, :], R2(bias),
                                            ALU.add).then_inc(bias_added, 1)
                if (kind, n) == ("s", 1) and u == 0:
                    other_loads()

        @block.tensor
        def _(pe):
            def mm(o, lhs, rhs, start):
                return nc.tensor.matmul(o, lhs, rhs, start=start, stop=True, skip_group_check=True)

            def turn(o, i, bf=False):
                ident = KB("ident") if bf else K("ident")
                return nc.tensor.transpose(o, i, ident)

            def bias(o, rhs):
                return mm(o, KB("ident"), rhs, False)

            def bank_heads(ps, heads, width, lo, hi):
                return ps[:, 0:heads * width].rearrange("p (h q) -> p h q", h=heads)[:, :, lo:hi]

            def scores(n, v):
                layer, b = STEPS[n]
                j = ORD[n]
                q, k = q_stack[j % RING], k_stack[j % RING]
                if v == 0:
                    pe.wait_ge(stacked[j % RING], 16 * 5 * (j // RING + 1))
                    pe.wait_ge(stack_blank[j % RING], 32)
                    if n == step_of(L2S, 0):
                        pe.wait_ge(masks_ready, len(MASKS_AT))
                for x, (t, h0, heads, keys) in enumerate(score_banks(n, v)):
                    i = SBANK[("s", n, v, x)]
                    ps = s_ps[i % 2]
                    if i >= 2:
                        pe.wait_ge(s_free, after_sbank(i))
                    for e in range(heads):
                        last = mm(ps[:, e * keys:(e + 1) * keys], q[0:SCORE_ROWS, h0 + e, t * P:(t + 1) * P],
                                  k[0:SCORE_ROWS, h0 + e, 0:keys], e == 0)
                    if layer == L0S:
                        last = bias(bank_heads(ps, heads, keys, t * P, (t + 1) * P), by_head(KB("causal"), heads))
                    elif layer == L2S:
                        last = bias(bank_heads(ps, heads, keys, 0, keys), by_head(tgt_bias[:, t, :], heads))
                    last.then_inc(s_full, 1)

            def scores_t(n, u):
                layer, b = STEPS[n]
                i = UNITS * n + u
                if i >= 2:
                    pe.wait_ge(exp_done, i - 1)
                ps = st_ps[i % 2]
                if wide(n):
                    pe.wait_ge(work_free, after_use("qk1", n, u))
                    q, k = q1_sb[u % 2], k1_sb[u % 2]
                    for t in (1, 0):
                        lo, keys = WIDE_AT[t], (t + 1) * P
                        for e in range(2):
                            mm(ps[:, lo + e * keys:lo + (e + 1) * keys], q[:, e, t * P:(t + 1) * P], k[:, 0:keys], e == 0)
                        last = bias(bank_heads(ps[:, lo:lo + 2 * keys], 2, keys, t * P, (t + 1) * P),
                                    by_head(KB("causal"), 2))
                    last.then_inc(st_full, 1)
                    return
                g, t = divmod(u, T)
                j = ORD[n]
                q, k = q_stack[j % RING], k_stack[j % RING]
                if u % 4 == 0:
                    pe.wait_ge(nm_stacked[u // 4], 16 * (j + 1))
                lo = t * P if layer in CAUSAL else 0
                wq = S - lo
                for e in range(4):
                    last = mm(ps[:, e * wq:(e + 1) * wq], k[0:ALL_ROWS, 4 * g + e, t * P:(t + 1) * P],
                              q[0:ALL_ROWS, 4 * g + e, lo:S], (e * wq) % 512 == 0)
                if layer == L0S and t == 0:
                    for x in range(2):
                        last = bias(bank_heads(ps[:, 512 * x:512 * x + 512], 2, S, 0, P), by_head(KB("causalT"), 2))
                elif layer == L0S:
                    last = bias(bank_heads(ps, 4, P, 0, P), by_head(KB("causalT"), 4))
                elif layer == L2S:
                    for x in range(2):
                        last = bias(bank_heads(ps[:, 512 * x:512 * x + 512], 2, S, 0, S),
                                    by_head(tgt_bias_t[:, t, :], 2))
                last.then_inc(st_full, 1)

            def times_v(n, u):
                layer, b = STEPS[n]
                i = UNITS * n + u
                p = probs[i % 2]
                if wide(n):
                    if u == 0:
                        pe.wait_ge(work_free, after_use("v1_3", n))
                    pe.wait_ge(s_free, SBANK[("pt", n, u, 1)] + 1)
                    pe.wait_ge(o_free, OUSE[(n, u)])
                    for t in range(T):
                        wq = S - t * P
                        for e in range(2):
                            h = 2 * u + e
                            last = mm(o_ps[HS * e:HS * e + HS, t * P:S], v1_sb[b % 2][:, t, h * HS:(h + 1) * HS],
                                      probs1_t[:, 512 * t + e * wq:512 * t + (e + 1) * wq], t == 0)
                    last.then_inc(pv_done, 1)
                    return
                pe.wait_ge(exp_done, i + 1)
                g, t = divmod(u, T)
                if u == 0:
                    pe.wait_ge(work_free, after_use("v", n))
                    pe.wait_ge(v_blank, b + 1)
                if u % 4 == 0 and OUSE[(n, u // 4)]:
                    pe.wait_ge(o_free, OUSE[(n, u // 4)])
                lo = t * P if layer in CAUSAL else 0
                wq = S - lo
                for e in range(4):
                    last = mm(o_ps[32 * e:32 * e + 32, (g % 2) * S + lo:(g % 2) * S + S],
                              v_sb[b][:, t, 4 * g + e, :], p[:, e * wq:(e + 1) * wq], t == 0)
                last.then_inc(pv_done, 1)

            def qk_wide(n, u):
                b = STEPS[n][1]
                if u == 0:
                    pe.wait_ge(w_loaded[1], 16)
                    pe.wait_ge(w_loaded[2], 16)
                mm(m_ps[:, 0:S], W("L1.q", u * P, P), x_turned[b][:, :], True)
                return mm(m_ps[:, S:2 * S], W("L1.k", u * P, P), kvn_turned[b][:, :], False)

            def turn_probs(n, u):
                i = UNITS * n + u
                pe.wait_ge(scaled, i - UNITS * step_of(L1, 0) + 1)
                for x in range(T):
                    bank = SBANK[("pt", n, u, x)]
                    ps, wq = s_ps[bank % 2], S - x * P
                    pe.wait_ge(s_free, after_sbank(bank))
                    for e in range(2):
                        for t in range(x, T):
                            p = probs[i % 2][:, WIDE_AT[t] + e * (t + 1) * P + x * P:][:, 0:P]
                            last = turn(ps[:, e * wq + (t - x) * P:e * wq + (t - x + 1) * P], p)
                    last.then_inc(s_full, 1)

            def piece(kind, n, u):
                layer, b = STEPS[n]
                if kind == "qk":
                    if layer == L0S:
                        pe.wait_ge(*((x0_loaded, 16) if b == 0 else (x_loaded, 16 * (B - 1))))
                        pe.wait_ge(w_loaded[0], 16)
                        mm(m_ps[:, 0:S], W("L0.q1"), x_turned[b][:, :], True)
                        return mm(m_ps[:, S:], W("L0.k1"), x_turned[b][:, :], False)
                    if layer == L0C:
                        mm(m_ps[:, 0:S], W("L0.q2"), x_turned[b][:, :], True)
                        return mm(m_ps[:, S:], W("L0.k2"), ctxm_turned[b][:, :], False)
                    if layer == L2S:
                        pe.wait_ge(late_loaded["first"], 16 * len(LATE["first"]))
                        mm(m_ps[:, 0:S], W("L2.q1"), x_turned[b][:, :], True)
                        return mm(m_ps[:, S:], W("L2.k1"), x_turned[b][:, :], False)
                    if layer == L2C:
                        pe.wait_ge(late_loaded["second"], 16 * len(LATE["second"]))
                        pe.wait_ge(ctx_t_loaded, 16 * B)
                        mm(m_ps[:, 0:S], W("L2.q2"), x_turned[b][:, :], True)
                        return mm(m_ps[:, S:], W("L2.k2"), ctx_turned[b][:, :], False)
                    mm(m_ps[:, 0:S], W("L3.q"), x_turned[b][:, :], True)
                    return mm(m_ps[:, S:], W("L3.k"), ctx_turned[b][:, :], False)
                if kind == "v":
                    src = {L0S: x_turned, L0C: ctxm_turned, L2S: x_turned, L2C: ctx_turned, L3: ctx_turned}[layer][b]
                    w = {L0S: "L0.v1", L0C: "L0.v2", L2S: "L2.v1", L2C: "L2.v2", L3: "L3.v"}[layer]
                    for t in range(T):
                        last = mm(m_ps[:, t * P:(t + 1) * P], src[:, t * P:(t + 1) * P], W(w), t == 0)
                    return last
                if kind == "count":
                    pe.wait_ge(q0_ready, COUNTS[n])
                    return mm(m_ps[0:H, 0:S], q0_own[:, :], qk_sb[ORD[n] % 2][:, 1, :], True)
                if kind == "nm":
                    pe.wait_ge(nm_parts_ready, 2 * ORD[n] + u + 1)
                    for t in range(T):
                        last = turn(m_bf[0:PARTS * 8, t * P:(t + 1) * P],
                                    nm_parts[u][:, t, :, :].rearrange("p a h -> p (a h)"), bf=True)
                    return last
                if kind in ("turn0", "turn1"):
                    t = int(kind[-1])
                    if t == 0:
                        pe.wait_ge(o_free, OUSE[(n, 1)] + 1)
                    for g in range(4):
                        last = turn(m_ps[:, g * P:(g + 1) * P], o_sb[:, g, t * P:(t + 1) * P])
                    return last
                if kind == "z_turn":
                    for t in range(T):
                        last = turn(m_ps[:, t * P:(t + 1) * P], z_sb[:, t, :])
                    return last
                if kind == "out":
                    if layer == L1:
                        pe.wait_ge(w_loaded[3], 16)
                        pe.wait_ge(o_free, OUSE[(n, UNITS - 1)] + 1)
                        for t in range(T):
                            for p in range(UNITS):
                                last = mm(m_ps[:, t * P:(t + 1) * P], ctx1_t[:, p, t * P:(t + 1) * P],
                                          W("L1.o", p * P, P), t == 0 and p == 0)
                        return last
                    if layer == L2C:
                        pe.wait_ge(late_loaded["third"], 16 * len(LATE["third"]))
                    for t in range(T):
                        last = mm(m_ps[:, t * P:(t + 1) * P], z_turned[:, t * P:(t + 1) * P],
                                  W("L2.o1" if layer == L2S else "L2.o2"), t == 0)
                    return last
                if kind == "x_turn":
                    if layer != L1:
                        pe.wait_ge(x_ready, X_TURNS[n])
                    r = res[b][x_buffer(layer)]
                    for t in range(T):
                        last = turn(m_ps[:, t * P:(t + 1) * P], r[:, t, :])
                    if layer == L0S:
                        for t in range(T):
                            last = turn(m_ps[:, S + t * P:S + (t + 1) * P], ctxm_sb[:, t, :])
                    return last
                if kind == "kv_turn":
                    pe.wait_ge(kv_ready, b + 1)
                    for t in range(T):
                        last = turn(m_ps[:, t * P:(t + 1) * P], kvn_sb[:, t, :])
                    return last
                if kind == "ff1":
                    pe.wait_ge(w_loaded[1], 16)
                    return mm(m_ps[:, 0:S], W("L0.fc1"), x_turned[b][:, :], True)
                if kind in ("ff1a", "ff1b"):
                    for x in range(2):
                        c = (2 if kind == "ff1b" else 0) + x
                        last = mm(m_ps[:, x * S:(x + 1) * S], W("L2.f1", c * P, P), x_turned[b][:, :], x == 0)
                    return last
                if kind == "ff2":
                    name, cs = ("L0.fc2", 1) if layer == L0C else ("L2.f2", 4)
                    for t in range(T):
                        for c in range(cs):
                            last = mm(m_ps[:, t * P:(t + 1) * P], hidden[:, c, t * P:(t + 1) * P],
                                      W(name, c * P, P), t == 0 and c == 0)
                    return last
                if kind == "y_turn":
                    pe.wait_ge(y_ready, Y_TURNS[n])
                    r = kvn_sb if layer == L0C else res[b][1]
                    for t in range(T):
                        last = turn(m_ps[:, t * P:(t + 1) * P], r[:, t, :])
                    return last
                if kind.startswith("v1_"):
                    t, half = divmod(int(kind[-1]), 2)
                    if kind == "v1_0":
                        pe.wait_ge(w_loaded[2], 16)
                    return mm(m_ps[:, :], kvn_turned[b][:, t * P:(t + 1) * P], W("L1.v", half * 512, 512), True)
                raise ValueError(kind)

            pe.wait_ge(small_loaded, 48)
            pe.wait_ge(consts_ready, 2)
            for kind, n, u in PLAN:
                if kind in NO_BANK and kind not in ("st", "pv", "s", "pt"):
                    continue
                if kind == "st":
                    scores_t(n, u)
                elif kind == "pv":
                    times_v(n, u)
                elif kind == "s":
                    scores(n, u)
                elif kind == "pt":
                    turn_probs(n, u)
                else:
                    use = WORK[(kind, n, u)]
                    if use:
                        pe.wait_ge(work_free, use)
                    made = qk_wide(n, u) if kind == "qk1" else piece(kind, n, u)
                    made.then_inc(work_full, 1)

        @block.scalar
        def _(act):
            def full(kind, n, u=0):
                act.wait_ge(work_full, WORK[(kind, n, u)] + 1)

            def biased(o, i, c):
                return nc.scalar.activation(o, i, ACT.Identity, bias=c, scale=1.0)

            act.wait_ge(small_loaded, 48)
            for kind, n, u in PLAN:
                layer, b = STEPS[n]
                i = UNITS * n + u
                if kind == "st" and narrow(n):
                    if i >= 2:
                        act.wait_ge(pv_done, i - 1)
                    act.wait_ge(st_full, i + 1)
                    size = 512 if layer in CAUSAL and u % T else 1024
                    nc.scalar.activation(probs[i % 2][:, 0:size], st_ps[i % 2][:, 0:size], ACT.Exp,
                                         scale=DK ** -0.5).then_inc(exp_done, 1)
                elif kind == "exp":
                    act.wait_ge(pv_done, i - 1)
                    act.wait_ge(max1_ready, i - UNITS * step_of(L1, 0) + 1)
                    for t in (1, 0):
                        for e in range(2):
                            at = slice(WIDE_AT[t] + e * (t + 1) * P, WIDE_AT[t] + (e + 1) * (t + 1) * P)
                            ins = nc.scalar.activation(probs[i % 2][:, at], st_ps[i % 2][:, at], ACT.Exp,
                                                       bias=negmax1[i % 2][:, t, e:e + 1], scale=1.0,
                                                       accum_out=sums1[i % 2][:, t, e:e + 1])
                    ins.then_inc(exp_done, 1)
                elif kind == "pt":
                    act.wait_ge(pv_done, i)
                    for x in range(T):
                        bank = SBANK[("pt", n, u, x)]
                        act.wait_ge(s_full, bank + 1)
                        size = 2 * (S - x * P)
                        nc.scalar.activation(probs1_t[:, 512 * x:512 * x + size], s_ps[bank % 2][:, 0:size],
                                             ACT.Copy).then_inc(s_free, 1)
                elif kind == "pv" and narrow(n) and u % 4 == 3:
                    half = u // 4
                    act.wait_ge(pv_done, UNITS * n + u + 1)
                    j = ORD[n]
                    if j and half == 0:
                        act.wait_ge(work_full, WORK[("turn1", NARROW[j - 1], 0)] + 1)
                    nc.scalar.activation(o_sb[:, 2 * half:2 * half + 2, :],
                                         o_ps[:, :].rearrange("p (g q) -> p g q", g=2), ACT.Copy).then_inc(o_free, 1)
                elif kind == "qk":
                    full(kind, n)
                    j = ORD[n]
                    q, first = qk_sb[j % 2], parts[j % 2][:, :, 0, :]
                    if j >= 2:
                        act.wait_ge(parts_ready, j - 1)
                        act.wait_ge(bounced[j % 2], 16 * (j // 2))
                        if ("count", NARROW[j - 2], 0) in WORK:
                            act.wait_ge(work_full, WORK[("count", NARROW[j - 2], 0)] + 1)
                    if layer in (L0S, L0C):
                        both = m_ps[:, :].rearrange("p (w q) -> p w q", w=2)
                        nc.scalar.activation(first, both, ACT.Copy)
                        nc.scalar.activation(q[:, :, :], both, ACT.Copy).then_inc(work_free, 1)
                    else:
                        bq, bk = {L2S: ("L2.bq1", "L2.bk1"), L2C: ("L2.bq2", "L2.bk2"), L3: ("L3.bq", "L3.bk")}[layer]
                        if layer == L3 and b == 0:
                            act.wait_ge(masks_ready, len(MASKS_AT))
                        for o in (first, q):
                            if layer == L3:
                                nc.scalar.activation(o[:, 0, :], m_ps[:, 0:S], ACT.Identity,
                                                     bias=q_gate_bias[:, :], scale=q_gate[:, :])
                            else:
                                biased(o[:, 0, :], m_ps[:, 0:S], C(bq))
                            ins = biased(o[:, 1, :], m_ps[:, S:2 * S], C(bk))
                        ins.then_inc(work_free, 1)
                elif kind == "nm":
                    full(kind, n, u)
                    if ORD[n]:
                        act.wait_ge(nm_stacked[u], 16 * ORD[n])
                    nc.scalar.activation(nm_rows[u][:, :], m_bf[0:PARTS * 8, 0:S], ACT.Copy).then_inc(work_free, 1)
                elif kind == "qk1":
                    pair = UNITS * b + u
                    full(kind, n, u)
                    if pair == 0:
                        act.wait_ge(blank, 1)
                        act.wait_ge(consts_ready, 3)
                    if pair >= 2:
                        act.wait_ge(st_full, i - 1)
                    q = q1_sb[u % 2]
                    for e in range(2):
                        half = slice(HS * e, HS * e + HS)
                        lo = C_AT["L1.bq"][0] + u
                        nc.scalar.activation(q[half, e, :], m_ps[half, 0:S], ACT.Identity,
                                             bias=col_sb[half, lo:lo + 1], scale=HS ** -0.5)
                    biased(k1_sb[u % 2][:, :], m_ps[:, S:2 * S], C("L1.bk", u)).then_inc(work_free, 1)
                elif kind == "v":
                    full(kind, n)
                    if n >= B:
                        act.wait_ge(pv_done, UNITS * (n - B) + UNITS)
                    else:
                        act.wait_ge(v_blank, b + 1)
                    for t in range(T):
                        ins = nc.scalar.activation(v_sb[b][:, t, :, 0:DK],
                                                   m_ps[:, t * P:(t + 1) * P].rearrange("p (h d) -> p h d", d=DK), ACT.Copy)
                    ins.then_inc(work_free, 1)
                elif kind == "z_turn":
                    full(kind, n)
                    biased(z_turned[:, :], m_ps[:, 0:S], C("L2.bv1" if layer == L2S else "L2.bv2")).then_inc(work_free, 1)
                elif kind == "x_turn":
                    full(kind, n)
                    if layer == L0S:
                        nc.scalar.activation(ctxm_turned[b][:, :], m_ps[:, S:2 * S], ACT.Copy)
                    nc.scalar.activation(x_turned[b][:, :], m_ps[:, 0:S], ACT.Copy).then_inc(work_free, 1)
                elif kind == "kv_turn":
                    full(kind, n)
                    nc.scalar.activation(kvn_turned[b][:, :], m_ps[:, 0:S], ACT.Copy).then_inc(work_free, 1)
                elif kind == "y_turn":
                    full(kind, n)
                    nc.scalar.activation(x_turned[b][:, :], m_ps[:, 0:S], ACT.Copy).then_inc(work_free, 1)
                elif kind in ("ff1", "ff1a", "ff1b"):
                    full(kind, n)
                    cs = {"ff1": [0], "ff1a": [0, 1], "ff1b": [2, 3]}[kind]
                    for x, c in enumerate(cs):
                        ins = nc.scalar.activation(hidden[:, c, :], m_ps[:, x * S:(x + 1) * S], ACT.Relu,
                                                   bias=C("L0.fc1b") if layer == L0C else C("L2.bf1", c), scale=1.0)
                    ins.then_inc(work_free, 1)

        @block.vector
        def _(dve):
            steps = [0]

            def then(ins):
                steps[0] += 1
                ins.then_inc(dve_step, 1)
                dve.wait_ge(dve_step, steps[0])

            def full(kind, n, u=0):
                dve.wait_ge(work_full, WORK[(kind, n, u)] + 1)

            v = nc.vector
            dve.wait_ge(small_loaded, 48)
            v.tensor_copy(const_bf[:, 0:P], K("ident")).then_inc(consts_ready, 1)
            v.tensor_copy(const_bf[:, P:K_N - K_BF], const_f).then_inc(consts_ready, 1)
            lo, hi = C_AT["L1.bq"]
            v.tensor_scalar(col_sb[:, lo:hi], col_sb[:, lo:hi], HS ** -0.5, None, ALU.mult).then_inc(consts_ready, 1)
            def masks(part):
                if part == 0:
                    dve.wait_ge(masks_loaded, 16 * (3 + DK))
                    v.tensor_scalar(src_rows[:, :, :], int_src[:, :, :], 0.0, NEG, ALU.is_equal,
                                    ALU.mult).then_inc(masks_ready, 1)
                elif part <= 2:
                    v.tensor_scalar((tgt_bias, tgt_bias_t)[part - 1][:, :, :], int_tgt[:, part - 1, :, :], 0.0, NEG,
                                    ALU.is_equal, ALU.mult).then_inc(masks_ready, 1)
                else:
                    then(v.tensor_copy(key_f[:, :], int_key[:, :]))
                    then(v.tensor_reduce(key_min[:, :], key_f[:, :], AX.X, ALU.min))
                    then(v.tensor_scalar(q_gate[:, :], key_min[:, :], 0.0, None, ALU.is_equal))
                    then(v.tensor_tensor(q_gate_bias[:, :], q_gate[:, :], C("L3.bq"), ALU.mult))
                    v.tensor_scalar(pad_row[:, :], key_f[0:H, :], key_min[0:H, :], PAD * DK ** 0.5, ALU.subtract,
                                    ALU.mult).then_inc(masks_ready, 1)

            def moments(y):
                for t in range(T):
                    ins = v.bn_stats(stats[:, t, :], y[:, t, :])
                then(ins)
                for t in range(T):
                    ins = v.bn_aggr(mean_var[:, t, :], stats[:, t, :])
                ins.then_inc(var_ready, 1)

            def normalise(o, y, g, beta, summed, sem_of=None):
                dve.wait_ge(var_ready, NORMS[summed] + 1)
                for t in range(T):
                    ins = v.scalar_tensor_tensor(out=xh_sb[:, t, :], in0=y[:, t, :], scalar=mean_var[:, t, 0:1],
                                                 in1=R(g), op0=ALU.subtract, op1=ALU.mult)
                then(ins)
                dve.wait_ge(rstd_ready, NORMS[summed] + 1)
                for t in range(T):
                    ins = v.scalar_tensor_tensor(out=o[:, t, :], in0=xh_sb[:, t, :], scalar=rstd[:, t:t + 1],
                                                 in1=R(beta), op0=ALU.mult, op1=ALU.add)
                if sem_of is None:
                    then(ins)
                else:
                    ins.then_inc(sem_of, 1)

            def row_mask(live, r):
                then(v.tensor_reduce(absmax[:, :], r[:, :, :], AX.X, ALU.max, apply_absolute_value=True))
                then(v.tensor_scalar(live[:, :], absmax[:, :], 0.0, None, ALU.not_equal))

            for kind, n, u in PLAN:
                layer, b = STEPS[n]
                old = res[b][STARTS_IN[layer]]
                if kind == "s":
                    j = ORD[n]
                    if j >= 2 and u % 4 == 0:
                        dve.wait_ge(nm_parts_ready, 2 * (j - 2) + u // 4 + 1)
                    for x, (t, h0, heads, keys) in enumerate(score_banks(n, u)):
                        i = SBANK[("s", n, u, x)]
                        dve.wait_ge(s_full, i + 1)
                        v.tensor_reduce(negmax[j % 2][:, t, h0:h0 + heads],
                                        s_ps[i % 2][:, 0:heads * keys].rearrange("p (h k) -> p h k", h=heads),
                                        AX.X, ALU.max, negate=True).then_inc(s_free, 1)
                elif kind == "st" and wide(n):
                    i = UNITS * n + u
                    dve.wait_ge(st_full, i + 1)
                    for t in (1, 0):
                        lo, keys = WIDE_AT[t], (t + 1) * P
                        ins = v.tensor_reduce(negmax1[i % 2][:, t, :],
                                              st_ps[i % 2][:, lo:lo + 2 * keys].rearrange("p (h k) -> p h k", h=2),
                                              AX.X, ALU.max, negate=True)
                    ins.then_inc(max1_ready, 1)
                elif kind == "scale":
                    i = UNITS * n + u
                    dve.wait_ge(exp_done, i + 1)
                    then(v.reciprocal(rec1[:, :, :], sums1[i % 2][:, :, :]))
                    for t in (1, 0):
                        lo, keys = WIDE_AT[t], (t + 1) * P
                        p = probs[i % 2][:, lo:lo + 2 * keys].rearrange("p (h k) -> p h k", h=2)
                        ins = v.tensor_tensor(p, p, rec1[:, t, :].unsqueeze(2).to_broadcast([P, 2, keys]), ALU.mult)
                    ins.then_inc(scaled, 1)
                elif kind == "pv" and wide(n):
                    dve.wait_ge(pv_done, UNITS * n + u + 1)
                    if u == 0 and b:
                        dve.wait_ge(work_full, WORK[("out", n - 1, 0)] + 1)
                    v.tensor_copy(ctx1_t[:, u, :], o_ps[:, 0:S]).then_inc(o_free, 1)
                elif kind == "split":
                    j = ORD[n]
                    q, p = qk_sb[j % 2], parts[j % 2]
                    dve.wait_ge(work_free, after_use("qk", n))
                    if layer in (L0S, L0C):
                        if COUNTS[n] > 1:
                            dve.wait_ge(work_full, WORK[("count", n - 1, 0)] + 1)
                        v.tensor_scalar(q0_own[:, :], K("own_head"), q[:, 0, 0:1], None, ALU.mult).then_inc(q0_ready, 1)
                    then(v.tensor_tensor(rest[:, :, :], q[:, :, :], p[:, :, 0, :], ALU.subtract))
                    then(v.tensor_copy(p[:, :, 1, :], rest[:, :, :]))
                    v.tensor_tensor(p[:, :, 2, :], rest[:, :, :], p[:, :, 1, :], ALU.subtract).then_inc(parts_ready, 1)
                elif kind == "count":
                    full(kind, n)
                    if layer == L0C:
                        j = ORD[step_of(L0S, b)]
                        dve.wait_ge(stacked[j % RING], 16 * 5 * (j // RING + 1))
                    v.tensor_scalar(nonzero[:, :], m_ps[0:H, 0:S], 0.0, None, ALU.not_equal).then_inc(work_free, 1)
                    dve.wait_ge(work_free, after_use(kind, n))
                    then(v.tensor_reduce(length[:, :], nonzero[:, :], AX.X, ALU.add))
                    lo, hi = K_AT["key"]
                    v.tensor_scalar(key_row[b][:, :], const_sb[0:H, lo:hi], length[:, :], NEG, ALU.is_ge,
                                    ALU.mult).then_inc(key_row_ready, 1)
                    if layer == L0S:
                        if b == 0:
                            dve.wait_ge(tok_loaded, 16 * B)
                        row_mask(live0[b], res[b][0])
                elif kind.startswith("v1_"):
                    t, half = divmod(int(kind[-1]), 2)
                    full(kind, n)
                    if kind == "v1_0" and b >= 2:
                        dve.wait_ge(pv_done, UNITS * (n - 2) + UNITS)
                    v.tensor_tensor(v1_sb[b % 2][:, t, half * 512:half * 512 + 512], m_ps[:, :],
                                    R("L1.bv", half * 512, 512), ALU.add).then_inc(work_free, 1)
                elif kind in ("turn0", "turn1"):
                    t = int(kind[-1])
                    full(kind, n)
                    heads = m_ps[:, :].rearrange("p (h w) -> p h w", w=32)
                    then(v.reciprocal(rec[:, :], heads[:, :, DK]))
                    if t == 0 and layer in (L2S, L2C) and Z_TURNS[n] > 1:
                        last = [m for m in Z_TURNS if m < n][-1]
                        dve.wait_ge(work_full, WORK[("z_turn", last, 0)] + 1)
                    v.tensor_tensor(z_sb[:, t, :].rearrange("p (h d) -> p h d", d=DK), heads[:, :, 0:DK],
                                    rec[:, :].unsqueeze(2).to_broadcast([P, H, DK]), ALU.mult).then_inc(work_free, 1)
                elif kind == "sum":
                    dve.wait_ge(work_free, after_use("turn1", n))
                    if layer == L3:
                        dve.wait_ge(bias_added, ADDS[("y_turn", (L2C, b))] + 1)
                        then(v.tensor_tensor(y_sb[:, :, :], z_sb[:, :, :], old[:, :, :], ALU.add))
                    else:
                        live = live0[b] if layer == L0S else live1[b]
                        for t in range(T):
                            ins = v.scalar_tensor_tensor(out=y_sb[:, t, :], in0=z_sb[:, t, :], scalar=live[:, t:t + 1],
                                                         in1=old[:, t, :], op0=ALU.mult, op1=ALU.add)
                        then(ins)
                    moments(y_sb)
                elif kind == "norm":
                    if n == 0:
                        dve.wait_ge(rows_loaded, 16)
                    if layer == L0S:
                        normalise(res[b][1], y_sb, "L0.g1", "L0.b1", ("sum", n, 0))
                    elif layer == L0C:
                        normalise(res[b][0], y_sb, "L0.g2", "L0.b2", ("sum", n, 0), x_ready)
                    elif layer == L2S:
                        normalise(res[b][1], y_sb, "L2.g1", "L2.be1", ("out", n, 0), x_ready)
                    elif layer == L2C:
                        normalise(res[b][0], y_sb, "L2.g2", "L2.be2", ("out", n, 0), x_ready)
                    else:
                        normalise(res[b][0], y_sb, "L3.g", "L3.b", ("sum", n, 0), result_ready)
                elif kind == "live":
                    row_mask(live1[b], res[b][1])
                    if b == 0:
                        dve.wait_ge(ctx_loaded, 16 * B)
                    else:
                        dve.wait_ge(work_full, WORK[("x_turn", n - 1, 0)] + 1)
                    for t in range(T):
                        ins = v.tensor_scalar(ctxm_sb[:, t, :], ctx_sb[b][:, t, :], live1[b][:, t:t + 1], None, ALU.mult)
                    ins.then_inc(x_ready, 1)
                elif kind == "kv_sum":
                    moments(ctx_sb[b])
                elif kind == "kv_norm":
                    dve.wait_ge(work_full, kvn_last_read(kind, n))
                    normalise(kvn_sb, ctx_sb[b], "L1.g", "L1.b", ("kv_sum", n, 0), kv_ready)
                elif kind == "out":
                    full(kind, n)
                    added = {L1: ("y_turn", (L0C, b)), L2S: ("x_turn", (L1, b)), L2C: ("x_turn", (L2S, b))}[layer]
                    dve.wait_ge(bias_added, ADDS[added] + 1)
                    summed = res[b][0] if layer == L1 else y_sb
                    v.tensor_tensor(summed[:, :, :], m_ps[:, 0:S].rearrange("p (t d) -> p t d", t=T), old[:, :, :],
                                    ALU.add).then_inc(work_free, 1)
                    if layer != L1:
                        dve.wait_ge(work_free, after_use(kind, n))
                        moments(y_sb)
                elif kind == "ff2":
                    full(kind, n)
                    if layer == L0C:
                        v.tensor_tensor(xh_sb[:, :, :], m_ps[:, 0:S].rearrange("p (t d) -> p t d", t=T), R2("L0.fc2b"),
                                        ALU.add).then_inc(work_free, 1)
                        dve.wait_ge(work_free, after_use(kind, n))
                        for t in range(T):
                            ins = v.scalar_tensor_tensor(out=y_sb[:, t, :], in0=xh_sb[:, t, :],
                                                         scalar=live0[b][:, t:t + 1], in1=res[b][0][:, t, :],
                                                         op0=ALU.mult, op1=ALU.add)
                        then(ins)
                    else:
                        dve.wait_ge(bias_added, ADDS[("x_turn", (L2C, b))] + 1)
                        v.tensor_tensor(y_sb[:, :, :], m_ps[:, 0:S].rearrange("p (t d) -> p t d", t=T), res[b][0][:, :, :],
                                        ALU.add).then_inc(work_free, 1)
                        dve.wait_ge(work_free, after_use(kind, n))
                    moments(y_sb)
                elif kind == "norm2":
                    if layer == L0C:
                        normalise(res[b][1], y_sb, "L0.g3", "L0.b3", ("ff2", n, 0))
                    else:
                        normalise(res[b][1], y_sb, "L2.g3", "L2.be3", ("ff2", n, 0), y_ready)
                elif kind == "again":
                    moments(res[b][1])
                elif kind == "norm3":
                    last = kvn_last_read(kind, n)
                    if last:
                        dve.wait_ge(work_full, last)
                    normalise(kvn_sb, res[b][1], "L1.g", "L1.b", ("again", n, 0), y_ready)
                elif kind == "masks":
                    masks(u)


def kvn_last_read(kind, n):
    reads = [e for e in PLAN[:PLAN.index((kind, n, 0))] if e[0] == "kv_turn" or e[0] == "y_turn" and STEPS[e[1]][0] == L0C]
    return WORK[reads[-1]] + 1 if reads else 0


def x_buffer(layer):
    return {L0S: 1, L0C: 0, L1: 0, L2S: 1, L2C: 0}[layer]


def shape_constants():
    c = np.zeros((P, K_N), np.float32)
    i = np.arange(P)
    c[:, slice(*K_AT["ident"])] = np.eye(P)
    c[:, slice(*K_AT["causal"])] = np.where(i[None, :] > i[:, None], NEG, 0)
    c[:, slice(*K_AT["causalT"])] = np.where(i[:, None] > i[None, :], NEG, 0)
    c[:, slice(*K_AT["own_head"])] = i[:, None] % H == np.arange(H)[None, :]
    c[:, slice(*K_AT["key"])] = np.arange(S)[None, :]
    return c


def fixed_rows():
    words = np.zeros((ALL_ROWS - PARTS * PARTS * DK, H * S // 2), np.uint32)
    words[MASK_ROW - PARTS * PARTS * DK:] = 0x3F803F80
    return words.view(np.float32)


def kernel(**inputs):
    import concourse.bacc as bacc
    from concourse.bass_utils import run_bass_kernel_spmd

    a = {k: np.asarray(v) for k, v in inputs.items()}

    def l0(name):
        return a[f"L0_xattn_{name}"]

    def by_depth(w):
        return w.reshape(D, H, DK).transpose(0, 2, 1).reshape(D, D)

    def tiles(w):
        return w.reshape(-1, P, w.shape[1]).transpose(1, 0, 2).reshape(P, -1)

    def l2(name):
        return a[f"L2_xattn_{name}"]

    def l3(name):
        return a[f"L3_xattn_{name}"]

    wkv = a["L1_xattn_wkv"]
    w = {"L0.fc1": l0("fc1_w").T, "L0.fc2": l0("fc2_w").T, "L1.q": a["L1_xattn_wq"], "L1.k": wkv[:, :H * HS],
         "L1.v": wkv[:, H * HS:], "L1.o": tiles(a["L1_xattn_wo"]), "L2.f1": l2("Wf1").T, "L2.f2": tiles(l2("Wf2").T),
         "L3.q": by_depth(l3("wq").T), "L3.k": by_depth(l3("wk").T), "L3.v": l3("wv").T}
    for i in "12":
        w[f"L0.q{i}"] = l0(f"Wq{i}").transpose(1, 2, 0).reshape(D, D)
        w[f"L0.k{i}"] = l0(f"Wk{i}").transpose(1, 2, 0).reshape(D, D)
        w[f"L0.v{i}"] = l0(f"Wv{i}").transpose(1, 0, 2).reshape(D, D)
        w[f"L2.q{i}"] = by_depth(l2(f"Wq{i}").T)
        w[f"L2.k{i}"] = by_depth(l2(f"Wk{i}").T)
        w[f"L2.v{i}"] = l2(f"Wv{i}").T
        w[f"L2.o{i}"] = l2(f"Wo{i}").T
    r = {"L0.fc2b": l0("fc2_b"), "L1.g": a["L1_xattn_ln_g"], "L1.b": a["L1_xattn_ln_b"],
         "L1.bv": a["L1_xattn_bkv"][H * HS:], "L1.bo": a["L1_xattn_bo"], "L2.bo1": l2("bo1"), "L2.bo2": l2("bo2"), "L2.bf2": l2("bf2"), "L3.bv": l3("bv"), "L3.g": l3("gamma"),
         "L3.b": l3("beta")}
    for i in "123":
        r[f"L0.g{i}"], r[f"L0.b{i}"] = l0(f"ln{i}_g"), l0(f"ln{i}_b")
        r[f"L2.g{i}"], r[f"L2.be{i}"] = l2(f"g{i}"), l2(f"be{i}")

    def depth_col(v):
        return v.reshape(H, DK).T.reshape(P, 1)

    c = {"L0.fc1b": l0("fc1_b").reshape(P, 1), "L1.bq": a["L1_xattn_bq"].reshape(UNITS, P).T,
         "L1.bk": a["L1_xattn_bkv"][:H * HS].reshape(UNITS, P).T, "L2.bq1": depth_col(l2("bq1")),
         "L2.bk1": depth_col(l2("bk1")), "L2.bq2": depth_col(l2("bq2")), "L2.bk2": depth_col(l2("bk2")),
         "L2.bf1": l2("bf1").reshape(4, P).T,
         "L2.bv1": l2("bv1").reshape(P, 1), "L2.bv2": l2("bv2").reshape(P, 1), "L3.bq": depth_col(l3("bq")), "L3.bk": depth_col(l3("bk"))}
    tgt = a["mask_1x1xSxS2_ik0"].reshape(S, S)
    arrays = {
        "x": a["x"], "x_t": a["x"].reshape(B * S, D).T, "ctx": a["ctx_1024"], "ctx_t": a["ctx_1024"].reshape(B * S, D).T,
        "weights": np.concatenate([w[name] for name, _ in WEIGHTS], axis=1),
        "rows": np.concatenate([r[name] for name, _ in ROWS]).reshape(1, R_N),
        "cols": np.concatenate([c[name] for name, _ in COLS], axis=1),
        "consts": shape_constants(), "fixed_rows": fixed_rows(),
        "src_mask": a["mask_Bx1x1xS2_if1"].reshape(1, B * S), "tgt_mask": tgt, "tgt_mask_t": tgt.T,
        "key_mask": a["mask_BxS2_ik0"],
    }
    arrays = {k: np.ascontiguousarray(v) for k, v in arrays.items()}
    nc = bacc.Bacc("TRN2", target_bir_lowering=False, num_devices=1)
    aps = {k: nc.dram_tensor(f"{k}_dram", v.shape, mybir.dt.from_np(v.dtype), kind="ExternalInput").ap()
           for k, v in arrays.items()}
    out = nc.dram_tensor("out_dram", (B, S, D), F32, kind="ExternalOutput").ap()
    attention_stack_program(nc, out=out, **aps)
    ran = run_bass_kernel_spmd(nc, [{f"{k}_dram": v for k, v in arrays.items()}], core_ids=[0])
    return ran.results[0]["out_dram"]
```

```python
from contextlib import ExitStack

import numpy as np

import concourse.bass as bass
from concourse import mybir

F32 = mybir.dt.float32
BF16 = mybir.dt.bfloat16
I32 = mybir.dt.int32
ALU = mybir.AluOpType
ACT = mybir.ActivationFunctionType
AX = mybir.AxisListType

P = 128
B, S, D, H = 4, 256, 128, 16
DK = D // H
HS = 64
T = S // P
EPS = 1e-5
NEG = -(2.0 ** 126)
CAP = 2.0 ** 125
PAD = float(-2 ** 32 + 1)
PARTS = 3
MASK_ROW = 96
NEGMAX_ROW = 97
SCORE_ROWS = MASK_ROW + 1
ALL_ROWS = NEGMAX_ROW + PARTS
RING = 3

L0S, L0C, L1, L2S, L2C, L3 = range(6)
LAYERS = [L0S, L0C, L1, L2S, L2C, L3]
STEPS = [(layer, b) for layer in LAYERS for b in range(B)]
N = len(STEPS)
CAUSAL = (L0S, L1)
UNITS = 8

WEIGHTS = [("L0.q1", 128), ("L0.k1", 128), ("L0.v1", 128), ("L0.q2", 128), ("L0.k2", 128), ("L0.v2", 128),
           ("L0.fc1", 128), ("L0.fc2", 128), ("L1.q", 1024), ("L1.k", 1024), ("L1.v", 1024), ("L1.o", 1024),
           ("L2.q1", 128), ("L2.k1", 128), ("L2.v1", 128), ("L2.o1", 128),
           ("L2.q2", 128), ("L2.k2", 128), ("L2.v2", 128), ("L2.o2", 128), ("L2.f1", 512), ("L2.f2", 512),
           ("L3.q", 128), ("L3.k", 128), ("L3.v", 128)]
ROWS = [("L0.g1", 128), ("L0.b1", 128), ("L0.g2", 128), ("L0.b2", 128), ("L0.g3", 128), ("L0.b3", 128),
        ("L0.fc2b", 128), ("L1.g", 128), ("L1.b", 128), ("L1.bv", 1024), ("L1.bo", 128),
        ("L2.bo1", 128), ("L2.g1", 128), ("L2.be1", 128), ("L2.bo2", 128), ("L2.g2", 128), ("L2.be2", 128),
        ("L2.bf2", 128), ("L2.g3", 128), ("L2.be3", 128), ("L3.bv", 128), ("L3.g", 128), ("L3.b", 128)]
COLS = [("L0.fc1b", 1), ("L1.bq", 8), ("L1.bk", 8), ("L2.bq1", 1), ("L2.bk1", 1), ("L2.bq2", 1), ("L2.bk2", 1),
        ("L2.bf1", 4), ("L2.bv1", 1), ("L2.bv2", 1), ("L3.bq", 1), ("L3.bk", 1)]
CONSTS = [("own_head", 16), ("key", 256), ("ident", 128), ("causal", 128), ("causalT", 128)]


def offsets(table):
    at, found = 0, {}
    for name, n in table:
        found[name] = (at, at + n)
        at += n
    return found, at


W_AT, W_N = offsets(WEIGHTS)
W_HOME = dict(W_AT)
W_HOME.update({f"L2.{x}1": W_AT[f"L0.{x}1"] for x in "qkv"} | {f"L2.{x}2": W_AT[f"L0.{x}2"] for x in "qkv"})
RESIDENT = W_AT["L2.q1"][0]
W_HOME["L2.o1"] = (RESIDENT, RESIDENT + P)
W_HOME["L2.f1"] = (W_AT["L1.q"][0], W_AT["L1.q"][0] + 512)
W_HOME["L2.f2"] = (W_AT["L1.q"][0] + 512, W_AT["L1.q"][1])
for i, name in enumerate(("L2.o2", "L3.q", "L3.k", "L3.v")):
    W_HOME[name] = (W_AT["L1.k"][0] + i * P, W_AT["L1.k"][0] + (i + 1) * P)
LATE = {"first": ["L2.q1", "L2.k1", "L2.v1", "L2.o1"], "second": ["L2.q2", "L2.k2", "L2.v2"],
        "third": ["L2.o2", "L2.f1", "L2.f2", "L3.q", "L3.k", "L3.v"]}
R_AT, R_N = offsets(ROWS)
C_AT, C_N = offsets(COLS)
K_AT, K_N = offsets(CONSTS)
K_BF = K_AT["ident"][0]
K_F32 = K_AT["causal"][0]
W_CUTS = [0, W_AT["L0.fc1"][0], W_AT["L1.k"][0], W_AT["L1.v"][0], W_AT["L1.o"][0], RESIDENT]
R_CUTS = [0, R_AT["L1.bv"][0], R_AT["L1.bo"][0], R_N]


def narrow(n):
    return 0 <= n < N and STEPS[n][0] != L1


def wide(n):
    return 0 <= n < N and STEPS[n][0] == L1


NARROW = [n for n in range(N) if narrow(n)]
ORD = {n: j for j, n in enumerate(NARROW)}


TAILS = {
    L0S: [("turn0", 0.25), ("turn1", 1.25), ("sum", 1.25), ("norm", 5), ("live", 6.75), ("x_turn", 8.25)],
    L0C: [("turn0", 1), ("turn1", 2.5), ("sum", 2.75), ("norm", 4), ("x_turn", 5), ("ff1", 5.5), ("ff2", 6.75),
          ("norm2", 7.75), ("again", 8.75), ("norm3", 10.25), ("y_turn", 10.75)],
    L1: [("out", 0.25), ("x_turn", 2.75)],
    L2S: [("turn0", 1.75), ("turn1", 2), ("z_turn", 3.75), ("out", 4.75), ("norm", 5.5), ("x_turn", 7.75)],
    L2C: [("turn0", 1.25), ("turn1", 2.25), ("z_turn", 2.5), ("out", 2.75), ("norm", 3.75), ("x_turn", 4.25),
          ("ff1a", 5.25), ("ff1b", 6), ("ff2", 7.5), ("norm2", 8.5), ("y_turn", 10.75)],
    L3: [("turn0", 1.25), ("turn1", 3.75), ("sum", 4.5), ("norm", 8.25)],
}
BEFORE_WIDE = [("turn0", 0.25), ("turn1", 2), ("sum", 2.75), ("norm", 3.5), ("x_turn", 3.75), ("ff1", 4),
               ("ff2", 4), ("norm2", 5), ("again", 5), ("norm3", 5.75), ("y_turn", 6.25)]
AHEAD = {
    L0S: [("qk", 0), ("split", 2), ("count", 4), ("v", 5)],
    L0C: [("qk", 3.25), ("split", 3.75), ("count", 4), ("v", 5.75)],
    L2S: [("qk", 1.75), ("split", 2.75), ("v", 7.5)],
    L2C: [("qk", 2), ("split", 2.5), ("v", 7)],
    L3: [("qk", 3.5), ("split", 3.75), ("v", 7)],
}
AHEAD_IN_WIDE = [("qk", 2), ("split", 3.5), ("v", 3.75)]
NM_AT = [("last", 0.75), ("first", 5)]
KV_AT = [("kv_sum", 5.25), ("kv_norm", 5.5), ("kv_turn", 6.75)]
KV_IN_WIDE = [("kv_sum", 6.5), ("kv_norm", 6.75), ("kv_turn", 7.75)]
V1_AT = [("v1_0", 0.25), ("v1_1", 1), ("v1_2", 2.5), ("v1_3", 5.75)]
LOADS_AT = [("rows 0", 5), ("weights 1", 9), ("masks", 10), ("rows 1", 19), ("rows 2", 26), ("weights 2", 25),
            ("weights 3", 30), ("context", 34), ("weights 4", 38)]
MASKS_AT = [("masks", 0.5), ("masks", 7), ("masks", 7.25), ("masks", 7.5)]
WIDE_AT = (512, 0)
NO_BANK = ("st", "pv", "scale", "exp", "pt", "sum", "norm", "live", "norm2", "again", "norm3", "split",
           "kv_sum", "kv_norm", "load", "masks")


def pieces_at(k, at):
    got = []
    for (which, p), (n, half) in zip(NM_AT, ((k, 1), (k + 1, 0))):
        if narrow(n) and p == at:
            got.append(("nm", n, half))
    for n, place in ((k - 2, at + UNITS), (k - 1, at)):
        if 0 <= n < N:
            tail = BEFORE_WIDE if STEPS[n] == (L0C, B - 1) else TAILS[STEPS[n][0]]
            got += [(name, n, 0) for name, p in tail if p == place]
    if k == -2 and at == UNITS - 0.25:
        got += [(name, 1, 0) for name, _ in AHEAD[L0S]]
    elif narrow(k + 2) and k != -1:
        layer = STEPS[k + 2][0]
        for name, p in AHEAD_IN_WIDE if wide(k) else AHEAD[layer]:
            if p == at:
                got.append((name, k + 2, 0))
    if wide(k + 2):
        got += [(name, k + 2, 0) for name, p in (KV_AT if narrow(k) else KV_IN_WIDE) if p == at]
    if wide(k + 1):
        got += [(name, k + 1, 0) for name, p in V1_AT if p == at]
    got += [("load", i, 0) for i, (name, p) in enumerate(LOADS_AT) if p == UNITS * k + at]
    if k == B - 1:
        got += [(name, k, i) for i, (name, p) in enumerate(MASKS_AT) if p == at]
    return got


def score_banks(n, v):
    g, t = divmod(v, T)
    if STEPS[n][0] in CAUSAL and t == 0:
        return [(t, 4 * g, 4, P)]
    return [(t, 4 * g + 2 * x, 2, S) for x in range(2)]


def second(n, v):
    return [("s_2", n, v)] if narrow(n) and len(score_banks(n, v)) == 2 else []


def make_plan():
    plan = []
    for k in range(-2, N + 2):
        for u in range(UNITS):
            i = UNITS * k + u
            one, two, three = (divmod(i + ahead, UNITS) for ahead in (1, 2, 3))
            plan += pieces_at(k, u)
            if wide(one[0]):
                plan.append(("scale", *one))
            if narrow(one[0]) and i + 1 >= 0:
                plan.append(("st", *one))
            if wide(two[0]):
                plan.append(("st", *two))
            if wide(three[0]):
                plan.append(("qk1", *three))
            if wide(two[0]):
                plan.append(("exp", *two))
            plan += pieces_at(k, u + 0.25)
            if narrow(k + 1):
                plan.append(("s", k + 1, u))
            plan += second(k + 1, u)
            plan += pieces_at(k, u + 0.5)
            if 0 <= k < N:
                plan.append(("pv", k, u))
            plan += pieces_at(k, u + 0.75)
            if wide(one[0]):
                plan.append(("pt", *one))
    return plan


PLAN = make_plan()


def number(events):
    return {e: i for i, e in enumerate(events)}


USES = number([(kind, n, v, x) for kind, n, v in PLAN if kind == "pt" or kind not in NO_BANK
               for x in range(2 if kind == "pt" else 1)])
BANKS = 3


def bank(kind, n, u=0, x=0):
    return USES[(kind, n, u, x)] % BANKS


def nth(kind, n, u=0, x=0):
    return USES[(kind, n, u, x)] // BANKS + 1


NORMS = number([e for e in PLAN if e[0] in ("sum", "again", "kv_sum", "ff2") or e[0] == "out" and narrow(e[1])])
ADDED = {("y_turn", L0C): (1, "L1.bo"), ("x_turn", L1): (0, "L2.bo1"), ("x_turn", L2S): (1, "L2.bo2"),
         ("x_turn", L2C): (0, "L2.bf2"), ("y_turn", L2C): (1, "L3.bv")}
ADDS = number([(kind, STEPS[n]) for kind, n, _ in PLAN if 0 <= n < N and (kind, STEPS[n][0]) in ADDED])
OUSE = number([(n, h) for n in range(N) for h in range(UNITS if wide(n) else 2)])


def attention_stack_program(nc, x, x_t, ctx, ctx_t, weights, rows, cols, consts, fixed_rows, src_mask, tgt_mask,
                            tgt_mask_t, key_mask, out):
    with ExitStack() as stack:
        def sb(name, shape, dt=F32):
            return stack.enter_context(nc.sbuf_tensor(name, shape, dt))

        def psum(name, shape):
            return stack.enter_context(nc.psum_tensor(name, shape, F32))

        def sem(name):
            return stack.enter_context(nc.semaphore(name))

        w_sb = sb("w_sb", [P, RESIDENT + P])
        row_sb = sb("row_sb", [P, R_N])
        col_sb = sb("col_sb", [P, C_N])
        const_sb = sb("const_sb", [P, K_F32])
        const_bf = sb("const_bf", [P, K_N - K_BF], BF16)
        q_stack = [sb(f"q_stack{i}", [P, H, S], BF16) for i in range(RING)]
        k_stack = [sb(f"k_stack{i}", [P, H, S], BF16) for i in range(RING)]
        qk_sb = [sb(f"qk_sb{i}", [P, 2, S]) for i in range(2)]
        parts = [sb(f"parts{i}", [P, 2, PARTS, S], BF16) for i in range(2)]
        rest = sb("rest", [P, 2, S])
        v_sb = [sb(f"v_sb{b}", [P, T, H, 32]) for b in range(B)]
        v1_sb = [sb(f"v1_sb{i}", [P, T, H * HS]) for i in range(2)]
        q1_sb = [sb(f"q1_sb{i}", [P, 2, S]) for i in range(2)]
        k1_sb = [sb(f"k1_sb{i}", [P, S]) for i in range(2)]
        ctx1_t = sb("ctx1_t", [P, UNITS, S])
        probs1_t = sb("probs1_t", [P, 3 * S])
        negmax1 = [sb(f"negmax1_{i}", [P, T, 2]) for i in range(2)]
        sums1 = [sb(f"sums1_{i}", [P, T, 2]) for i in range(2)]
        rec1 = sb("rec1", [P, T, 2])
        probs = [sb(f"probs{i}", [P, 4 * S]) for i in range(2)]
        negmax = [sb(f"negmax{i}", [P, T, H]) for i in range(2)]
        nm_rest = sb("nm_rest", [P, T, 8])
        nm_parts = [sb(f"nm_parts{i}", [P, T, PARTS, 8], BF16) for i in range(2)]
        nm_rows = [sb(f"nm_rows{i}", [PARTS * 8, S], BF16) for i in range(2)]
        q0_own = sb("q0_own", [P, H])
        nonzero = sb("nonzero", [H, S])
        length = sb("length", [H, 1])
        key_row = [sb(f"key_row{b}", [H, S], BF16) for b in range(B)]
        src_rows = sb("src_rows", [H, B, S], BF16)
        zero_row = sb("zero_row", [H, S], BF16)
        pad_row = sb("pad_row", [H, S], BF16)
        tgt_bias = sb("tgt_bias", [P, T, S], BF16)
        tgt_bias_t = sb("tgt_bias_t", [P, T, S], BF16)
        raw = [t[:, :, :].rearrange("p t n -> p (t n)") for t in v1_sb]
        int_tgt = raw[0][:, 0:4 * S].bitcast(I32).rearrange("p (w t k) -> p w t k", w=2, t=T)
        int_src = raw[0][0:H, 4 * S:8 * S].bitcast(I32).rearrange("p (b k) -> p b k", b=B)
        int_key = raw[1][:, 0:S].bitcast(I32)
        key_f = raw[1][:, S:2 * S]
        const_f = raw[1][:, 2 * S:2 * S + K_N - K_F32]
        key_min = sb("key_min", [P, 1])
        q_gate = sb("q_gate", [P, 1])
        q_gate_bias = sb("q_gate_bias", [P, 1])
        o_sb = sb("o_sb", [P, 4, S])
        res = [[sb(f"res{b}_{i}", [P, T, D]) for i in range(2)] for b in range(B)]
        ctx_sb = [sb(f"ctx_sb{b}", [P, T, D]) for b in range(B)]
        x_turned = [sb(f"x_turned{b}", [P, S]) for b in range(B)]
        ctx_turned = [sb(f"ctx_turned{b}", [P, S]) for b in range(B)]
        ctxm_turned = [sb(f"ctxm_turned{b}", [P, S]) for b in range(B)]
        kvn_turned = [sb(f"kvn_turned{b}", [P, S]) for b in range(B)]
        z_sb = sb("z_sb", [P, T, D])
        z_turned = sb("z_turned", [P, S])
        y_sb = sb("y_sb", [P, T, D])
        xh_sb = sb("xh_sb", [P, T, D])
        kvn_sb = sb("kvn_sb", [P, T, D])
        ctxm_sb = sb("ctxm_sb", [P, T, D])
        hidden = ctx1_t[:, 4:8, :]
        rec = sb("rec", [P, H])
        stats = sb("stats", [P, T, 6])
        mean_var = sb("mean_var", [P, T, 2])
        var_eps = sb("var_eps", [P, T])
        rstd = sb("rstd", [P, T])
        minus_half = sb("minus_half", [P, T])
        absmax = sb("absmax", [P, T])
        live0 = [sb(f"live0_{b}", [P, T]) for b in range(B)]
        live1 = [sb(f"live1_{b}", [P, T]) for b in range(B)]

        st_ps = [psum(f"st_ps{i}", [P, 1024]) for i in range(2)]
        o_ps = psum("o_ps", [P, 512])
        bank_ps = [psum(f"bank_ps{i}", [P, 512]) for i in range(BANKS)]

        small_loaded = sem("small_loaded")
        rows_loaded = [sem(f"rows_loaded{i}") for i in range(len(R_CUTS) - 1)]
        ctx_t_loaded = sem("ctx_t_loaded")
        x0_loaded = sem("x0_loaded")
        x_loaded = sem("x_loaded")
        tok_loaded = sem("tok_loaded")
        ctx_loaded = sem("ctx_loaded")
        bias_added = sem("bias_added")
        w_loaded = [sem(f"w_loaded{i}") for i in range(len(W_CUTS) - 1)]
        late_loaded = {x: sem(f"late_loaded_{x}") for x in LATE}
        masks_loaded = sem("masks_loaded")
        dve_step = sem("dve_step")
        pool_step = sem("pool_step")
        stack_blank = [sem(f"stack_blank{i}") for i in range(RING)]
        v_blank = sem("v_blank")
        blank = sem("blank")
        consts_ready = sem("consts_ready")
        masks_ready = sem("masks_ready")
        bank_full = [sem(f"bank_full{i}") for i in range(BANKS)]
        bank_read = [sem(f"bank_read{i}") for i in range(BANKS)]
        st_full = sem("st_full")
        exp_done = sem("exp_done")
        pv_done = sem("pv_done")
        o_free = sem("o_free")
        q0_ready = sem("q0_ready")
        parts_ready = sem("parts_ready")
        bounced = [sem(f"bounced{i}") for i in range(2)]
        stacked = [sem(f"stacked{i}") for i in range(RING)]
        key_row_ready = sem("key_row_ready")
        nm_parts_ready = sem("nm_parts_ready")
        nm_stacked = [sem(f"nm_stacked{i}") for i in range(2)]
        max1_ready = sem("max1_ready")
        scaled = sem("scaled")
        ctxm_ready = sem("ctxm_ready")
        var_ready = sem("var_ready")
        rstd_ready = sem("rstd_ready")
        norm_done = sem("norm_done")
        stored = sem("stored")

        bounce = [nc.dram_tensor(f"bounce{i}", [2, PARTS, P, S], BF16, kind="Internal").ap() for i in range(2)]

        def W(name, a=0, n=None):
            lo, hi = W_HOME[name]
            return w_sb[:, lo + a:(hi if n is None else lo + a + n)]

        def R(name, a=0, n=None):
            lo, hi = R_AT[name]
            return row_sb[:, lo + a:(hi if n is None else lo + a + n)]

        def R2(name):
            return R(name).unsqueeze(1).to_broadcast([P, T, D])

        def C(name, i=0):
            lo = C_AT[name][0] + i
            return col_sb[:, lo:lo + 1]

        def K(name):
            return const_sb[:, K_AT[name][0]:K_AT[name][1]]

        def KB(name):
            return const_bf[:, K_AT[name][0] - K_BF:K_AT[name][1] - K_BF]

        def by_head(ap, heads):
            return ap.unsqueeze(1).to_broadcast([ap.shape[0], heads, ap.shape[1]])

        def has(name):
            return {n: i + 1 for i, n in enumerate(n for n in NARROW if (name, n, 0, 0) in USES)}

        Z_TURNS, COUNTS = has("z_turn"), has("count")

        def full_of(kind, n, u=0, x=0):
            return bank_full[bank(kind, n, u, x)], nth(kind, n, u, x)

        def read_of(kind, n, u=0, x=0):
            return bank_read[bank(kind, n, u, x)], nth(kind, n, u, x)

        def step_of(layer, b):
            return STEPS.index((layer, b))

        STARTS_IN = {L0S: 0, L0C: 1, L1: 1, L2S: 0, L2C: 1, L3: 1}

        def split(engine, then_, src, rest_, p):
            then_(engine.tensor_scalar(src, src, CAP, None, ALU.min))
            then_(engine.tensor_copy(p(0), src))
            then_(engine.tensor_tensor(rest_, src, p(0), ALU.subtract))
            then_(engine.tensor_copy(p(1), rest_))
            return engine.tensor_tensor(p(2), rest_, p(1), ALU.subtract)

        block = stack.enter_context(nc.Block())

        @block.sync
        def _(sp):
            sp.dma_start(x_turned[0][:, :], x_t[:, 0:S]).then_inc(x0_loaded, 16)
            sp.dma_start(w_sb[:, W_CUTS[0]:W_CUTS[1]], weights[:, W_CUTS[0]:W_CUTS[1]]).then_inc(w_loaded[0], 16)
            sp.dma_start(const_sb[:, :], consts[:, 0:K_F32]).then_inc(small_loaded, 16)
            sp.dma_start(const_f, consts[:, K_F32:K_N]).then_inc(small_loaded, 16)
            sp.dma_start(col_sb[:, :], cols).then_inc(small_loaded, 16)

            def blank_stack(i):
                for t in (q_stack[i], k_stack[i]):
                    rows_ = t[PARTS * PARTS * DK:ALL_ROWS, :, :].rearrange("p h q -> p (h q)").bitcast(F32)
                    sp.dma_start(rows_, fixed_rows).then_inc(stack_blank[i], 16)

            blank_stack(0)
            for b in range(1, B):
                sp.dma_start(x_turned[b][:, :], x_t[:, b * S:(b + 1) * S]).then_inc(x_loaded, 16)
            for b in range(B):
                sp.dma_start(res[b][0][:, :, :], x[b].rearrange("(t p) d -> p t d", p=P)).then_inc(tok_loaded, 16)

            def store_parts(n):
                j = ORD[n]
                sp.wait_ge(parts_ready, j + 1)
                if j >= 2:
                    sp.wait_ge(stacked[(j - 2) % RING], 16 * 5 * ((j - 2) // RING + 1))
                sp.dma_start(bounce[j % 2].rearrange("w a p q -> p (w a) q"),
                             parts[j % 2][:, :, :, :].rearrange("p w a q -> p (w a) q")).then_inc(bounced[j % 2], 16)

            def stack_step(n):
                j, layer, b = ORD[n], *STEPS[n]
                slot = j % RING
                if layer in (L0S, L0C):
                    sp.wait_ge(key_row_ready, COUNTS[n])
                    row = key_row[b][:, :]
                else:
                    if j == ORD[step_of(L2S, 0)]:
                        sp.wait_ge(masks_ready, len(MASKS_AT))
                    row = {L2S: zero_row[:, :], L2C: src_rows[:, b, :], L3: pad_row[:, :]}[layer]
                sp.wait_ge(stack_blank[slot], 32)
                if j >= RING:
                    sp.wait_ge(pv_done, UNITS * NARROW[j - RING] + UNITS)
                sp.wait_ge(bounced[j % 2], 16 * (j // 2 + 1))
                src = bounce[j % 2]
                for a in range(PARTS):
                    part = src[0, a].rearrange("(d h) q -> d (h q)", h=H)
                    sp.dma_start(q_stack[slot][24 * a:24 * a + 24, :, :].rearrange("p h q -> p (h q)"),
                                 part.unsqueeze(0).to_broadcast([PARTS, DK, H * S])).then_inc(stacked[slot], 16)
                every = src[1].rearrange("a (d h) q -> (a d) (h q)", h=H)
                sp.dma_start(k_stack[slot][0:72, :, :].rearrange("p h q -> p (h q)"),
                             every.unsqueeze(0).to_broadcast([PARTS, PARTS * DK, H * S])).then_inc(stacked[slot], 16)
                sp.dma_start(k_stack[slot][MASK_ROW:MASK_ROW + 1, :, :], row).then_inc(stacked[slot], 16)

            blank_stack(1)
            blank_stack(2)
            def late_weights(x):
                for name in LATE[x]:
                    lo, hi = W_AT[name]
                    sp.dma_start(W(name), weights[:, lo:hi]).then_inc(late_loaded[x], 16)

            for kind, n, half in PLAN:
                if kind == "split":
                    store_parts(n)
                elif kind == "v":
                    stack_step(n)
                    if n == B:
                        sp.wait_ge(*full_of("v", B - 1, 0))
                        late_weights("first")
                    elif n == step_of(L2S, 0):
                        sp.wait_ge(*full_of("v", 2 * B - 1, 0))
                        late_weights("second")
                    elif n == step_of(L2C, 0):
                        sp.wait_ge(*full_of("qk1", step_of(L1, B - 1), UNITS - 1))
                        late_weights("third")
                elif kind == "nm":
                    j = ORD[n]
                    sp.wait_ge(*read_of(kind, n, half))
                    sp.dma_start(q_stack[j % RING][NEGMAX_ROW:NEGMAX_ROW + PARTS, 8 * half:8 * half + 8, :],
                                 nm_rows[half][:, :]).then_inc(nm_stacked[half], 16)
            for b in range(B):
                sp.wait_ge(norm_done, NORMS[("sum", step_of(L3, b), 0)] + 1)
                sp.dma_start(out[b].rearrange("(t p) d -> p t d", p=P), res[b][0][:, :, :]).then_inc(stored, 16)
            sp.wait_ge(stored, 16 * B)

        @block.gpsimd
        def _(pool):
            steps = [0]

            def then(ins):
                steps[0] += 1
                ins.then_inc(pool_step, 1)
                pool.wait_ge(pool_step, steps[0])

            for b, t in enumerate(v_sb):
                then(nc.gpsimd.memset(t[:, :, :, :], 0.0))
                nc.gpsimd.memset(t[:, :, :, DK:DK + 1], 1.0).then_inc(v_blank, 1)
            then(nc.gpsimd.memset(zero_row[:, :], 0.0))
            for t in q1_sb:
                then(nc.gpsimd.memset(t[:, :, :], 0.0))
            nc.gpsimd.memset(minus_half[:, :], -0.5).then_inc(blank, 1)
            pool.wait_ge(blank, 1)
            for b in range(B):
                pool.dma_start(ctx_sb[b][:, :, :], ctx[b].rearrange("(t p) d -> p t d", p=P)).then_inc(ctx_loaded, 16)

            def load_weights(i):
                lo, hi = W_CUTS[i], W_CUTS[i + 1]
                pool.dma_start(w_sb[:, lo:hi], weights[:, lo:hi]).then_inc(w_loaded[i], 16)

            def load_rows(i):
                lo, hi = R_CUTS[i], R_CUTS[i + 1]
                pool.dma_start(row_sb[:, lo:hi], rows[:, lo:hi].to_broadcast([P, hi - lo])).then_inc(rows_loaded[i], 16)

            def load_masks():
                pool.dma_start(int_src[:, :, :], src_mask.to_broadcast([H, B * S])).then_inc(masks_loaded, 16)
                for i, m in enumerate((tgt_mask, tgt_mask_t)):
                    pool.dma_start(int_tgt[:, i, :, :], m.rearrange("(t p) k -> p t k", p=P)).then_inc(masks_loaded, 16)
                pool.dma_start(int_key, key_mask).then_inc(masks_loaded, 16)

            def load_context():
                for b in range(B):
                    pool.dma_start(ctx_turned[b][:, :], ctx_t[:, b * S:(b + 1) * S]).then_inc(ctx_t_loaded, 16)

            for kind, n, u in PLAN:
                layer, b = STEPS[n] if 0 <= n < N else (None, None)
                if kind == "s_2" and u % 4 == 3:
                    j, half = ORD[n], u // 4
                    pool.wait_ge(*read_of(kind, n, u))
                    if j:
                        pool.wait_ge(*full_of("nm", NARROW[j - 1], half))
                    p = nm_parts[half]
                    split(nc.gpsimd, then, negmax[j % 2][:, :, 8 * half:8 * half + 8], nm_rest[:, :, :],
                          lambda a: p[:, :, a, :]).then_inc(nm_parts_ready, 1)
                if kind == "load":
                    what, _, i = LOADS_AT[n][0].partition(" ")
                    if what == "rows":
                        load_rows(int(i))
                    elif what == "weights":
                        load_weights(int(i))
                    elif what == "masks":
                        load_masks()
                    else:
                        load_context()
                if (kind, n, u) in NORMS:
                    pool.wait_ge(var_ready, NORMS[(kind, n, u)] + 1)
                    then(nc.gpsimd.tensor_scalar(var_eps[:, :], mean_var[:, :, 1], EPS, None, ALU.add))
                    nc.gpsimd.tensor_tensor(rstd[:, :], var_eps[:, :], minus_half[:, :],
                                            ALU.pow).then_inc(rstd_ready, 1)
                if (kind, layer) in ADDED:
                    buffer, bias = ADDED[(kind, layer)]
                    if (kind, n) == ("y_turn", step_of(L0C, 0)):
                        pool.wait_ge(rows_loaded[2], 16)
                    pool.wait_ge(*full_of(kind, n))
                    nc.gpsimd.tensor_tensor(res[b][buffer][:, :, :], res[b][buffer][:, :, :], R2(bias),
                                            ALU.add).then_inc(bias_added, 1)

        @block.tensor
        def _(pe):
            def mm(o, lhs, rhs, start):
                return nc.tensor.matmul(o, lhs, rhs, start=start, stop=True, skip_group_check=True)

            def turn(o, i, bf=False):
                ident = KB("ident") if bf else K("ident")
                return nc.tensor.transpose(o, i, ident)

            def bias(o, rhs):
                return mm(o, KB("ident"), rhs, False)

            def bank_heads(ps, heads, width, lo, hi):
                return ps[:, 0:heads * width].rearrange("p (h q) -> p h q", h=heads)[:, :, lo:hi]

            def free_bank(kind, n, u, x=0):
                if USES[(kind, n, u, x)] >= BANKS:
                    pe.wait_ge(bank_read[bank(kind, n, u, x)], nth(kind, n, u, x) - 1)
                return bank_ps[bank(kind, n, u, x)]

            def scores(kind, n, v):
                layer, b = STEPS[n]
                j = ORD[n]
                q, k = q_stack[j % RING], k_stack[j % RING]
                if v == 0 and kind == "s":
                    pe.wait_ge(stacked[j % RING], 16 * 5 * (j // RING + 1))
                    pe.wait_ge(stack_blank[j % RING], 32)
                    if n == 0:
                        pe.wait_ge(small_loaded, 48)
                        pe.wait_ge(consts_ready, 2)
                    if n == step_of(L2S, 0):
                        pe.wait_ge(masks_ready, len(MASKS_AT))
                t, h0, heads, keys = score_banks(n, v)[kind == "s_2"]
                ps = free_bank(kind, n, v)
                for e in range(heads):
                    last = mm(ps[:, e * keys:(e + 1) * keys], q[0:SCORE_ROWS, h0 + e, t * P:(t + 1) * P],
                              k[0:SCORE_ROWS, h0 + e, 0:keys], e == 0)
                if layer == L0S:
                    last = bias(bank_heads(ps, heads, keys, t * P, (t + 1) * P), by_head(KB("causal"), heads))
                elif layer == L2S:
                    last = bias(bank_heads(ps, heads, keys, 0, keys), by_head(tgt_bias[:, t, :], heads))
                last.then_inc(bank_full[bank(kind, n, v)], 1)

            def scores_t(n, u):
                layer, b = STEPS[n]
                i = UNITS * n + u
                if i >= 2:
                    pe.wait_ge(exp_done, i - 1)
                ps = st_ps[i % 2]
                if wide(n):
                    pe.wait_ge(*read_of("qk1", n, u))
                    q, k = q1_sb[u % 2], k1_sb[u % 2]
                    for t in (1, 0):
                        lo, keys = WIDE_AT[t], (t + 1) * P
                        for e in range(2):
                            mm(ps[:, lo + e * keys:lo + (e + 1) * keys], q[:, e, t * P:(t + 1) * P], k[:, 0:keys],
                               e == 0)
                        last = bias(bank_heads(ps[:, lo:lo + 2 * keys], 2, keys, t * P, (t + 1) * P),
                                    by_head(KB("causal"), 2))
                    last.then_inc(st_full, 1)
                    return
                g, t = divmod(u, T)
                j = ORD[n]
                q, k = q_stack[j % RING], k_stack[j % RING]
                if u % 4 == 0:
                    pe.wait_ge(nm_stacked[u // 4], 16 * (j + 1))
                lo = t * P if layer in CAUSAL else 0
                wq = S - lo
                for e in range(4):
                    last = mm(ps[:, e * wq:(e + 1) * wq], k[0:ALL_ROWS, 4 * g + e, t * P:(t + 1) * P],
                              q[0:ALL_ROWS, 4 * g + e, lo:S], (e * wq) % 512 == 0)
                if layer == L0S and t == 0:
                    for x in range(2):
                        last = bias(bank_heads(ps[:, 512 * x:512 * x + 512], 2, S, 0, P), by_head(KB("causalT"), 2))
                elif layer == L0S:
                    last = bias(bank_heads(ps, 4, P, 0, P), by_head(KB("causalT"), 4))
                elif layer == L2S:
                    for x in range(2):
                        last = bias(bank_heads(ps[:, 512 * x:512 * x + 512], 2, S, 0, S),
                                    by_head(tgt_bias_t[:, t, :], 2))
                last.then_inc(st_full, 1)

            def times_v(n, u):
                layer, b = STEPS[n]
                i = UNITS * n + u
                p = probs[i % 2]
                if wide(n):
                    if u == 0:
                        pe.wait_ge(*read_of("v1_3", n))
                    for x in range(T):
                        pe.wait_ge(*read_of("pt", n, u, x))
                    pe.wait_ge(o_free, OUSE[(n, u)])
                    for t in range(T):
                        wq = S - t * P
                        for e in range(2):
                            h = 2 * u + e
                            last = mm(o_ps[HS * e:HS * e + HS, t * P:S], v1_sb[b % 2][:, t, h * HS:(h + 1) * HS],
                                      probs1_t[:, 512 * t + e * wq:512 * t + (e + 1) * wq], t == 0)
                    last.then_inc(pv_done, 1)
                    return
                pe.wait_ge(exp_done, i + 1)
                g, t = divmod(u, T)
                if u == 0:
                    pe.wait_ge(*read_of("v", n))
                    pe.wait_ge(v_blank, b + 1)
                if u % 4 == 0 and OUSE[(n, u // 4)]:
                    pe.wait_ge(o_free, OUSE[(n, u // 4)])
                lo = t * P if layer in CAUSAL else 0
                wq = S - lo
                for e in range(4):
                    last = mm(o_ps[32 * e:32 * e + 32, (g % 2) * S + lo:(g % 2) * S + S],
                              v_sb[b][:, t, 4 * g + e, :], p[:, e * wq:(e + 1) * wq], t == 0)
                last.then_inc(pv_done, 1)

            def qk_wide(m_ps, n, u):
                b = STEPS[n][1]
                if u == 0:
                    pe.wait_ge(w_loaded[1], 16)
                    pe.wait_ge(w_loaded[2], 16)
                    pe.wait_ge(*read_of("y_turn", n - B))
                    pe.wait_ge(*read_of("kv_turn", n))
                mm(m_ps[:, 0:S], W("L1.q", u * P, P), x_turned[b][:, :], True)
                return mm(m_ps[:, S:2 * S], W("L1.k", u * P, P), kvn_turned[b][:, :], False)

            def turn_probs(n, u):
                i = UNITS * n + u
                pe.wait_ge(scaled, i - UNITS * step_of(L1, 0) + 1)
                for x in range(T):
                    ps, wq = free_bank("pt", n, u, x), S - x * P
                    for e in range(2):
                        for t in range(x, T):
                            p = probs[i % 2][:, WIDE_AT[t] + e * (t + 1) * P + x * P:][:, 0:P]
                            last = turn(ps[:, e * wq + (t - x) * P:e * wq + (t - x + 1) * P], p)
                    last.then_inc(bank_full[bank("pt", n, u, x)], 1)

            def piece(m_ps, kind, n, u):
                layer, b = STEPS[n]
                if kind in ("qk", "v") and layer != L0S:
                    pe.wait_ge(*read_of("y_turn" if layer == L3 else "x_turn", n - B))
                if kind == "qk":
                    if layer == L0S:
                        pe.wait_ge(*((x0_loaded, 16) if b == 0 else (x_loaded, 16 * (B - 1))))
                        pe.wait_ge(w_loaded[0], 16)
                        mm(m_ps[:, 0:S], W("L0.q1"), x_turned[b][:, :], True)
                        return mm(m_ps[:, S:], W("L0.k1"), x_turned[b][:, :], False)
                    if layer == L0C:
                        mm(m_ps[:, 0:S], W("L0.q2"), x_turned[b][:, :], True)
                        return mm(m_ps[:, S:], W("L0.k2"), ctxm_turned[b][:, :], False)
                    if layer == L2S:
                        pe.wait_ge(late_loaded["first"], 16 * len(LATE["first"]))
                        mm(m_ps[:, 0:S], W("L2.q1"), x_turned[b][:, :], True)
                        return mm(m_ps[:, S:], W("L2.k1"), x_turned[b][:, :], False)
                    if layer == L2C:
                        pe.wait_ge(late_loaded["second"], 16 * len(LATE["second"]))
                        pe.wait_ge(ctx_t_loaded, 16 * B)
                        mm(m_ps[:, 0:S], W("L2.q2"), x_turned[b][:, :], True)
                        return mm(m_ps[:, S:], W("L2.k2"), ctx_turned[b][:, :], False)
                    mm(m_ps[:, 0:S], W("L3.q"), x_turned[b][:, :], True)
                    return mm(m_ps[:, S:], W("L3.k"), ctx_turned[b][:, :], False)
                if kind == "v":
                    src = {L0S: x_turned, L0C: ctxm_turned, L2S: x_turned, L2C: ctx_turned, L3: ctx_turned}[layer][b]
                    w = {L0S: "L0.v1", L0C: "L0.v2", L2S: "L2.v1", L2C: "L2.v2", L3: "L3.v"}[layer]
                    for t in range(T):
                        last = mm(m_ps[:, t * P:(t + 1) * P], src[:, t * P:(t + 1) * P], W(w), t == 0)
                    return last
                if kind == "count":
                    pe.wait_ge(q0_ready, COUNTS[n])
                    return mm(m_ps[0:H, 0:S], q0_own[:, :], qk_sb[ORD[n] % 2][:, 1, :], True)
                if kind == "nm":
                    pe.wait_ge(nm_parts_ready, 2 * ORD[n] + u + 1)
                    for t in range(T):
                        last = turn(m_ps[:, :].bitcast(BF16)[0:PARTS * 8, t * P:(t + 1) * P],
                                    nm_parts[u][:, t, :, :].rearrange("p a h -> p (a h)"), bf=True)
                    return last
                if kind in ("turn0", "turn1"):
                    t = int(kind[-1])
                    if t == 0:
                        pe.wait_ge(o_free, OUSE[(n, 1)] + 1)
                    for g in range(4):
                        last = turn(m_ps[:, g * P:(g + 1) * P], o_sb[:, g, t * P:(t + 1) * P])
                    return last
                if kind == "z_turn":
                    pe.wait_ge(*read_of("turn1", n))
                    for t in range(T):
                        last = turn(m_ps[:, t * P:(t + 1) * P], z_sb[:, t, :])
                    return last
                if kind == "out":
                    if layer == L1:
                        pe.wait_ge(w_loaded[4], 16)
                        pe.wait_ge(o_free, OUSE[(n, UNITS - 1)] + 1)
                        for t in range(T):
                            for p in range(UNITS):
                                last = mm(m_ps[:, t * P:(t + 1) * P], ctx1_t[:, p, t * P:(t + 1) * P],
                                          W("L1.o", p * P, P), t == 0 and p == 0)
                        return last
                    pe.wait_ge(*read_of("z_turn", n))
                    if layer == L2C:
                        pe.wait_ge(late_loaded["third"], 16 * len(LATE["third"]))
                    for t in range(T):
                        last = mm(m_ps[:, t * P:(t + 1) * P], z_turned[:, t * P:(t + 1) * P],
                                  W("L2.o1" if layer == L2S else "L2.o2"), t == 0)
                    return last
                if kind == "x_turn":
                    if layer == L0S:
                        pe.wait_ge(ctxm_ready, b + 1)
                    elif layer == L1:
                        pe.wait_ge(*read_of("out", n))
                    else:
                        pe.wait_ge(norm_done, NORMS[("sum" if layer == L0C else "out", n, 0)] + 1)
                    r = res[b][x_buffer(layer)]
                    for t in range(T):
                        last = turn(m_ps[:, t * P:(t + 1) * P], r[:, t, :])
                    if layer == L0S:
                        for t in range(T):
                            last = turn(m_ps[:, S + t * P:S + (t + 1) * P], ctxm_sb[:, t, :])
                    return last
                if kind == "kv_turn":
                    pe.wait_ge(norm_done, NORMS[("kv_sum", n, 0)] + 1)
                    for t in range(T):
                        last = turn(m_ps[:, t * P:(t + 1) * P], kvn_sb[:, t, :])
                    return last
                if kind == "ff1":
                    pe.wait_ge(w_loaded[1], 16)
                    pe.wait_ge(*read_of("x_turn", n))
                    return mm(m_ps[:, 0:S], W("L0.fc1"), x_turned[b][:, :], True)
                if kind in ("ff1a", "ff1b"):
                    pe.wait_ge(*read_of("x_turn", n))
                    for x in range(2):
                        c = (2 if kind == "ff1b" else 0) + x
                        last = mm(m_ps[:, x * S:(x + 1) * S], W("L2.f1", c * P, P), x_turned[b][:, :], x == 0)
                    return last
                if kind == "ff2":
                    pe.wait_ge(*read_of("ff1" if layer == L0C else "ff1b", n))
                    name, cs = ("L0.fc2", 1) if layer == L0C else ("L2.f2", 4)
                    for t in range(T):
                        for c in range(cs):
                            last = mm(m_ps[:, t * P:(t + 1) * P], hidden[:, c, t * P:(t + 1) * P],
                                      W(name, c * P, P), t == 0 and c == 0)
                    return last
                if kind == "y_turn":
                    pe.wait_ge(norm_done, NORMS[("again" if layer == L0C else "ff2", n, 0)] + 1)
                    r = kvn_sb if layer == L0C else res[b][1]
                    for t in range(T):
                        last = turn(m_ps[:, t * P:(t + 1) * P], r[:, t, :])
                    return last
                if kind.startswith("v1_"):
                    t, half = divmod(int(kind[-1]), 2)
                    if kind == "v1_0":
                        pe.wait_ge(w_loaded[3], 16)
                        pe.wait_ge(*read_of("kv_turn", n))
                    return mm(m_ps[:, :], kvn_turned[b][:, t * P:(t + 1) * P], W("L1.v", half * 512, 512), True)
                raise ValueError(kind)

            for kind, n, u in PLAN:
                if kind in NO_BANK and kind not in ("st", "pv", "s", "pt"):
                    continue
                if kind == "st":
                    scores_t(n, u)
                elif kind == "pv":
                    times_v(n, u)
                elif kind in ("s", "s_2"):
                    scores(kind, n, u)
                elif kind == "pt":
                    turn_probs(n, u)
                else:
                    m_ps = free_bank(kind, n, u)
                    made = qk_wide(m_ps, n, u) if kind == "qk1" else piece(m_ps, kind, n, u)
                    made.then_inc(bank_full[bank(kind, n, u)], 1)

        @block.scalar
        def _(act):
            def full(kind, n, u=0, x=0):
                act.wait_ge(*full_of(kind, n, u, x))
                return bank_ps[bank(kind, n, u, x)]

            def biased(o, i, c):
                return nc.scalar.activation(o, i, ACT.Identity, bias=c, scale=1.0)

            for kind, n, u in PLAN:
                layer, b = STEPS[n]
                i = UNITS * n + u
                if (kind, n, u, 0) in USES:
                    piece_read = bank_read[bank(kind, n, u)]
                if kind == "st" and narrow(n):
                    if i >= 2:
                        act.wait_ge(pv_done, i - 1)
                    act.wait_ge(st_full, i + 1)
                    size = 512 if layer in CAUSAL and u % T else 1024
                    nc.scalar.activation(probs[i % 2][:, 0:size], st_ps[i % 2][:, 0:size], ACT.Exp,
                                         scale=DK ** -0.5).then_inc(exp_done, 1)
                elif kind == "exp":
                    act.wait_ge(pv_done, i - 1)
                    act.wait_ge(max1_ready, i - UNITS * step_of(L1, 0) + 1)
                    for t in (1, 0):
                        for e in range(2):
                            at = slice(WIDE_AT[t] + e * (t + 1) * P, WIDE_AT[t] + (e + 1) * (t + 1) * P)
                            ins = nc.scalar.activation(probs[i % 2][:, at], st_ps[i % 2][:, at], ACT.Exp,
                                                       bias=negmax1[i % 2][:, t, e:e + 1], scale=1.0,
                                                       accum_out=sums1[i % 2][:, t, e:e + 1])
                    ins.then_inc(exp_done, 1)
                elif kind == "pt":
                    act.wait_ge(pv_done, i)
                    for x in range(T):
                        s_ps = full("pt", n, u, x)
                        size = 2 * (S - x * P)
                        nc.scalar.activation(probs1_t[:, 512 * x:512 * x + size], s_ps[:, 0:size],
                                             ACT.Copy).then_inc(bank_read[bank("pt", n, u, x)], 1)
                elif kind == "pv" and narrow(n) and u % 4 == 3:
                    half = u // 4
                    act.wait_ge(pv_done, UNITS * n + u + 1)
                    j = ORD[n]
                    if j and half == 0:
                        act.wait_ge(*full_of("turn1", NARROW[j - 1], 0))
                    nc.scalar.activation(o_sb[:, 2 * half:2 * half + 2, :],
                                         o_ps[:, :].rearrange("p (g q) -> p g q", g=2), ACT.Copy).then_inc(o_free, 1)
                elif kind == "qk":
                    m_ps = full(kind, n)
                    j = ORD[n]
                    q, first = qk_sb[j % 2], parts[j % 2][:, :, 0, :]
                    if j >= 2:
                        act.wait_ge(parts_ready, j - 1)
                        act.wait_ge(bounced[j % 2], 16 * (j // 2))
                        if ("count", NARROW[j - 2], 0, 0) in USES:
                            act.wait_ge(*full_of("count", NARROW[j - 2], 0))
                    if layer in (L0S, L0C):
                        both = m_ps[:, :].rearrange("p (w q) -> p w q", w=2)
                        nc.scalar.activation(first, both, ACT.Copy)
                        nc.scalar.activation(q[:, :, :], both, ACT.Copy).then_inc(piece_read, 1)
                    else:
                        bq, bk = {L2S: ("L2.bq1", "L2.bk1"), L2C: ("L2.bq2", "L2.bk2"), L3: ("L3.bq", "L3.bk")}[layer]
                        if layer == L3 and b == 0:
                            act.wait_ge(masks_ready, len(MASKS_AT))
                        for o in (first, q):
                            if layer == L3:
                                nc.scalar.activation(o[:, 0, :], m_ps[:, 0:S], ACT.Identity,
                                                     bias=q_gate_bias[:, :], scale=q_gate[:, :])
                            else:
                                biased(o[:, 0, :], m_ps[:, 0:S], C(bq))
                            ins = biased(o[:, 1, :], m_ps[:, S:2 * S], C(bk))
                        ins.then_inc(piece_read, 1)
                elif kind == "nm":
                    m_ps = full(kind, n, u)
                    if ORD[n]:
                        act.wait_ge(nm_stacked[u], 16 * ORD[n])
                    nc.scalar.activation(nm_rows[u][:, :], m_ps[:, :].bitcast(BF16)[0:PARTS * 8, 0:S],
                                         ACT.Copy).then_inc(piece_read, 1)
                elif kind == "qk1":
                    pair = UNITS * b + u
                    m_ps = full(kind, n, u)
                    if pair == 0:
                        act.wait_ge(blank, 1)
                        act.wait_ge(consts_ready, 3)
                    if pair >= 2:
                        act.wait_ge(st_full, i - 1)
                    q = q1_sb[u % 2]
                    for e in range(2):
                        half = slice(HS * e, HS * e + HS)
                        lo = C_AT["L1.bq"][0] + u
                        nc.scalar.activation(q[half, e, :], m_ps[half, 0:S], ACT.Identity,
                                             bias=col_sb[half, lo:lo + 1], scale=HS ** -0.5)
                    biased(k1_sb[u % 2][:, :], m_ps[:, S:2 * S], C("L1.bk", u)).then_inc(piece_read, 1)
                elif kind == "v":
                    m_ps = full(kind, n)
                    if n >= B:
                        act.wait_ge(pv_done, UNITS * (n - B) + UNITS)
                    else:
                        act.wait_ge(v_blank, b + 1)
                    for t in range(T):
                        ins = nc.scalar.activation(v_sb[b][:, t, :, 0:DK],
                                                   m_ps[:, t * P:(t + 1) * P].rearrange("p (h d) -> p h d", d=DK),
                                                   ACT.Copy)
                    ins.then_inc(piece_read, 1)
                elif kind == "z_turn":
                    m_ps = full(kind, n)
                    bv = C("L2.bv1" if layer == L2S else "L2.bv2")
                    biased(z_turned[:, :], m_ps[:, 0:S], bv).then_inc(piece_read, 1)
                elif kind == "x_turn":
                    m_ps = full(kind, n)
                    if layer == L0S:
                        nc.scalar.activation(ctxm_turned[b][:, :], m_ps[:, S:2 * S], ACT.Copy)
                    nc.scalar.activation(x_turned[b][:, :], m_ps[:, 0:S], ACT.Copy).then_inc(piece_read, 1)
                elif kind == "kv_turn":
                    m_ps = full(kind, n)
                    nc.scalar.activation(kvn_turned[b][:, :], m_ps[:, 0:S], ACT.Copy).then_inc(piece_read, 1)
                elif kind == "y_turn":
                    m_ps = full(kind, n)
                    nc.scalar.activation(x_turned[b][:, :], m_ps[:, 0:S], ACT.Copy).then_inc(piece_read, 1)
                elif kind in ("ff1", "ff1a", "ff1b"):
                    if n == step_of(L0C, 0):
                        act.wait_ge(small_loaded, 48)
                    m_ps = full(kind, n)
                    cs = {"ff1": [0], "ff1a": [0, 1], "ff1b": [2, 3]}[kind]
                    for x, c in enumerate(cs):
                        ins = nc.scalar.activation(hidden[:, c, :], m_ps[:, x * S:(x + 1) * S], ACT.Relu,
                                                   bias=C("L0.fc1b") if layer == L0C else C("L2.bf1", c), scale=1.0)
                    ins.then_inc(piece_read, 1)

        @block.vector
        def _(dve):
            steps = [0]

            def then(ins):
                steps[0] += 1
                ins.then_inc(dve_step, 1)
                dve.wait_ge(dve_step, steps[0])

            def full(kind, n, u=0, x=0):
                dve.wait_ge(*full_of(kind, n, u, x))
                return bank_ps[bank(kind, n, u, x)]

            v = nc.vector
            dve.wait_ge(small_loaded, 48)
            v.tensor_copy(const_bf[:, 0:P], K("ident")).then_inc(consts_ready, 1)
            v.tensor_copy(const_bf[:, P:K_N - K_BF], const_f).then_inc(consts_ready, 1)
            lo, hi = C_AT["L1.bq"]
            v.tensor_scalar(col_sb[:, lo:hi], col_sb[:, lo:hi], HS ** -0.5, None, ALU.mult).then_inc(consts_ready, 1)
            def masks(part):
                if part == 0:
                    dve.wait_ge(masks_loaded, 16 * 4)
                    v.tensor_scalar(src_rows[:, :, :], int_src[:, :, :], 0.0, NEG, ALU.is_equal,
                                    ALU.mult).then_inc(masks_ready, 1)
                elif part <= 2:
                    v.tensor_scalar((tgt_bias, tgt_bias_t)[part - 1][:, :, :], int_tgt[:, part - 1, :, :], 0.0, NEG,
                                    ALU.is_equal, ALU.mult).then_inc(masks_ready, 1)
                else:
                    then(v.tensor_copy(key_f[:, :], int_key[:, :]))
                    then(v.tensor_reduce(key_min[:, :], key_f[:, :], AX.X, ALU.min))
                    then(v.tensor_scalar(q_gate[:, :], key_min[:, :], 0.0, None, ALU.is_equal))
                    then(v.tensor_tensor(q_gate_bias[:, :], q_gate[:, :], C("L3.bq"), ALU.mult))
                    v.tensor_scalar(pad_row[:, :], key_f[0:H, :], key_min[0:H, :], PAD * DK ** 0.5, ALU.subtract,
                                    ALU.mult).then_inc(masks_ready, 1)

            def moments(y):
                for t in range(T):
                    ins = v.bn_stats(stats[:, t, :], y[:, t, :])
                then(ins)
                for t in range(T):
                    ins = v.bn_aggr(mean_var[:, t, :], stats[:, t, :])
                ins.then_inc(var_ready, 1)

            def normalise(o, y, g, beta, summed):
                if NORMS[summed]:
                    dve.wait_ge(norm_done, NORMS[summed])
                dve.wait_ge(var_ready, NORMS[summed] + 1)
                for t in range(T):
                    ins = v.scalar_tensor_tensor(out=xh_sb[:, t, :], in0=y[:, t, :], scalar=mean_var[:, t, 0:1],
                                                 in1=R(g), op0=ALU.subtract, op1=ALU.mult)
                then(ins)
                dve.wait_ge(rstd_ready, NORMS[summed] + 1)
                for t in range(T):
                    ins = v.scalar_tensor_tensor(out=o[:, t, :], in0=xh_sb[:, t, :], scalar=rstd[:, t:t + 1],
                                                 in1=R(beta), op0=ALU.mult, op1=ALU.add)
                ins.then_inc(norm_done, 1)

            def row_mask(live, r):
                then(v.tensor_reduce(absmax[:, :], r[:, :, :], AX.X, ALU.max, apply_absolute_value=True))
                then(v.tensor_scalar(live[:, :], absmax[:, :], 0.0, None, ALU.not_equal))

            for kind, n, u in PLAN:
                layer, b = STEPS[n]
                old = res[b][STARTS_IN[layer]]
                if (kind, n, u, 0) in USES:
                    piece_read = bank_read[bank(kind, n, u)]
                if kind in ("s", "s_2"):
                    j = ORD[n]
                    if j >= 2 and u % 4 == 0 and kind == "s":
                        dve.wait_ge(nm_parts_ready, 2 * (j - 2) + u // 4 + 1)
                    t, h0, heads, keys = score_banks(n, u)[kind == "s_2"]
                    s_ps = full(kind, n, u)
                    v.tensor_reduce(negmax[j % 2][:, t, h0:h0 + heads],
                                    s_ps[:, 0:heads * keys].rearrange("p (h k) -> p h k", h=heads),
                                    AX.X, ALU.max, negate=True).then_inc(piece_read, 1)
                elif kind == "st" and wide(n):
                    i = UNITS * n + u
                    dve.wait_ge(st_full, i + 1)
                    for t in (1, 0):
                        lo, keys = WIDE_AT[t], (t + 1) * P
                        ins = v.tensor_reduce(negmax1[i % 2][:, t, :],
                                              st_ps[i % 2][:, lo:lo + 2 * keys].rearrange("p (h k) -> p h k", h=2),
                                              AX.X, ALU.max, negate=True)
                    ins.then_inc(max1_ready, 1)
                elif kind == "scale":
                    i = UNITS * n + u
                    dve.wait_ge(exp_done, i + 1)
                    then(v.reciprocal(rec1[:, :, :], sums1[i % 2][:, :, :]))
                    for t in (1, 0):
                        lo, keys = WIDE_AT[t], (t + 1) * P
                        p = probs[i % 2][:, lo:lo + 2 * keys].rearrange("p (h k) -> p h k", h=2)
                        ins = v.tensor_tensor(p, p, rec1[:, t, :].unsqueeze(2).to_broadcast([P, 2, keys]), ALU.mult)
                    ins.then_inc(scaled, 1)
                elif kind == "pv" and wide(n):
                    dve.wait_ge(pv_done, UNITS * n + u + 1)
                    if u == 0 and b:
                        dve.wait_ge(*full_of("out", n - 1, 0))
                    v.tensor_copy(ctx1_t[:, u, :], o_ps[:, 0:S]).then_inc(o_free, 1)
                elif kind == "split":
                    j = ORD[n]
                    q, p = qk_sb[j % 2], parts[j % 2]
                    dve.wait_ge(*read_of("qk", n))
                    if layer in (L0S, L0C):
                        if COUNTS[n] > 1:
                            dve.wait_ge(*full_of("count", n - 1, 0))
                        v.tensor_scalar(q0_own[:, :], K("own_head"), q[:, 0, 0:1], None, ALU.mult).then_inc(q0_ready, 1)
                    then(v.tensor_tensor(rest[:, :, :], q[:, :, :], p[:, :, 0, :], ALU.subtract))
                    then(v.tensor_copy(p[:, :, 1, :], rest[:, :, :]))
                    v.tensor_tensor(p[:, :, 2, :], rest[:, :, :], p[:, :, 1, :], ALU.subtract).then_inc(parts_ready, 1)
                elif kind == "count":
                    m_ps = full(kind, n)
                    if layer == L0C:
                        j = ORD[step_of(L0S, b)]
                        dve.wait_ge(stacked[j % RING], 16 * 5 * (j // RING + 1))
                    v.tensor_scalar(nonzero[:, :], m_ps[0:H, 0:S], 0.0, None, ALU.not_equal).then_inc(piece_read, 1)
                    dve.wait_ge(*read_of(kind, n))
                    then(v.tensor_reduce(length[:, :], nonzero[:, :], AX.X, ALU.add))
                    lo, hi = K_AT["key"]
                    v.tensor_scalar(key_row[b][:, :], const_sb[0:H, lo:hi], length[:, :], NEG, ALU.is_ge,
                                    ALU.mult).then_inc(key_row_ready, 1)
                    if layer == L0S:
                        if b == 0:
                            dve.wait_ge(tok_loaded, 16 * B)
                        row_mask(live0[b], res[b][0])
                elif kind.startswith("v1_"):
                    t, half = divmod(int(kind[-1]), 2)
                    m_ps = full(kind, n)
                    if kind == "v1_0" and b == 0:
                        dve.wait_ge(rows_loaded[1], 16)
                    if kind == "v1_0" and b >= 2:
                        dve.wait_ge(pv_done, UNITS * (n - 2) + UNITS)
                    v.tensor_tensor(v1_sb[b % 2][:, t, half * 512:half * 512 + 512], m_ps[:, :],
                                    R("L1.bv", half * 512, 512), ALU.add).then_inc(piece_read, 1)
                elif kind in ("turn0", "turn1"):
                    t = int(kind[-1])
                    m_ps = full(kind, n)
                    heads = m_ps[:, :].rearrange("p (h w) -> p h w", w=32)
                    if t or ORD[n]:
                        dve.wait_ge(*(read_of("turn0", n) if t else read_of("turn1", NARROW[ORD[n] - 1])))
                    then(v.reciprocal(rec[:, :], heads[:, :, DK]))
                    if t == 0 and layer in (L2S, L2C) and Z_TURNS[n] > 1:
                        last = [m for m in Z_TURNS if m < n][-1]
                        dve.wait_ge(*full_of("z_turn", last, 0))
                    v.tensor_tensor(z_sb[:, t, :].rearrange("p (h d) -> p h d", d=DK), heads[:, :, 0:DK],
                                    rec[:, :].unsqueeze(2).to_broadcast([P, H, DK]), ALU.mult).then_inc(piece_read, 1)
                elif kind == "sum":
                    dve.wait_ge(*read_of("turn1", n))
                    if layer == L3:
                        dve.wait_ge(bias_added, ADDS[("y_turn", (L2C, b))] + 1)
                        then(v.tensor_tensor(y_sb[:, :, :], z_sb[:, :, :], old[:, :, :], ALU.add))
                    else:
                        live = live0[b] if layer == L0S else live1[b]
                        for t in range(T):
                            ins = v.scalar_tensor_tensor(out=y_sb[:, t, :], in0=z_sb[:, t, :], scalar=live[:, t:t + 1],
                                                         in1=old[:, t, :], op0=ALU.mult, op1=ALU.add)
                        then(ins)
                    moments(y_sb)
                elif kind == "norm":
                    if n == 0:
                        dve.wait_ge(rows_loaded[0], 16)
                    elif n == step_of(L2S, 0):
                        dve.wait_ge(rows_loaded[2], 16)
                    if layer == L0S:
                        normalise(res[b][1], y_sb, "L0.g1", "L0.b1", ("sum", n, 0))
                    elif layer == L0C:
                        normalise(res[b][0], y_sb, "L0.g2", "L0.b2", ("sum", n, 0))
                    elif layer == L2S:
                        normalise(res[b][1], y_sb, "L2.g1", "L2.be1", ("out", n, 0))
                    elif layer == L2C:
                        normalise(res[b][0], y_sb, "L2.g2", "L2.be2", ("out", n, 0))
                    else:
                        normalise(res[b][0], y_sb, "L3.g", "L3.b", ("sum", n, 0))
                elif kind == "live":
                    dve.wait_ge(norm_done, NORMS[("sum", n, 0)] + 1)
                    row_mask(live1[b], res[b][1])
                    if b == 0:
                        dve.wait_ge(ctx_loaded, 16 * B)
                    else:
                        dve.wait_ge(*full_of("x_turn", n - 1, 0))
                    for t in range(T):
                        ins = v.tensor_scalar(ctxm_sb[:, t, :], ctx_sb[b][:, t, :], live1[b][:, t:t + 1], None, ALU.mult)
                    ins.then_inc(ctxm_ready, 1)
                elif kind == "kv_sum":
                    moments(ctx_sb[b])
                elif kind == "kv_norm":
                    dve.wait_ge(*full_of(*kvn_last_read(kind, n)))
                    normalise(kvn_sb, ctx_sb[b], "L1.g", "L1.b", ("kv_sum", n, 0))
                elif kind == "out":
                    m_ps = full(kind, n)
                    added = {L1: ("y_turn", (L0C, b)), L2S: ("x_turn", (L1, b)), L2C: ("x_turn", (L2S, b))}[layer]
                    dve.wait_ge(bias_added, ADDS[added] + 1)
                    summed = res[b][0] if layer == L1 else y_sb
                    v.tensor_tensor(summed[:, :, :], m_ps[:, 0:S].rearrange("p (t d) -> p t d", t=T), old[:, :, :],
                                    ALU.add).then_inc(piece_read, 1)
                    if layer != L1:
                        dve.wait_ge(*read_of(kind, n))
                        moments(y_sb)
                elif kind == "ff2":
                    m_ps = full(kind, n)
                    if layer == L0C:
                        dve.wait_ge(norm_done, NORMS[(kind, n, 0)])
                        v.tensor_tensor(xh_sb[:, :, :], m_ps[:, 0:S].rearrange("p (t d) -> p t d", t=T), R2("L0.fc2b"),
                                        ALU.add).then_inc(piece_read, 1)
                        dve.wait_ge(*read_of(kind, n))
                        for t in range(T):
                            ins = v.scalar_tensor_tensor(out=y_sb[:, t, :], in0=xh_sb[:, t, :],
                                                         scalar=live0[b][:, t:t + 1], in1=res[b][0][:, t, :],
                                                         op0=ALU.mult, op1=ALU.add)
                        then(ins)
                    else:
                        dve.wait_ge(bias_added, ADDS[("x_turn", (L2C, b))] + 1)
                        v.tensor_tensor(y_sb[:, :, :], m_ps[:, 0:S].rearrange("p (t d) -> p t d", t=T),
                                        res[b][0][:, :, :], ALU.add).then_inc(piece_read, 1)
                        dve.wait_ge(*read_of(kind, n))
                    moments(y_sb)
                elif kind == "norm2":
                    if layer == L0C:
                        normalise(res[b][1], y_sb, "L0.g3", "L0.b3", ("ff2", n, 0))
                    else:
                        normalise(res[b][1], y_sb, "L2.g3", "L2.be3", ("ff2", n, 0))
                elif kind == "again":
                    dve.wait_ge(norm_done, NORMS[("ff2", n, 0)] + 1)
                    moments(res[b][1])
                elif kind == "norm3":
                    last = kvn_last_read(kind, n)
                    if last:
                        dve.wait_ge(*full_of(*last))
                    normalise(kvn_sb, res[b][1], "L1.g", "L1.b", ("again", n, 0))
                elif kind == "masks":
                    masks(u)


def kvn_last_read(kind, n):
    reads = [e for e in PLAN[:PLAN.index((kind, n, 0))]
             if e[0] == "kv_turn" or e[0] == "y_turn" and STEPS[e[1]][0] == L0C]
    return reads[-1] if reads else None


def x_buffer(layer):
    return {L0S: 1, L0C: 0, L1: 0, L2S: 1, L2C: 0}[layer]


def shape_constants():
    c = np.zeros((P, K_N), np.float32)
    i = np.arange(P)
    c[:, slice(*K_AT["ident"])] = np.eye(P)
    c[:, slice(*K_AT["causal"])] = np.where(i[None, :] > i[:, None], NEG, 0)
    c[:, slice(*K_AT["causalT"])] = np.where(i[:, None] > i[None, :], NEG, 0)
    c[:, slice(*K_AT["own_head"])] = i[:, None] % H == np.arange(H)[None, :]
    c[:, slice(*K_AT["key"])] = np.arange(S)[None, :]
    return c


def fixed_rows():
    words = np.zeros((ALL_ROWS - PARTS * PARTS * DK, H * S // 2), np.uint32)
    words[MASK_ROW - PARTS * PARTS * DK:] = 0x3F803F80
    return words.view(np.float32)


def kernel(**inputs):
    import concourse.bacc as bacc
    from concourse.bass_utils import run_bass_kernel_spmd

    a = {k: np.asarray(v) for k, v in inputs.items()}

    def l0(name):
        return a[f"L0_xattn_{name}"]

    def by_depth(w):
        return w.reshape(D, H, DK).transpose(0, 2, 1).reshape(D, D)

    def tiles(w):
        return w.reshape(-1, P, w.shape[1]).transpose(1, 0, 2).reshape(P, -1)

    def l2(name):
        return a[f"L2_xattn_{name}"]

    def l3(name):
        return a[f"L3_xattn_{name}"]

    wkv = a["L1_xattn_wkv"]
    w = {"L0.fc1": l0("fc1_w").T, "L0.fc2": l0("fc2_w").T, "L1.q": a["L1_xattn_wq"], "L1.k": wkv[:, :H * HS],
         "L1.v": wkv[:, H * HS:], "L1.o": tiles(a["L1_xattn_wo"]), "L2.f1": l2("Wf1").T, "L2.f2": tiles(l2("Wf2").T),
         "L3.q": by_depth(l3("wq").T), "L3.k": by_depth(l3("wk").T), "L3.v": l3("wv").T}
    for i in "12":
        w[f"L0.q{i}"] = l0(f"Wq{i}").transpose(1, 2, 0).reshape(D, D)
        w[f"L0.k{i}"] = l0(f"Wk{i}").transpose(1, 2, 0).reshape(D, D)
        w[f"L0.v{i}"] = l0(f"Wv{i}").transpose(1, 0, 2).reshape(D, D)
        w[f"L2.q{i}"] = by_depth(l2(f"Wq{i}").T)
        w[f"L2.k{i}"] = by_depth(l2(f"Wk{i}").T)
        w[f"L2.v{i}"] = l2(f"Wv{i}").T
        w[f"L2.o{i}"] = l2(f"Wo{i}").T
    r = {"L0.fc2b": l0("fc2_b"), "L1.g": a["L1_xattn_ln_g"], "L1.b": a["L1_xattn_ln_b"],
         "L1.bv": a["L1_xattn_bkv"][H * HS:],
         "L1.bo": a["L1_xattn_bo"], "L2.bo1": l2("bo1"), "L2.bo2": l2("bo2"), "L2.bf2": l2("bf2"), "L3.bv": l3("bv"), "L3.g": l3("gamma"),
         "L3.b": l3("beta")}
    for i in "123":
        r[f"L0.g{i}"], r[f"L0.b{i}"] = l0(f"ln{i}_g"), l0(f"ln{i}_b")
        r[f"L2.g{i}"], r[f"L2.be{i}"] = l2(f"g{i}"), l2(f"be{i}")

    def depth_col(v):
        return v.reshape(H, DK).T.reshape(P, 1)

    c = {"L0.fc1b": l0("fc1_b").reshape(P, 1), "L1.bq": a["L1_xattn_bq"].reshape(UNITS, P).T,
         "L1.bk": a["L1_xattn_bkv"][:H * HS].reshape(UNITS, P).T, "L2.bq1": depth_col(l2("bq1")),
         "L2.bk1": depth_col(l2("bk1")), "L2.bq2": depth_col(l2("bq2")), "L2.bk2": depth_col(l2("bk2")),
         "L2.bf1": l2("bf1").reshape(4, P).T,
         "L2.bv1": l2("bv1").reshape(P, 1), "L2.bv2": l2("bv2").reshape(P, 1),
         "L3.bq": depth_col(l3("bq")), "L3.bk": depth_col(l3("bk"))}
    tgt = a["mask_1x1xSxS2_ik0"].reshape(S, S)
    arrays = {
        "x": a["x"], "x_t": a["x"].reshape(B * S, D).T,
        "ctx": a["ctx_1024"], "ctx_t": a["ctx_1024"].reshape(B * S, D).T,
        "weights": np.concatenate([w[name] for name, _ in WEIGHTS], axis=1),
        "rows": np.concatenate([r[name] for name, _ in ROWS]).reshape(1, R_N),
        "cols": np.concatenate([c[name] for name, _ in COLS], axis=1),
        "consts": shape_constants(), "fixed_rows": fixed_rows(),
        "src_mask": a["mask_Bx1x1xS2_if1"].reshape(1, B * S), "tgt_mask": tgt, "tgt_mask_t": tgt.T,
        "key_mask": np.tile(np.repeat(a["mask_BxS2_ik0"], H // B, axis=0), (DK, 1)),
    }
    arrays = {k: np.ascontiguousarray(v) for k, v in arrays.items()}
    nc = bacc.Bacc("TRN2", target_bir_lowering=False, num_devices=1)
    aps = {k: nc.dram_tensor(f"{k}_dram", v.shape, mybir.dt.from_np(v.dtype), kind="ExternalInput").ap()
           for k, v in arrays.items()}
    out = nc.dram_tensor("out_dram", (B, S, D), F32, kind="ExternalOutput").ap()
    attention_stack_program(nc, out=out, **aps)
    ran = run_bass_kernel_spmd(nc, [{f"{k}_dram": v for k, v in arrays.items()}], core_ids=[0])
    return ran.results[0]["out_dram"]
```
